# Optimizing a Trainium2 kernel written in Bass

```python
import numpy as np
import jax
import jax.numpy as jnp

def _softmax(x, axis=-1):
    return jax.nn.softmax(x, axis=axis)

def _gelu(x):
    return jax.nn.gelu(x, approximate=True)

def _silu(x):
    return jax.nn.silu(x)

def _sigmoid(x):
    return jax.nn.sigmoid(x)

def _layernorm(x, axis=-1, eps=1e-05):
    m = jnp.mean(x, axis=axis, keepdims=True)
    v = jnp.var(x, axis=axis, keepdims=True)
    return (x - m) / jnp.sqrt(v + eps)

def _scatter_add(tgt, idx, src, axis=0):
    return tgt.at[idx].add(src)

def _segment_sum(src, seg, n):
    return jax.ops.segment_sum(src, seg, n)
kernel_name = 'mk_gps_d2_gnn_r16_c71a63'

def setup_inputs(seed: int=0):
    np.random.seed(seed)
    _w = jnp.asarray

    def _rec_inputs():
        import jax
        import jax.numpy as jnp
        _gk = jax.random.key(seed)
        x = -7.329e-05 + 0.9999 * jax.random.normal(jax.random.fold_in(_gk, 1), (625, 512), jnp.float32)
        src = jax.random.randint(jax.random.fold_in(_gk, 2), (20000,), 0, 625, jnp.int32)
        dst = jnp.minimum((625 * jax.random.uniform(jax.random.fold_in(_gk, 3), (20000,)) ** 2.0).astype(jnp.int32), 9999)
        _o = jnp.argsort(dst, stable=True)
        src = src[_o]
        dst = dst[_o]
        edge_weight = jax.random.uniform(jax.random.fold_in(_gk, 13), (20000,), jnp.float32, 0.0, 0.999999)
        return (x, src, dst, edge_weight)
    x, src, dst, edge_weight = _rec_inputs()

    def _L0_gnn_setup():
        import jax, jax.numpy as jnp
        import numpy as np
        N_NODES = 6250
        N_EDGES = 100000
        D_IN = 512
        D_OUT = 512
        key = jax.random.key(seed)
        k1, k2, k3, k4, k5 = jax.random.split(key, 5)
        h = jax.random.normal(k1, (N_NODES, D_IN), dtype=jnp.float32)
        weight = jax.random.normal(k2, (D_IN, D_OUT), dtype=jnp.float32) * (1.0 / np.sqrt(D_IN))
        edge_weight = jax.random.uniform(k3, (N_EDGES,), dtype=jnp.float32)
        src = jax.random.randint(k4, (N_EDGES,), 0, N_NODES, dtype=jnp.int64)
        dst = jax.random.randint(k5, (N_EDGES,), 0, N_NODES, dtype=jnp.int64)
        return {'h': h, 'weight': weight, 'edge_weight': edge_weight, 'src': src, 'dst': dst}
    _L0_gnn_all = _L0_gnn_setup()
    _L0_gnn_in = {k: v for k, v in _L0_gnn_all.items() if k in ('weight',)}
    del _L0_gnn_all

    def _L0_mix_setup():
        import jax, jax.numpy as jnp
        import numpy as np
        B, S, DM = (4, 512, 512)
        H = 8
        D = DM // H

        def _feature_map(t):
            return jax.nn.elu(t) + 1.0
        key = jax.random.key(seed)
        ks = jax.random.split(key, 9)
        s = 1.0 / np.sqrt(DM)
        x = jax.random.normal(ks[0], (B, S, DM), dtype=jnp.float32)
        Wq = jax.random.normal(ks[1], (DM, DM), dtype=jnp.float32) * s
        bq = jnp.zeros((DM,), dtype=jnp.float32)
        Wk = jax.random.normal(ks[2], (DM, DM), dtype=jnp.float32) * s
        bk = jnp.zeros((DM,), dtype=jnp.float32)
        Wv = jax.random.normal(ks[3], (DM, DM), dtype=jnp.float32) * s
        bv = jnp.zeros((DM,), dtype=jnp.float32)
        Wp = jax.random.normal(ks[4], (DM, DM), dtype=jnp.float32) * s
        bp = jnp.zeros((DM,), dtype=jnp.float32)
        return {'x': x, 'Wq': Wq, 'bq': bq, 'Wk': Wk, 'bk': bk, 'Wv': Wv, 'bv': bv, 'Wp': Wp, 'bp': bp}
    _L0_mix_all = _L0_mix_setup()
    _L0_mix_in = {k: v for k, v in _L0_mix_all.items() if k in ('Wq', 'bq', 'Wk', 'bk', 'Wv', 'bv', 'Wp', 'bp')}
    del _L0_mix_all

    def _L0_ffn_setup():
        import jax, jax.numpy as jnp
        import numpy as np
        B, S, D, H, E = (4, 128, 512, 8, 8)
        FF = 4 * D
        HD = D // H
        EPS = 1e-05

        def _layernorm(x, g, b):
            mu = jnp.mean(x, axis=-1, keepdims=True)
            var = jnp.mean((x - mu) ** 2, axis=-1, keepdims=True)
            return (x - mu) * jax.lax.rsqrt(var + EPS) * g + b
        key = jax.random.key(seed)
        ks = jax.random.split(key, 16)
        s = 0.02
        return {'x': jax.random.normal(ks[0], (B, S, D), dtype=jnp.float32), 'ln1_g': jnp.ones((D,), jnp.float32), 'ln1_b': jnp.zeros((D,), jnp.float32), 'Wq': jax.random.normal(ks[1], (D, D), jnp.float32) * s, 'bq': jnp.zeros((D,), jnp.float32), 'Wk': jax.random.normal(ks[2], (D, D), jnp.float32) * s, 'bk': jnp.zeros((D,), jnp.float32), 'Wv': jax.random.normal(ks[3], (D, D), jnp.float32) * s, 'bv': jnp.zeros((D,), jnp.float32), 'Wo': jax.random.normal(ks[4], (D, D), jnp.float32) * s, 'bo': jnp.zeros((D,), jnp.float32), 'gate_W': jax.random.normal(ks[5], (D, E), jnp.float32) * s, 'gate_b': jnp.zeros((E,), jnp.float32), 'W1': jax.random.normal(ks[6], (E, D, FF), jnp.float32) * s, 'b1': jnp.zeros((E, FF), jnp.float32), 'W2': jax.random.normal(ks[7], (E, FF, D), jnp.float32) * s, 'b2': jnp.zeros((E, D), jnp.float32)}
    _L0_ffn_all = _L0_ffn_setup()
    _L0_ffn_in = {k: v for k, v in _L0_ffn_all.items() if k in ('ln1_g', 'ln1_b', 'Wq', 'bq', 'Wk', 'bk', 'Wv', 'bv', 'Wo', 'bo', 'gate_W', 'gate_b', 'W1', 'b1', 'W2', 'b2')}
    del _L0_ffn_all

    def _L1_gnn_setup():
        import jax, jax.numpy as jnp
        import numpy as np
        D = 512
        H = 8
        DH = D // H
        F = 128
        L = 2
        N = 1250
        E = 20000
        EPS = 1e-05

        def _xavier(key, shape):
            fan_out, fan_in = (shape[-2], shape[-1])
            lim = float(np.sqrt(6.0 / (fan_in + fan_out)))
            return jax.random.uniform(key, shape, jnp.float32, -lim, lim)

        def _batchnorm(x, g, b):
            mu = jnp.mean(x, axis=0)
            var = jnp.mean(jnp.square(x - mu), axis=0)
            return (x - mu) * jax.lax.rsqrt(var + EPS) * g + b

        def _layernorm(x, g, b):
            mu = jnp.mean(x, axis=-1, keepdims=True)
            var = jnp.mean(jnp.square(x - mu), axis=-1, keepdims=True)
            return (x - mu) * jax.lax.rsqrt(var + EPS) * g + b
        key = jax.random.key(seed)
        ks = jax.random.split(key, 12)
        src = jax.random.normal(ks[0], (N, D), jnp.float32)
        edge_index = jax.random.randint(ks[1], (2, E), 0, N)
        return {'src': src, 'edge_index': edge_index, 'Wq': _xavier(ks[2], (L, D, D)), 'bq': jnp.zeros((L, D), jnp.float32), 'Wk': _xavier(ks[3], (L, D, D)), 'Wv': _xavier(ks[4], (L, D, D)), 'Wo': _xavier(ks[5], (L, D, D)), 'bo': jnp.zeros((L, D), jnp.float32), 'W1': _xavier(ks[6], (L, F, D)), 'b1': jnp.zeros((L, F), jnp.float32), 'W2': _xavier(ks[7], (L, D, F)), 'b2': jnp.zeros((L, D), jnp.float32), 'g1': jnp.ones((L, D), jnp.float32), 'beta1': jnp.zeros((L, D), jnp.float32), 'g2': jnp.ones((L, D), jnp.float32), 'beta2': jnp.zeros((L, D), jnp.float32), 'ln_g': jnp.ones((D,), jnp.float32), 'ln_b': jnp.zeros((D,), jnp.float32)}
    _L1_gnn_all = _L1_gnn_setup()
    _L1_gnn_in = {k: v for k, v in _L1_gnn_all.items() if k in ('Wq', 'bq', 'Wk', 'Wv', 'Wo', 'bo', 'W1', 'b1', 'W2', 'b2', 'g1', 'beta1', 'g2', 'beta2', 'ln_g', 'ln_b')}
    del _L1_gnn_all

    def _L1_mix_setup():
        import jax, jax.numpy as jnp
        import numpy as np
        NUM_HEADS = 16
        EPS = 1e-15
        key = jax.random.key(seed)
        k1, k2, k3, k4 = jax.random.split(key, 4)
        B, N, C = (4, 1024, 512)
        x = jax.random.normal(k1, (B, N, C), dtype=jnp.float32)
        qkv_weight = jax.random.normal(k2, (3 * C, C), dtype=jnp.float32) * 0.02
        proj_weight = jax.random.normal(k3, (C, C), dtype=jnp.float32) * 0.02
        proj_bias = jax.random.normal(k4, (C,), dtype=jnp.float32) * 0.02
        return {'x': x, 'qkv_weight': qkv_weight, 'proj_weight': proj_weight, 'proj_bias': proj_bias}
    _L1_mix_all = _L1_mix_setup()
    _L1_mix_in = {k: v for k, v in _L1_mix_all.items() if k in ('qkv_weight', 'proj_weight', 'proj_bias')}
    del _L1_mix_all

    def _L1_ffn_setup():
        import jax, jax.numpy as jnp
        import numpy as np
        K = 2
        key = jax.random.key(seed)
        ks = jax.random.split(key, 6)
        B, T, d, E, dff = (2, 128, 512, 8, 128)
        x = jax.random.normal(ks[0], (B, T, d), dtype=jnp.float32)
        Wg = jax.random.normal(ks[1], (d, E), dtype=jnp.float32) * 0.02
        W1 = jax.random.normal(ks[2], (E, d, dff), dtype=jnp.float32) * 0.02
        b1 = jnp.zeros((E, dff), dtype=jnp.float32)
        W2 = jax.random.normal(ks[3], (E, dff, d), dtype=jnp.float32) * 0.02
        b2 = jnp.zeros((E, d), dtype=jnp.float32)
        return {'x': x, 'Wg': Wg, 'W1': W1, 'b1': b1, 'W2': W2, 'b2': b2}
    _L1_ffn_all = _L1_ffn_setup()
    _L1_ffn_in = {k: v for k, v in _L1_ffn_all.items() if k in ('Wg', 'W1', 'b1', 'W2', 'b2')}
    del _L1_ffn_all
    return {'x': x, 'src': src, 'dst': dst, 'edge_weight': edge_weight, 'L0_gnn_weight': _L0_gnn_in['weight'], 'L0_mix_Wq': _L0_mix_in['Wq'], 'L0_mix_bq': _L0_mix_in['bq'], 'L0_mix_Wk': _L0_mix_in['Wk'], 'L0_mix_bk': _L0_mix_in['bk'], 'L0_mix_Wv': _L0_mix_in['Wv'], 'L0_mix_bv': _L0_mix_in['bv'], 'L0_mix_Wp': _L0_mix_in['Wp'], 'L0_mix_bp': _L0_mix_in['bp'], 'L0_ffn_ln1_g': _L0_ffn_in['ln1_g'], 'L0_ffn_ln1_b': _L0_ffn_in['ln1_b'], 'L0_ffn_Wq': _L0_ffn_in['Wq'], 'L0_ffn_bq': _L0_ffn_in['bq'], 'L0_ffn_Wk': _L0_ffn_in['Wk'], 'L0_ffn_bk': _L0_ffn_in['bk'], 'L0_ffn_Wv': _L0_ffn_in['Wv'], 'L0_ffn_bv': _L0_ffn_in['bv'], 'L0_ffn_Wo': _L0_ffn_in['Wo'], 'L0_ffn_bo': _L0_ffn_in['bo'], 'L0_ffn_gate_W': _L0_ffn_in['gate_W'], 'L0_ffn_gate_b': _L0_ffn_in['gate_b'], 'L0_ffn_W1': _L0_ffn_in['W1'], 'L0_ffn_b1': _L0_ffn_in['b1'], 'L0_ffn_W2': _L0_ffn_in['W2'], 'L0_ffn_b2': _L0_ffn_in['b2'], 'L1_gnn_Wq': _L1_gnn_in['Wq'], 'L1_gnn_bq': _L1_gnn_in['bq'], 'L1_gnn_Wk': _L1_gnn_in['Wk'], 'L1_gnn_Wv': _L1_gnn_in['Wv'], 'L1_gnn_Wo': _L1_gnn_in['Wo'], 'L1_gnn_bo': _L1_gnn_in['bo'], 'L1_gnn_W1': _L1_gnn_in['W1'], 'L1_gnn_b1': _L1_gnn_in['b1'], 'L1_gnn_W2': _L1_gnn_in['W2'], 'L1_gnn_b2': _L1_gnn_in['b2'], 'L1_gnn_g1': _L1_gnn_in['g1'], 'L1_gnn_beta1': _L1_gnn_in['beta1'], 'L1_gnn_g2': _L1_gnn_in['g2'], 'L1_gnn_beta2': _L1_gnn_in['beta2'], 'L1_gnn_ln_g': _L1_gnn_in['ln_g'], 'L1_gnn_ln_b': _L1_gnn_in['ln_b'], 'L1_mix_qkv_weight': _L1_mix_in['qkv_weight'], 'L1_mix_proj_weight': _L1_mix_in['proj_weight'], 'L1_mix_proj_bias': _L1_mix_in['proj_bias'], 'L1_ffn_Wg': _L1_ffn_in['Wg'], 'L1_ffn_W1': _L1_ffn_in['W1'], 'L1_ffn_b1': _L1_ffn_in['b1'], 'L1_ffn_W2': _L1_ffn_in['W2'], 'L1_ffn_b2': _L1_ffn_in['b2']}

def reference(x, src, dst, edge_weight, L0_gnn_weight, L0_mix_Wq, L0_mix_bq, L0_mix_Wk, L0_mix_bk, L0_mix_Wv, L0_mix_bv, L0_mix_Wp, L0_mix_bp, L0_ffn_ln1_g, L0_ffn_ln1_b, L0_ffn_Wq, L0_ffn_bq, L0_ffn_Wk, L0_ffn_bk, L0_ffn_Wv, L0_ffn_bv, L0_ffn_Wo, L0_ffn_bo, L0_ffn_gate_W, L0_ffn_gate_b, L0_ffn_W1, L0_ffn_b1, L0_ffn_W2, L0_ffn_b2, L1_gnn_Wq, L1_gnn_bq, L1_gnn_Wk, L1_gnn_Wv, L1_gnn_Wo, L1_gnn_bo, L1_gnn_W1, L1_gnn_b1, L1_gnn_W2, L1_gnn_b2, L1_gnn_g1, L1_gnn_beta1, L1_gnn_g2, L1_gnn_beta2, L1_gnn_ln_g, L1_gnn_ln_b, L1_mix_qkv_weight, L1_mix_proj_weight, L1_mix_proj_bias, L1_ffn_Wg, L1_ffn_W1, L1_ffn_b1, L1_ffn_W2, L1_ffn_b2):
    import jax
    import jax.numpy as jnp

    def _L0_gnn_ref(h, weight, edge_weight, src, dst):
        import jax, jax.numpy as jnp
        import numpy as np
        N_NODES = 6250
        N_EDGES = 100000
        D_IN = 512
        D_OUT = 512
        hp = h @ weight
        msgs = hp[src] * edge_weight[:, None]
        agg = jax.ops.segment_sum(msgs, dst, num_segments=h.shape[0])
        return jax.nn.relu(agg)

    def _L0_mix_ref(x, Wq, bq, Wk, bk, Wv, bv, Wp, bp):
        import jax, jax.numpy as jnp
        import numpy as np
        B, S, DM = (4, 512, 512)
        H = 8
        D = DM // H

        def _feature_map(t):
            return jax.nn.elu(t) + 1.0
        b, s, _ = x.shape
        q = _feature_map(x @ Wq + bq).reshape(b, s, H, D)
        k = _feature_map(x @ Wk + bk).reshape(b, s, H, D)
        v = (x @ Wv + bv).reshape(b, s, H, D)
        kv = jnp.einsum('bshd,bshe->bhde', k, v)
        z = 1.0 / jnp.einsum('bshd,bhd->bsh', q, k.sum(axis=1))
        out = jnp.einsum('bshd,bhde,bsh->bshe', q, kv, z)
        out = out.reshape(b, s, H * D)
        return out @ Wp + bp

    def _L0_ffn_ref(x, ln1_g, ln1_b, Wq, bq, Wk, bk, Wv, bv, Wo, bo, gate_W, gate_b, W1, b1, W2, b2):
        import jax, jax.numpy as jnp
        import numpy as np
        B, S, D, H, E = (4, 128, 512, 8, 8)
        FF = 4 * D
        HD = D // H
        EPS = 1e-05

        def _layernorm(x, g, b):
            mu = jnp.mean(x, axis=-1, keepdims=True)
            var = jnp.mean((x - mu) ** 2, axis=-1, keepdims=True)
            return (x - mu) * jax.lax.rsqrt(var + EPS) * g + b
        b, s, d = x.shape
        q = (x @ Wq + bq).reshape(b, s, H, HD)
        k = (x @ Wk + bk).reshape(b, s, H, HD)
        v = (x @ Wv + bv).reshape(b, s, H, HD)
        scores = jnp.einsum('bqhd,bkhd->bhqk', q, k) / jnp.sqrt(jnp.float32(HD))
        attn = jax.nn.softmax(scores, axis=-1)
        o = jnp.einsum('bhqk,bkhd->bqhd', attn, v).reshape(b, s, d) @ Wo + bo
        h = _layernorm(x + o, ln1_g, ln1_b)
        t = h.reshape(b * s, d)
        probs = jax.nn.softmax(t @ gate_W + gate_b, axis=-1)
        idx = jnp.argmax(probs, axis=-1)
        gw = jnp.max(probs, axis=-1)
        hid = jax.nn.gelu(jnp.einsum('nd,edf->enf', t, W1) + b1[:, None, :])
        out_all = jnp.einsum('enf,efd->end', hid, W2) + b2[:, None, :]
        onehot = jax.nn.one_hot(idx, E, dtype=t.dtype)
        out = jnp.einsum('ne,end->nd', onehot, out_all)
        out = out * gw[:, None]
        return out.reshape(b, s, d)

    def _L1_gnn_ref(src, edge_index, Wq, bq, Wk, Wv, Wo, bo, W1, b1, W2, b2, g1, beta1, g2, beta2, ln_g, ln_b):
        import jax, jax.numpy as jnp
        import numpy as np
        D = 512
        H = 8
        DH = D // H
        F = 128
        L = 2
        N = 1250
        E = 20000
        EPS = 1e-05

        def _xavier(key, shape):
            fan_out, fan_in = (shape[-2], shape[-1])
            lim = float(np.sqrt(6.0 / (fan_in + fan_out)))
            return jax.random.uniform(key, shape, jnp.float32, -lim, lim)

        def _batchnorm(x, g, b):
            mu = jnp.mean(x, axis=0)
            var = jnp.mean(jnp.square(x - mu), axis=0)
            return (x - mu) * jax.lax.rsqrt(var + EPS) * g + b

        def _layernorm(x, g, b):
            mu = jnp.mean(x, axis=-1, keepdims=True)
            var = jnp.mean(jnp.square(x - mu), axis=-1, keepdims=True)
            return (x - mu) * jax.lax.rsqrt(var + EPS) * g + b
        n = src.shape[0]
        scaling = float(DH) ** (-0.5)
        tgt = edge_index[1]
        srcidx = edge_index[0]
        x = src
        for l in range(L):
            q = ((x @ Wq[l].T + bq[l]) * scaling).reshape(n, H, DH)
            k = (x @ Wk[l].T).reshape(n, H, DH)
            v = (x @ Wv[l].T).reshape(n, H, DH)
            scores = jnp.einsum('ehd,ehd->eh', q[tgt], k[srcidx])
            m = jax.ops.segment_max(scores, tgt, num_segments=n)
            p = jnp.exp(scores - m[tgt])
            s = jax.ops.segment_sum(p, tgt, num_segments=n)
            w = p / (s[tgt] + 1e-16)
            agg = jax.ops.segment_sum(w[:, :, None] * v[srcidx], tgt, num_segments=n)
            attn = agg.reshape(n, D) @ Wo[l].T + bo[l]
            x = _batchnorm(x + attn, g1[l], beta1[l])
            ff = jax.nn.relu(x @ W1[l].T + b1[l]) @ W2[l].T + b2[l]
            x = _batchnorm(x + ff, g2[l], beta2[l])
        return _layernorm(x, ln_g, ln_b)

    def _L1_mix_ref(x, qkv_weight, proj_weight, proj_bias):
        import jax, jax.numpy as jnp
        import numpy as np
        NUM_HEADS = 16
        EPS = 1e-15
        B, N, C = x.shape
        H = NUM_HEADS
        D = C // H
        qkv = (x @ qkv_weight.T).reshape(B, N, 3, C)
        q = jax.nn.relu(qkv[:, :, 0]).reshape(B, N, H, D)
        k = jax.nn.relu(qkv[:, :, 1]).reshape(B, N, H, D)
        v = qkv[:, :, 2].reshape(B, N, H, D)
        qf = q.astype(jnp.float32)
        kf = k.astype(jnp.float32)
        vf = v.astype(jnp.float32)
        v_pad = jnp.concatenate([vf, jnp.ones_like(vf[..., :1])], axis=-1)
        vk = jnp.einsum('bnhc,bnhd->bhcd', v_pad, kf)
        vk_q = jnp.einsum('bnhd,bhcd->bnhc', qf, vk)
        proj_input = (vk_q[..., :-1] / (vk_q[..., -1:] + EPS)).astype(x.dtype).reshape(B, N, C)
        return proj_input @ proj_weight.T + proj_bias

    def _L1_ffn_ref(x, Wg, W1, b1, W2, b2):
        import jax, jax.numpy as jnp
        import numpy as np
        K = 2
        logits = jnp.einsum('btd,de->bte', x, Wg)
        probs = jax.nn.softmax(logits, axis=-1)
        top_p, _top_i = jax.lax.top_k(probs, K)
        top_p = top_p / jnp.sum(top_p, axis=-1, keepdims=True)
        b2_sum = jnp.sum(b2, axis=0)
        out = jnp.zeros_like(x)
        for i in range(K):
            w_in = x * top_p[..., i:i + 1]
            h = jax.nn.gelu(jnp.einsum('btd,edf->ebtf', w_in, W1) + b1[:, None, None, :], approximate=False)
            out = out + jnp.einsum('ebtf,efd->btd', h, W2) + b2_sum
        return out
    edge_index = jnp.stack([src, dst])
    xn = _layernorm(x, axis=-1)
    x = x + _L0_gnn_ref(xn, L0_gnn_weight, edge_weight, src, dst) + _L0_mix_ref(xn[None], L0_mix_Wq, L0_mix_bq, L0_mix_Wk, L0_mix_bk, L0_mix_Wv, L0_mix_bv, L0_mix_Wp, L0_mix_bp)[0]
    x = x + _L0_ffn_ref(_layernorm(x, axis=-1)[None], L0_ffn_ln1_g, L0_ffn_ln1_b, L0_ffn_Wq, L0_ffn_bq, L0_ffn_Wk, L0_ffn_bk, L0_ffn_Wv, L0_ffn_bv, L0_ffn_Wo, L0_ffn_bo, L0_ffn_gate_W, L0_ffn_gate_b, L0_ffn_W1, L0_ffn_b1, L0_ffn_W2, L0_ffn_b2)[0]
    xn = _layernorm(x, axis=-1)
    x = x + _L1_gnn_ref(xn, edge_index, L1_gnn_Wq, L1_gnn_bq, L1_gnn_Wk, L1_gnn_Wv, L1_gnn_Wo, L1_gnn_bo, L1_gnn_W1, L1_gnn_b1, L1_gnn_W2, L1_gnn_b2, L1_gnn_g1, L1_gnn_beta1, L1_gnn_g2, L1_gnn_beta2, L1_gnn_ln_g, L1_gnn_ln_b) + _L1_mix_ref(xn[None], L1_mix_qkv_weight, L1_mix_proj_weight, L1_mix_proj_bias)[0]
    x = x + _L1_ffn_ref(_layernorm(x, axis=-1)[None], L1_ffn_Wg, L1_ffn_W1, L1_ffn_b1, L1_ffn_W2, L1_ffn_b2)[0]
    return x

_drawn_inputs = setup_inputs


def setup_inputs(seed=0):
    import zlib

    import numpy as np

    out = dict(_drawn_inputs(seed))
    spreads = {'L0_mix_bq': (0.0, 2.0),
     'L0_mix_bk': (0.0, 2.0),
     'L0_mix_bv': (0.0, 0.1),
     'L0_mix_bp': (0.0, 0.1),
     'L0_ffn_ln1_g': (1.0, 0.6),
     'L0_ffn_ln1_b': (0.0, 0.8),
     'L0_ffn_bq': (0.0, 0.8),
     'L0_ffn_bk': (0.0, 2.0),
     'L0_ffn_bv': (0.0, 0.8),
     'L0_ffn_bo': (0.0, 2.0),
     'L0_ffn_gate_b': (0.0, 0.505),
     'L0_ffn_b1': (0.0, 0.8),
     'L0_ffn_b2': (0.0, 0.765),
     'L1_gnn_bq': (0.0, 0.621),
     'L1_gnn_bo': (0.0, 2.0),
     'L1_gnn_b1': (0.0, 0.618),
     'L1_gnn_b2': (0.0, 2.0),
     'L1_gnn_g1': (1.0, 0.2),
     'L1_gnn_beta1': (0.0, 0.451),
     'L1_gnn_g2': (1.0, 0.2),
     'L1_gnn_beta2': (0.0, 0.279),
     'L1_gnn_ln_g': (1.0, 0.2),
     'L1_gnn_ln_b': (0.0, 0.275),
     'L1_ffn_b1': (0.0, 0.366),
     'L1_ffn_b2': (0.0, 0.1)}
    factors = {'L0_mix_Wq': 8.0,
     'L0_mix_Wk': 8.0,
     'L0_mix_Wv': 4.574,
     'L0_ffn_Wq': 8.0,
     'L0_ffn_Wk': 8.0,
     'L0_ffn_Wv': 8.0,
     'L0_ffn_Wo': 8.0,
     'L1_mix_qkv_weight': 5.577,
     'L1_mix_proj_weight': 5.835,
     'L1_mix_proj_bias': 8.0,
     'L1_ffn_Wg': 64.0}
    for name, (base, spread) in spreads.items():
        noise = np.random.default_rng([zlib.crc32(name.encode()), seed]).standard_normal(out[name].shape)
        drawn = base * np.exp(spread * noise) if base else spread * noise
        out[name] = jnp.asarray(drawn.astype(out[name].dtype))
    for name, factor in factors.items():
        out[name] = (out[name] * factor).astype(out[name].dtype)
    return out
```

```python
from contextlib import ExitStack

import concourse.bass as bass
from concourse import mybir

F32 = mybir.dt.float32
BF16 = mybir.dt.bfloat16
FP16 = mybir.dt.float16
I32 = mybir.dt.int32
U32 = mybir.dt.uint32
ALU = mybir.AluOpType
ACT = mybir.ActivationFunctionType
AX = mybir.AxisListType.X

N = 625
D = 512
P = 128
KC = D // P
NC = 5
NP = N // NC
EDGES = 20000
ET = EDGES // NP
EG = ET // 2
EX = 8
FF = 2048
FC = FF // P
TT = 64
MAXT = (N + EX * (TT - 1)) // TT
KT = -(-N // TT)
F1 = 128
HD = 64
PAIRS = D // (2 * HD)
ASCALE = HD ** -0.5
HALF = [(0, 313), (313, 312)]
WIDE = [(0, 512), (512, 113)]
NEG = -1.0e30
EPS = 1e-5

COLS = {}
_n = 0
for _name, _w in [("mix_bq", 4), ("ffn_bq", 4), ("ffn_bk", 4)] + [
        (f"{v}{l}", w) for l in range(2) for v, w in
        [("bq", 4), ("bo", 4), ("b1", 1), ("b2", 4), ("g1", 4), ("beta1", 4), ("g2", 4), ("beta2", 4)]] + [
        ("moe_b1", EX * FC), ("l1_b1", EX)]:
    COLS[_name] = (_n, _w)
    _n += _w
NCOL = _n
ROWS = {n: i for i, n in enumerate(
    ["mix_bk", "mix_bv", "mix_bp", "ffn_bv", "ffn_bo", "ln1_g", "ln1_b", "ln_g", "ln_b", "proj_b"])}
RING = [("gnnW", "hp"), ("mixWq", "mq"), ("mixWk", "mk"), ("mixWv", "mv"), ("mixWp", "mp"), ("ffnWo", "ao"),
        ("gnnWo0", "wo0"), ("gnnWo1", "wo1"), ("m1q", "nq"), ("m1k", "nk"), ("m1v", "nv"), ("m1p", "np")]

STAGES = [
    ("xnT0", 5, "a"), ("hp", 5, "a"), ("WT", 10, "av"), ("agg", 5, "v"),
    ("mq", 8, "v"), ("mk", 5, "v"), ("mv", 5, "v"), ("mkv", 4, "v"), ("mo", 10, "v"), ("moT", 5, "a"),
    ("mp", 5, "v"), ("yT", 5, "a"), ("ao", 5, "v"), ("tT", 5, "a"), ("gate0", 1, "v"), ("rank", 1, "v"),
    ("xnT1", 5, "a"),
    ("wo0", 8, "v"), ("ffa0", 2, "a"), ("ffb0", 8, "v"),
    ("wo1", 8, "v"), ("ffa1", 2, "a"), ("ffb1", 8, "v"), ("gN", 5, "a"),
    ("nq", 8, "a"), ("nk", 5, "a"), ("nv", 5, "a"), ("nkv", 4, "v"), ("no", 10, "v"), ("noT", 5, "a"),
    ("np", 5, "v"), ("zT", 5, "a"), ("gate1", 1, "v"), ("pb", 4, "a"), ("h1", 16, "v"), ("o1", 5, "v"),
]
UNIT = []
FIRST = {}
COUNT = {s: k for s, k, _ in STAGES}
for _s, _k, _e in STAGES:
    FIRST[_s] = len(UNIT)
    UNIT += [_e[i % len(_e)] for i in range(_k)]


def freed_count(engine, unit):
    return sum(e == engine for e in UNIT[:unit + 1])


def build(nc, ins, out):
    ctx = ExitStack()
    with ctx:
        def sem(name):
            return ctx.enter_context(nc.semaphore(name))

        def sb(name, shape, dt=F32):
            return ctx.enter_context(nc.sbuf_tensor(name, shape, dt))

        xres = sb("xres", [NP, NC, D])
        cnt_adj = sb("cnt_adj", [NP, NC, N])
        ident = sb("ident", [P, P])
        cols = sb("cols", [P, NCOL])
        rows = sb("rows", [NP, len(ROWS), D])
        gate_b = sb("gate_b", [NP, EX])
        onesf = sb("onesf", [P, P])
        upper = sb("upper", [NP, NP])
        twos = sb("twos", [EX, NP])
        b2rows = sb("b2rows", [EX, D])
        gateW = sb("gateW", [P, KC, EX])
        gateW1 = sb("gateW1", [P, KC, EX])
        ffW1 = sb("ffW1", [P, KC, F1])
        ffW2 = sb("ffW2", [P, D])
        small = sb("small", [P, 640])
        idx = sb("idx", [NP, NC], U32)
        bounds = sb("bounds", [1, 2, EX], I32)
        tiles = sb("tiles", [1, 3, EX], I32)
        AR = 8192 + 30901
        arena = sb("arena", [P, AR])

        def at(off, p, *dims):
            n = 1
            for d in dims:
                n *= d
            v = arena[0:p, off:off + n]
            if len(dims) == 2:
                return v.rearrange("p (a b) -> p a b", b=dims[1])
            if len(dims) == 3:
                return v.rearrange("p (a b c) -> p a b c", b=dims[1], c=dims[2])
            return v

        o_ring = 8192
        o_T = o_ring + 2 * KC * D
        o_N = o_T + 3 * KC * N
        o_A = o_N + 3 * NC * D
        o_M = o_A + 8500
        ring = [at(o_ring + i * KC * D, P, KC, D) for i in range(2)]
        T1, T2, T3 = [at(o_T + i * KC * N, P, KC, N) for i in range(3)]
        N1, N2, N3 = [at(o_N + i * NC * D, NP, NC, D) for i in range(3)]
        maskb = at(o_M, NP, NC, N)
        assert o_M + NC * N <= AR
        Wrows = maskb
        WT = at(o_T + KC * N, NP, NC, N)
        oa = [o_A]

        def take(p, *dims, dt=F32):
            n = 1
            for d in dims:
                n *= d
            w = n if dt in (F32, I32) else (n + 1) // 2
            v = arena[0:p, oa[0]:oa[0] + w]
            oa[0] += w
            assert oa[0] <= o_M
            if dt != F32:
                v = v.bitcast(dt)[:, 0:n]
            if len(dims) == 2:
                return v.rearrange("p (a b) -> p a b", b=dims[1])
            if len(dims) == 3:
                return v.rearrange("p (a b c) -> p a b c", b=dims[1], c=dims[2])
            return v

        srci, dsti = take(NP, ET, dt=I32), take(NP, ET, dt=I32)
        wgt = take(NP, ET)
        srcf, dstf, dstr = take(NP, ET), take(NP, ET), take(NP, NC, ET)
        wpart, wrest = take(NP, 3, ET), take(NP, 2, ET)
        wbf = take(NP, ET, dt=BF16)
        ind, ind2 = take(NP, NC, ET), take(NP, NC, ET)
        iota_src, iota_dst = take(NP, N + 1, dt=FP16), take(NP, NP + 1, dt=BF16)
        one_dst, one_src = take(NP, 2, 4, P, dt=BF16), take(NP, 2, N + 1, dt=BF16)
        zero_bf = take(NP, P, dt=BF16)
        zero_rows_sb = take(TT, D)
        iota_g = at(o_A + 6500, 1, 2, EG)
        g_cnt, g_a, g_b = [at(o_A + 6700 + 400 * i, 1, NC, EG) for i in range(3)]
        g_lo, g_hi, g_n = [at(o_A + 7900 + 8 * i, 1, NC) for i in range(3)]
        assert oa[0] <= o_A + 6500
        oa[0] = o_A
        aw = take(P, 3, KC, P)
        qt, kt = take(P, N), take(P, N)
        vv = take(NP, NC, P)
        Sp, Pr, PTs = [take(NP, 2, N) for _ in range(3)]
        actx = take(NP, NC, P)
        oa[0] = o_A
        fm = take(P, 4, D)
        bd = take(P, KC, 132)
        mz = take(NP, 2, 8)
        hid = at(o_A, P, N)
        EW1 = [at(0, P, KC, FF), at(o_ring + 8192, P, KC, FF)]
        EW2 = [at(o_ring, P, FC, D), at(o_ring + 16384, P, FC, D)]
        o_E = o_ring + 3 * 8192
        xs = at(o_E, TT, D)
        xsT = at(o_E + 1024, P, KC, TT)
        hT = at(o_E + 1280, P, FC, TT)
        hs = at(o_E + 2304, P, FF // 2)
        ys = at(o_E + 3328, P, D // 2)
        eb2 = [at(o_E + 3584 + i * D // 2, P, D // 2) for i in range(2)]
        assert o_E + 3584 + D <= AR
        yg = at(o_N, NP, NC, D)
        l1W1 = at(0, P, KC, EX * F1)
        l1W2 = at(4096, P, EX, D)
        oa[0] = o_A
        pbl = take(NP, 2, NC, P)
        PB = take(P, 2, N)
        hb = take(P, 4, 320)
        h1T = at(o_T + KC * N, P, EX, N)

        psum = ctx.enter_context(nc.psum_tensor("psum", [P, 8 * 512], F32))

        def bank(b, p, w, off=0):
            return psum[0:p, 512 * b + off:512 * b + off + w]

        xs_dram = nc.dram_tensor("token_rows", [(MAXT + 2) * TT, D], F32, kind="Internal").ap()
        ys_dram = nc.dram_tensor("expert_rows", [MAXT * TT, D], F32, kind="Internal").ap()

        unit_full, freed_a, freed_v = sem("unit_full"), sem("freed_a"), sem("freed_v")
        ld_edges, ld_x, ld_const = sem("ld_edges"), sem("ld_x"), sem("ld_const")
        ld_ring = [sem(f"ld_ring{i}") for i in range(2)]
        ld_ff = sem("ld_ff")
        consts = sem("consts")
        dve, actc = sem("dve"), sem("actc")
        ln_var, ln_sd, ln_out = sem("ln_var"), sem("ln_sd"), sem("ln_out")
        bn_var, bn_sd, bn_out = sem("bn_var"), sem("bn_sd"), sem("bn_out")
        range_full, range_ready, chunk_ind = sem("range_full"), sem("range_ready"), sem("chunk_ind")
        hot_ready = [sem(f"hot_ready{c}") for c in range(NC)]
        hot_free = [sem(f"hot_free{c}") for c in range(NC)]
        adj_full, adj_out = sem("adj_full"), sem("adj_out")
        fm_min, fm_exp = sem("fm_min"), sem("fm_exp")
        bd_zero = sem("bd_zero")
        mask_ready = sem("mask_ready")
        A = []
        for a in range(3):
            A.append({n: sem(f"att{a}_{n}") for n in (
                "w", "proj", "qk", "v", "score", "max", "exp", "prob", "pT", "pTa", "pTv", "av", "ctx", "chain")})
        gates_ready, slots_ready, scattered, gathered, zero_rows = (
            sem("gates_ready"), sem("slots_ready"), sem("scattered"), sem("gathered"), sem("zero_rows"))
        M = {n: sem(f"moe_{n}") for n in (
            "first0", "first1", "second0", "second1", "xs", "xsT", "xsTa", "h", "hs", "hT", "ha", "y", "yv",
            "st", "done")}
        p_top, pb_l = sem("p_top"), sem("pb_l")
        gl_in, gl_out = sem("gl_in"), sem("gl_out")
        h_in, h_g = sem("h_in"), sem("h_g")
        l1w, b2w = sem("l1w"), sem("b2w")
        x_done, stored = sem("x_done"), sem("stored")

        def full(eng, stage, i):
            eng.wait_ge(unit_full, FIRST[stage] + i % COUNT[stage] + 1)

        def stage_out(eng, stage, upto=None):
            last = FIRST[stage] + (COUNT[stage] if upto is None else upto) - 1
            for e, s in (("a", freed_a), ("v", freed_v)):
                if e in UNIT[FIRST[stage]:last + 1]:
                    eng.wait_ge(s, freed_count(e, last))

        def unit_bank(stage, i):
            return (FIRST[stage] + i) % 8

        def out_sem(stage, i):
            return freed_a if UNIT[FIRST[stage] + i] == "a" else freed_v

        block = ctx.enter_context(nc.Block())
        col = lambda name, i=0: cols[:, COLS[name][0] + i:COLS[name][0] + i + 1]
        row = lambda name: rows[:, ROWS[name], :]

        @block.sync
        def _(sp):
            sp.dma_start(srci, ins["src"]).then_inc(ld_edges, 16)
            sp.dma_start(dsti, ins["dst"]).then_inc(ld_edges, 16)
            sp.dma_start(wgt, ins["edge_w"]).then_inc(ld_edges, 16)
            sp.dma_start(xres[:], ins["x"]).then_inc(ld_x, 16)
            sp.dma_start(ring[0], ins["gnnW"]).then_inc(ld_ring[0], 16)
            sp.dma_start(ring[1], ins["mixWq"]).then_inc(ld_ring[1], 16)
            sp.dma_start(cols[:], ins["cols"]).then_inc(ld_const, 16)
            sp.dma_start(rows[:], ins["rows"].partition_broadcast(NP)).then_inc(ld_const, 16)
            sp.dma_start(gate_b[:], ins["gate_b"].partition_broadcast(NP)).then_inc(ld_const, 16)
            sp.dma_start(b2rows[:], ins["l1_b2"]).then_inc(ld_const, 16)
            sp.dma_start(gateW[:], ins["gateW"]).then_inc(ld_const, 16)
            sp.dma_start(gateW1[:], ins["gateW1"]).then_inc(ld_const, 16)
            sp.dma_start(EW1[0], ins["moeW1"][0]).then_inc(M["first0"], 16)

            def ring_load(n):
                full(sp, RING[n - 2][1], -1)
                sp.dma_start(ring[n % 2], ins[RING[n][0]]).then_inc(ld_ring[n % 2], 16)

            def attention_loads(a, name):
                with sp.Fori(0, PAIRS) as i:
                    sp.wait_ge(A[a]["proj"], i * 3 + 1)
                    sp.dma_start(aw, ins[name][i]).then_inc(A[a]["w"], 16)

            for n in range(2, 6):
                ring_load(n)
            stage_out(sp, "yT")
            sp.wait_ge(zero_rows, 16 * (2 * MAXT + 1))
            sp.wait_ge(M["st"], 16)
            attention_loads(0, "att0")

            def first_weights(buf, expert):
                sp.dma_start(EW1[buf], ins["moeW1"][expert]).then_inc(M[f"first{buf}"], 16)

            def second_weights(buf, expert):
                sp.dma_start(EW2[buf], ins["moeW2"][expert]).then_inc(M[f"second{buf}"], 16)
                for q in range(2):
                    sp.dma_start(eb2[buf][q * TT:(q + 1) * TT, :],
                                 ins["moe_b2"][expert, q * (D // 2):(q + 1) * (D // 2)].partition_broadcast(TT)
                                 ).then_inc(M[f"second{buf}"], 16)

            full(sp, "ao", -1)
            second_weights(0, 0)
            full(sp, "gate0", -1)
            first_weights(1, 1)
            sp.wait_ge(scattered, 16 * NC)
            second_weights(1, 1)
            with sp.Fori(0, EX // 2 - 1) as i:
                for buf in range(2):
                    end = sp.value_load(tiles[0:1, 1, bass.ds(i * 2 + (buf + 1), 1)], min_val=1, max_val=MAXT)
                    sp.wait_ge(M["h"], end * 2)
                    first_weights(buf, i * 2 + (buf + 2))
                    sp.wait_ge(M["yv"], end + 1)
                    second_weights(buf, i * 2 + (buf + 2))
            end = sp.value_load(tiles[0:1, 2, 0:1], min_val=EX, max_val=MAXT)
            sp.wait_ge(M["yv"], end + 1)
            sp.dma_start(l1W1, ins["l1W1"]).then_inc(l1w, 16)
            sp.dma_start(l1W2, ins["l1W2"]).then_inc(l1w, 16)
            sp.wait_ge(M["done"], 1)
            for n in range(6, 8):
                ring_load(n)
            for l in range(2):
                if l:
                    full(sp, f"ffb{l - 1}", -1)
                sp.dma_start(ffW1[:], ins[f"ffW1_{l}"]).then_inc(ld_ff, 16)
                sp.dma_start(ffW2[:], ins[f"ffW2_{l}"]).then_inc(ld_ff, 16)
                if l:
                    stage_out(sp, f"ffa{l - 1}")
                    stage_out(sp, f"ffb{l - 1}")
                attention_loads(1 + l, f"att{1 + l}")
            for n in range(8, 12):
                ring_load(n)
            sp.wait_ge(x_done, NC)
            sp.dma_start(out, xres[:]).then_inc(stored, 16)
            sp.wait_ge(stored, 16)

        @block.gpsimd
        def _(pool):
            pool.iota(iota_src[:, 0:N], [[1, N]], base=0, channel_multiplier=0,
                      allow_small_or_imprecise_dtypes=True).then_inc(consts, 1)
            pool.iota(iota_dst[:, 0:NP], [[1, NP]], base=0, channel_multiplier=0,
                      allow_small_or_imprecise_dtypes=True).then_inc(consts, 1)
            pool.iota(iota_g[:, 0, :], [[1, EG]], base=1, channel_multiplier=0,
                      allow_small_or_imprecise_dtypes=True).then_inc(consts, 1)
            pool.iota(iota_g[:, 1, :], [[-1, EG]], base=EG, channel_multiplier=0,
                      allow_small_or_imprecise_dtypes=True).then_inc(consts, 1)
            pool.memset(onesf[:], 1.0).then_inc(consts, 1)
            pool.memset(zero_bf, 0.0).then_inc(consts, 1)
            pool.memset(twos[:], 2.0).then_inc(consts, 1)
            pool.memset(ident[:], 0.0).then_inc(consts, 1)
            pool.memset(zero_rows_sb, 0.0).then_inc(consts, 1)
            pool.wait_ge(consts, 9)
            pool.affine_select(out=ident[:], in_=ident[:], compare_op=ALU.not_equal, fill=1.0, base=0,
                               pattern=[[-1, P]], channel_multiplier=1).then_inc(consts, 1)
            pool.affine_select(out=upper[:], in_=onesf[0:NP, 0:NP], compare_op=ALU.is_gt, fill=0.0, base=0,
                               pattern=[[1, NP]], channel_multiplier=-1).then_inc(consts, 1)
            for t in range(MAXT + 2):
                pool.dma_start(xs_dram[t * TT:(t + 1) * TT, :], zero_rows_sb).then_inc(
                    zero_rows if t <= MAXT else M["st"], 16)
                if t < MAXT:
                    pool.dma_start(ys_dram[t * TT:(t + 1) * TT, :], zero_rows_sb).then_inc(zero_rows, 16)
            pool.wait_ge(adj_out, 4 * NC)
            pool.memset(bd[:, :, :], 0.0).then_inc(bd_zero, 1)
            pool.wait_ge(zero_rows, 16 * (2 * MAXT + 1))
            pool.wait_ge(M["st"], 16)
            pool.wait_ge(slots_ready, 1)
            for c in range(NC):
                pool.indirect_dma_start(
                    out=xs_dram, out_offset=bass.IndirectOffsetOnAxis(ap=idx[:, c:c + 1], axis=0),
                    in_=N3[:, c, :], in_offset=None).then_inc(scattered, 16)
            pool.wait_ge(scattered, 16 * NC)
            pool.dma_start(xs, xs_dram[0:TT, :]).then_inc(M["xs"], 16)
            pool.wait_ge(M["xsT"], 1)
            pool.dma_start(xs, xs_dram[TT:2 * TT, :]).then_inc(M["xs"], 16)
            total_tiles = pool.value_load(tiles[0:1, 2, 0:1], min_val=EX, max_val=MAXT)
            with pool.Fori(0, total_tiles) as g:
                pool.wait_ge(M["xsT"], g + 2)
                pool.dma_start(xs, xs_dram[bass.ds((g + 2) * TT, TT), :]).then_inc(M["xs"], 16)
                pool.wait_ge(M["yv"], g + 2)
                for q in range(2):
                    pool.dma_start(ys_dram[bass.ds(g * TT, TT), q * (D // 2):(q + 1) * (D // 2)],
                                   ys[q * TT:(q + 1) * TT, :]).then_inc(M["st"], 16)
            pool.wait_ge(M["st"], total_tiles * 32 + 16)
            pool.wait_ge(M["xs"], total_tiles * 16 + 32)
            pool.nop().then_inc(M["done"], 1)
            for c in range(NC):
                pool.indirect_dma_start(
                    out=yg[:, c, :], out_offset=None, in_=ys_dram,
                    in_offset=bass.IndirectOffsetOnAxis(ap=idx[:, c:c + 1], axis=0)).then_inc(gathered, 16)
            stage_out(pool, "ffb1")
            pool.memset(bd[:, :, :], 0.0).then_inc(bd_zero, 1)

        @block.tensor
        def _(pe):
            def take_bank(stage, i):
                n = FIRST[stage] + i
                if n >= 8:
                    e = UNIT[n - 8]
                    pe.wait_ge(freed_a if e == "a" else freed_v, freed_count(e, n - 8))
                return n % 8

            def rows_to_cols(stage, src, ready):
                for c in range(NC):
                    ready(c)
                    b = take_bank(stage, c)
                    for k in range(KC):
                        mm = pe.transpose(bank(b, P, NP, NP * k), src[:, c, k * P:(k + 1) * P], ident[0:NP, 0:NP])
                    mm.then_inc(unit_full, 1)

            def ring_ready(n):
                pe.wait_ge(ld_ring[n % 2], 16 * (n // 2 + 1))

            def product_rows(stage, srcT, n):
                ring_ready(n)
                for c in range(NC):
                    b = take_bank(stage, c)
                    for k in range(KC):
                        mm = pe.matmul(bank(b, NP, D), srcT[:, k, c * NP:(c + 1) * NP], ring[n % 2][:, k, :],
                                       start=(k == 0), stop=(k == KC - 1))
                    mm.then_inc(unit_full, 1)

            def product_cols(stage, srcT, n):
                ring_ready(n)
                for m in range(KC):
                    for h, (o, w) in enumerate(HALF):
                        b = take_bank(stage, 2 * m + h)
                        for k in range(KC):
                            mm = pe.matmul(bank(b, P, w), ring[n % 2][:, k, m * P:(m + 1) * P],
                                           srcT[:, k, o:o + w], start=(k == 0), stop=(k == KC - 1))
                        mm.then_inc(unit_full, 1)

            pe.wait_ge(consts, 11)
            rows_to_cols("xnT0", N1, lambda c: pe.wait_ge(ln_out, c + 1))
            stage_out(pe, "xnT0")
            product_rows("hp", T1, 0)

            pe.wait_ge(chunk_ind, 1)
            stage_out(pe, "hp")
            for h in range(2):
                pe.matmul(bank(h, 1, 400), onesf[0:NP, 0:1],
                          ind2.rearrange("p c t -> p (c t)")[:, 400 * h:400 * h + 400],
                          start=True, stop=True).then_inc(range_full, 1)
            pe.wait_ge(range_ready, 1)
            for c in range(NC):
                k = pe.value_load(bounds[0:1, 1, c:c + 1], min_val=1, max_val=EG)
                b0 = 4 * (c % 2)
                if c >= 2:
                    pe.wait_ge(adj_out, 4 * (c - 1))
                for q in range(4):
                    w = WIDE[q % 2][1]
                    mm = pe.matmul(bank(b0 + q, NP, w), zero_bf[:, 0:NP], iota_src[:, 0:w],
                                   start=True, stop=False, skip_group_check=True)
                    if q >= 2:
                        mm.then_inc(hot_free[c], 1)
                with pe.Fori(0, k) as j:
                    for s in range(2):
                        pe.wait_ge(hot_ready[c], j * 2 + s + 1)
                        for v in range(4):
                            for h, (o, w) in enumerate(WIDE):
                                mm = pe.matmul(bank(b0 + (2 if v == 3 else 0) + h, NP, w), one_dst[:, s, v, 0:NP],
                                               one_src[:, s, o:o + w], start=False, stop=False,
                                               skip_group_check=True)
                        mm.then_inc(hot_free[c], 1)
                for q in range(4):
                    w = WIDE[q % 2][1]
                    mm = pe.matmul(bank(b0 + q, NP, w), zero_bf[:, 0:NP], iota_src[:, 0:w],
                                   start=False, stop=True, skip_group_check=True)
                mm.then_inc(adj_full, 1)
            pe.wait_ge(adj_out, 4 * NC)
            for s in range(NC):
                for h in range(2):
                    b = take_bank("WT", 2 * s + h)
                    for c in (range(4) if h == 0 else [4]):
                        mm = pe.transpose(bank(b, NP, NP, NP * (c % 4)), Wrows[:, c, s * NP:(s + 1) * NP],
                                          ident[0:NP, 0:NP])
                    mm.then_inc(unit_full, 1)
            stage_out(pe, "WT")
            for c in range(NC):
                b = take_bank("agg", c)
                for s in range(NC):
                    mm = pe.matmul(bank(b, NP, D), WT[:, s, c * NP:(c + 1) * NP], N2[:, s, :],
                                   start=(s == 0), stop=(s == NC - 1))
                mm.then_inc(unit_full, 1)

            product_cols("mq", T1, 1)
            product_rows("mk", T1, 2)
            product_rows("mv", T1, 3)

            def key_values(stage, kr, vr):
                for m in range(KC):
                    b = take_bank(stage, m)
                    for c in range(NC):
                        pe.matmul(bank(b, P, P), kr[:, c, m * P:(m + 1) * P], vr[:, c, m * P:(m + 1) * P],
                                  start=(c == 0), stop=(c == NC - 1))
                    for c in range(NC):
                        mm = pe.matmul(bank(b, P, 1, P), kr[:, c, m * P:(m + 1) * P], onesf[0:NP, 0:1],
                                       start=(c == 0), stop=(c == NC - 1))
                    mm.then_inc(unit_full, 1)

            def query_products(stage, qT, w):
                for c in range(NC):
                    for h in range(2):
                        b = take_bank(stage, 2 * c + h)
                        for m in (2 * h, 2 * h + 1):
                            mm = pe.matmul(bank(b, NP, w, w * (m % 2)), qT[:, m, c * NP:(c + 1) * NP],
                                           bd[:, m, 0:w], start=True, stop=True)
                        mm.then_inc(unit_full, 1)

            stage_out(pe, "mk")
            stage_out(pe, "mv")
            key_values("mkv", N1, N3)
            stage_out(pe, "mq")
            stage_out(pe, "mkv")
            query_products("mo", T2, 130)
            rows_to_cols("moT", N2, lambda c: stage_out(pe, "mo", 2 * c + 2))
            stage_out(pe, "moT")
            product_rows("mp", T3, 4)
            rows_to_cols("yT", N1, lambda c: pe.wait_ge(ln_out, NC + c + 1))
            stage_out(pe, "yT")

            def attention(a, srcT):
                s = A[a]
                for first in ("proj", "pT", "av"):
                    pe.nop().then_inc(s[first], 1)
                with pe.Fori(0, PAIRS) as i:
                    pe.wait_ge(s["w"], i * 16 + 16)
                    pe.wait_ge(s["pTa"], i * 11 + 1)
                    pe.wait_ge(s["pTv"], i * 11 + 1)
                    pe.wait_ge(s["ctx"], i * 10 + 1)
                    for w, b0 in ((0, 4), (1, 6)):
                        for h, (o, n) in enumerate(WIDE):
                            for k in range(KC):
                                mm = pe.matmul(bank(b0 + h, P, n), aw[:, w, k, :], srcT[:, k, o:o + n],
                                               start=(k == 0), stop=(k == KC - 1))
                        mm.then_inc(s["proj"], 1)
                    for c in range(NC):
                        for k in range(KC):
                            mm = pe.matmul(bank(0, NP, P, P * c), srcT[:, k, c * NP:(c + 1) * NP], aw[:, 2, k, :],
                                           start=(k == 0), stop=(k == KC - 1))
                    mm.then_inc(s["proj"], 1)
                    pe.wait_ge(s["qk"], i * 2 + 2)
                    pe.wait_ge(s["v"], i + 1)
                    for t in range(13):
                        if t < 10:
                            hh, c = divmod(t, NC)
                            if t >= 2:
                                pe.wait_ge(s["exp"], i * 10 + t - 1)
                            for h, (o, n) in enumerate(WIDE):
                                mm = pe.matmul(bank(2 * (t % 2) + h, NP, n),
                                               qt[hh * HD:(hh + 1) * HD, c * NP:(c + 1) * NP],
                                               kt[hh * HD:(hh + 1) * HD, o:o + n], start=True, stop=True)
                            mm.then_inc(s["score"], 1)
                        if 2 <= t < 12:
                            u = t - 2
                            pe.wait_ge(s["prob"] if a else s["exp"], i * 10 + u + 1)
                            if u >= 1:
                                pe.wait_ge(s["pTa"], i * 11 + u + 1)
                                pe.wait_ge(s["pTv"], i * 11 + u + 1)
                            for j in range(NC):
                                mm = pe.transpose(bank(4 + j // 4, NP, NP, NP * (j % 4)),
                                                  Pr[:, u % 2, j * NP:(j + 1) * NP], ident[0:NP, 0:NP])
                            mm.then_inc(s["pT"], 1)
                        if t >= 3:
                            u = t - 3
                            hh, c = divmod(u, NC)
                            pe.wait_ge(s["pTa"], i * 11 + u + 2)
                            pe.wait_ge(s["pTv"], i * 11 + u + 2)
                            if u >= 2:
                                pe.wait_ge(s["ctx"], i * 10 + u)
                            for j in range(NC):
                                mm = pe.matmul(bank(6 + u % 2, NP, HD), PTs[:, u % 2, j * NP:(j + 1) * NP],
                                               vv[:, j, hh * HD:(hh + 1) * HD], start=(j == 0), stop=(j == NC - 1))
                            mm.then_inc(s["av"], 1)
                    pe.wait_ge(s["ctx"], i * 10 + 11)
                    for j in range(NC):
                        mm = pe.transpose(bank(4 + j // 4, P, NP, NP * (j % 4)), actx[:, j, :], ident[0:NP, 0:NP])
                    mm.then_inc(s["pT"], 1)
                pe.wait_ge(s["pTa"], 11 * PAIRS + 1)
                pe.wait_ge(s["pTv"], 11 * PAIRS + 1)

            attention(0, T1)
            product_rows("ao", T2, 5)
            rows_to_cols("tT", N3, lambda c: pe.wait_ge(ln_out, 2 * NC + c + 1))
            stage_out(pe, "tT")

            def gates(stage, srcT, W):
                b = take_bank(stage, 0)
                for c in range(NC):
                    for k in range(KC):
                        mm = pe.matmul(bank(b, NP, EX, EX * c), srcT[:, k, c * NP:(c + 1) * NP], W[:, k, :],
                                       start=(k == 0), stop=(k == KC - 1))
                mm.then_inc(unit_full, 1)

            pe.wait_ge(ld_const, 16 * 6)
            gates("gate0", T3, gateW)
            pe.wait_ge(gates_ready, 1)
            b = take_bank("rank", 0)
            onehot = small[0:NP, 200:240].rearrange("p (c e) -> p c e", e=EX)
            for c in range(NC + 1):
                for s in range(min(c + 1, NC)):
                    mm = pe.matmul(bank(b, NP, EX, EX * c), upper[:] if s == c else onesf[0:NP, 0:NP],
                                   onehot[:, s, :], start=(s == 0), stop=(s == min(c, NC - 1)))
            mm.then_inc(unit_full, 1)

            pe.wait_ge(slots_ready, 1)
            pe.nop().then_inc(M["y"], 1)

            def tile_columns(n):
                pe.wait_ge(M["xs"], n * 16 + 16)
                pe.matmul(bank(5, P, TT), xs[:, 0:P], ident[0:TT, 0:TT], start=True, stop=True)
                for k4 in range(1, KC):
                    mm = pe.transpose(bank(5, P, TT, TT * k4), xs[:, k4 * P:(k4 + 1) * P], ident[0:TT, 0:TT])
                mm.then_inc(M["xsT"], 1)

            tile_columns(0)
            with pe.Fori(0, EX // 2) as i:
                for par in range(2):
                    k = pe.value_load(tiles[0:1, 0, bass.ds(i * 2 + par, 1)], min_val=1, max_val=KT)
                    b0 = pe.value_load(tiles[0:1, 1, bass.ds(i * 2 + par, 1)], min_val=0, max_val=MAXT - 1)
                    with pe.Fori(0, k) as j:
                        g = b0 + j
                        pe.wait_ge(M[f"first{par}"], i * 16 + 16)
                        pe.wait_ge(M["xsTa"], g + 1)
                        for b in range(2):
                            for k4 in range(KC):
                                for q in range(2):
                                    o = q * (FF // 2) + b * D
                                    mm = pe.matmul(psum[q * TT:(q + 1) * TT, 512 * b:512 * b + D], xsT[:, k4, :],
                                                   EW1[par][:, k4, o:o + D], start=(k4 == 0), stop=(k4 == KC - 1))
                            mm.then_inc(M["h"], 1)
                        for b in range(2):
                            pe.wait_ge(M["hs"], g * 2 + b + 1)
                            for j4 in range(4):
                                mm = pe.transpose(bank(2 + b, P, P, P * j4), hs[:, b * D + j4 * P:b * D + (j4 + 1) * P],
                                                  ident[:, :])
                            mm.then_inc(M["hT"], 1)
                            if b == 0:
                                tile_columns(g + 1)
                        pe.wait_ge(M[f"second{par}"], i * 48 + 48)
                        pe.wait_ge(M["yv"], g + 1)
                        for n in range(FC):
                            b, j4, q_ = n // 8, n // 2 % 4, n % 2
                            f = q_ * (FC // 2) + b * 4 + j4
                            if q_ == 0:
                                pe.wait_ge(M["ha"], g * 8 + n // 2 + 1)
                            for q in range(2):
                                mm = pe.matmul(psum[q * TT:(q + 1) * TT, 4 * 512:4 * 512 + D // 2], hT[:, f, :],
                                               EW2[par][:, f, q * (D // 2):(q + 1) * (D // 2)],
                                               start=(n == 0), stop=(n == FC - 1))
                        mm.then_inc(M["y"], 1)

            rows_to_cols("xnT1", N2, lambda c: pe.wait_ge(ln_out, 3 * NC + c + 1))
            stage_out(pe, "xnT1")
            for l in range(2):
                attention(1 + l, T1 if l == 0 else T2)
                product_cols(f"wo{l}", T3, 6 + l)
                pe.wait_ge(bn_out, 8 * l + 4)
                pe.wait_ge(ld_ff, 32 * (l + 1))
                for h, (o, w) in enumerate(HALF):
                    b = take_bank(f"ffa{l}", h)
                    for k in range(KC):
                        mm = pe.matmul(bank(b, P, w), ffW1[:, k, :], T2[:, k, o:o + w], start=(k == 0), stop=(k == KC - 1))
                    mm.then_inc(unit_full, 1)
                stage_out(pe, f"ffa{l}")
                for m in range(KC):
                    for h, (o, w) in enumerate(HALF):
                        b = take_bank(f"ffb{l}", 2 * m + h)
                        mm = pe.matmul(bank(b, P, w), ffW2[:, m * P:(m + 1) * P], hid[:, o:o + w], start=True, stop=True)
                        mm.then_inc(unit_full, 1)
                pe.wait_ge(bn_out, 8 * l + 8)
            for c in range(NC):
                b = take_bank("gN", c)
                for k in range(KC):
                    mm = pe.transpose(bank(b, NP, P, P * k), T2[:, k, c * NP:(c + 1) * NP], ident[:, :])
                mm.then_inc(unit_full, 1)

            product_cols("nq", T1, 8)
            product_rows("nk", T1, 9)
            product_rows("nv", T1, 10)
            stage_out(pe, "nk")
            stage_out(pe, "nv")
            key_values("nkv", N1, N3)
            stage_out(pe, "nq")
            stage_out(pe, "nkv")
            query_products("no", T3, 132)
            rows_to_cols("noT", N2, lambda c: stage_out(pe, "no", 2 * c + 2))
            stage_out(pe, "noT")
            product_rows("np", T2, 11)

            rows_to_cols("zT", N1, lambda c: pe.wait_ge(ln_out, 5 * NC + c + 1))
            stage_out(pe, "zT")
            gates("gate1", T1, gateW1)
            pe.wait_ge(pb_l, 2)
            for w in range(2):
                for h in range(2):
                    b = take_bank("pb", 2 * w + h)
                    for c in (range(4) if h == 0 else [4]):
                        mm = pe.matmul(bank(b, P, NP, NP * (c % 4)), pbl[:, w, c, :], ident[0:NP, 0:NP],
                                       start=True, stop=True)
                    mm.then_inc(unit_full, 1)
            pe.wait_ge(l1w, 32)
            for f in range(EX):
                for h, (o, w) in enumerate(HALF):
                    b = take_bank("h1", 2 * f + h)
                    for k in range(KC):
                        mm = pe.matmul(bank(b, P, w), l1W1[:, k, f * P:(f + 1) * P], T1[:, k, o:o + w],
                                       start=(k == 0), stop=(k == KC - 1))
                    mm.then_inc(unit_full, 1)
            stage_out(pe, "h1")
            for c in range(NC):
                b = take_bank("o1", c)
                for f in range(EX):
                    pe.matmul(bank(b, NP, D), h1T[:, f, c * NP:(c + 1) * NP], l1W2[:, f, :], start=(f == 0), stop=False)
                pe.matmul(bank(b, NP, D), twos[:], b2rows[:], start=False, stop=True).then_inc(unit_full, 1)

        @block.scalar
        def _(act):
            def chunk_view(b):
                return bank(b, P, KC * NP).rearrange("p (k n) -> p k n", k=KC)

            def cols_out(stage, dst):
                for c in range(NC):
                    full(act, stage, c)
                    act.activation(dst[:, :, c * NP:(c + 1) * NP], chunk_view(unit_bank(stage, c)),
                                   ACT.Copy).then_inc(freed_a, 1)

            def rows_out(stage, dst, func=ACT.Copy):
                for c in range(NC):
                    full(act, stage, c)
                    act.activation(dst[:, c, :], bank(unit_bank(stage, c), NP, D), func).then_inc(freed_a, 1)

            def deviation(n):
                act.wait_ge(ln_var, n + 1)
                act.activation(small[0:NP, 40:45], small[0:NP, 30:35], ACT.Sqrt).then_inc(ln_sd, 1)

            deviation(0)
            cols_out("xnT0", T1)
            rows_out("hp", N2)
            for c in range(NC):
                act.wait_ge(adj_full, c + 1)
                b0 = 4 * (c % 2)
                for q in range(4):
                    o, w = WIDE[q % 2]
                    dst = (Wrows if q < 2 else cnt_adj)[:, c, o:o + w]
                    act.activation(dst, bank(b0 + q, NP, w), ACT.Copy).then_inc(adj_out, 1)
            for s in range(NC):
                full(act, "WT", 2 * s)
                act.activation(WT[:, s, 0:4 * NP], bank(unit_bank("WT", 2 * s), NP, 4 * NP), ACT.Copy).then_inc(freed_a, 1)
            for n in range(8 + NC):
                act.wait_ge(fm_min, n + 1)
                p, w = (P, HALF[n % 2][1]) if n < 8 else (NP, D)
                act.activation(fm[0:p, 1, 0:w], fm[0:p, 0, 0:w], ACT.Exp).then_inc(fm_exp, 1)
            cols_out("moT", T3)
            deviation(1)
            cols_out("yT", T1)

            def attention(a, bq, bk, dst):
                s = A[a]
                act.nop().then_inc(s["pTa"], 1)
                with act.Fori(0, PAIRS) as i:
                    act.wait_ge(s["proj"], i * 3 + 2)
                    act.activation(qt, psum[:, 2048:2048 + N], ACT.Identity,
                                   bias=cols[:, bass.ds(i + COLS[bq][0], 1)]).then_inc(s["qk"], 1)
                    act.wait_ge(s["proj"], i * 3 + 3)
                    if bk:
                        act.activation(kt, psum[:, 3072:3072 + N], ACT.Identity,
                                       bias=cols[:, bass.ds(i + COLS[bk][0], 1)]).then_inc(s["qk"], 1)
                    else:
                        act.activation(kt, psum[:, 3072:3072 + N], ACT.Copy).then_inc(s["qk"], 1)
                    for t in range(12):
                        if t < 10:
                            act.wait_ge(s["max"], i * 10 + t + 1)
                            if t >= 2:
                                act.wait_ge(s["pT"], i * 11 + t)
                            else:
                                act.wait_ge(s["pT"], i * 11 + 1)
                            nmax = small[0:NP, 100 + t:101 + t]
                            if a:
                                act.activation(Pr[:, t % 2, :], Sp[:, t % 2, :], ACT.Exp, bias=nmax,
                                               scale=ASCALE).then_inc(s["exp"], 1)
                            else:
                                act.activation(Pr[:, t % 2, :], psum[0:NP, 1024 * (t % 2):1024 * (t % 2) + N], ACT.Exp,
                                               bias=nmax, scale=ASCALE,
                                               accum_out=small[0:NP, 120 + t:121 + t]).then_inc(s["exp"], 1)
                        if t >= 2:
                            u = t - 2
                            act.wait_ge(s["pT"], i * 11 + u + 2)
                            if u >= 2:
                                act.wait_ge(s["av"], i * 10 + u)
                            else:
                                act.wait_ge(s["av"], i * 10 + 1)
                            act.activation(PTs[:, u % 2, 0:4 * NP], bank(4, NP, 4 * NP), ACT.Copy).then_inc(s["pTa"], 1)
                    act.wait_ge(s["pT"], i * 11 + 12)
                    act.activation(dst[:, bass.ds(i, 1), 0:4 * NP], bank(4, P, 4 * NP).unsqueeze(1), ACT.Copy).then_inc(s["pTa"], 1)

            act.wait_ge(ld_const, 16 * 6)
            attention(0, "ffn_bq", "ffn_bk", T2)
            deviation(2)
            cols_out("tT", T3)
            act.wait_ge(gl_in, 1)
            act.activation(small[0:NP, 240:280], small[0:NP, 160:200], ACT.Exp).then_inc(gl_out, 1)
            act.wait_ge(slots_ready, 1)

            def tile_columns(n):
                act.wait_ge(M["xsT"], n + 1)
                act.activation(xsT.rearrange("p a b -> p (a b)"), bank(5, P, KC * TT), ACT.Copy).then_inc(M["xsTa"], 1)

            tile_columns(0)
            with act.Fori(0, EX) as e:
                k = act.value_load(tiles[0:1, 0, bass.ds(e, 1)], min_val=1, max_val=KT)
                b0 = act.value_load(tiles[0:1, 1, bass.ds(e, 1)], min_val=0, max_val=MAXT - 1)
                with act.Fori(0, k) as j:
                    g = b0 + j
                    act.wait_ge(M["y"], g + 1)
                    for b in range(2):
                        act.wait_ge(M["hT"], g * 2 + b + 1)
                        for j4 in range(4):
                            for q in range(2):
                                f = q * (FC // 2) + b * 4 + j4
                                done = act.activation(hT[:, f, :], bank(2 + b, P, TT, P * j4 + TT * q),
                                                      ACT.Gelu_apprx_tanh,
                                                      bias=cols[:, bass.ds(e * FC + (COLS["moe_b1"][0] + f), 1)])
                            done.then_inc(M["ha"], 1)
                    tile_columns(g + 1)
            deviation(3)
            cols_out("xnT1", T1)

            def batch_deviation(n):
                act.wait_ge(bn_var, n + 1)
                act.activation(small[:, 40:44], small[:, 30:34], ACT.Sqrt).then_inc(bn_sd, 1)

            for l in range(2):
                attention(1 + l, f"bq{l}", None, T3)
                batch_deviation(2 * l)
                for h, (o, w) in enumerate(HALF):
                    full(act, f"ffa{l}", h)
                    act.activation(hid[:, o:o + w], bank(unit_bank(f"ffa{l}", h), P, w), ACT.Relu,
                                   bias=col(f"b1{l}")).then_inc(freed_a, 1)
                batch_deviation(2 * l + 1)
            rows_out("gN", N2)
            deviation(4)
            for m in range(KC):
                for h, (o, w) in enumerate(HALF):
                    full(act, "nq", 2 * m + h)
                    act.activation(T3[:, m, o:o + w], bank(unit_bank("nq", 2 * m + h), P, w), ACT.Relu).then_inc(freed_a, 1)
            rows_out("nk", N1, ACT.Relu)
            rows_out("nv", N3)
            cols_out("noT", T2)
            deviation(5)
            cols_out("zT", T1)
            act.wait_ge(gl_in, 2)
            act.activation(small[0:NP, 240:280], small[0:NP, 160:200], ACT.Exp).then_inc(gl_out, 1)
            for w in range(2):
                for h, (o, n) in enumerate([(0, 4 * NP), (4 * NP, NP)]):
                    full(act, "pb", 2 * w + h)
                    act.activation(PB[:, w, o:o + n], bank(unit_bank("pb", 2 * w + h), P, n), ACT.Copy).then_inc(freed_a, 1)
            for n in range(16):
                f, h = divmod(n, 2)
                w = HALF[h][1]
                for q in range(2):
                    act.wait_ge(h_in, 2 * n + q + 1)
                    act.activation(hb[:, 2 + q, 0:w], hb[:, q, 0:w], ACT.Gelu, bias=col("l1_b1", f)).then_inc(h_g, 1)

        @block.vector
        def _(ve):
            done = [0]

            def link(ins_):
                done[0] += 1
                ins_.then_inc(dve, 1)
                ve.wait_ge(dve, done[0])

            def layer_norm(n, src, dst, gamma=None, beta=None):
                for c in range(NC):
                    ve.bn_stats(small[0:NP, 6 * c:6 * c + 6], src[:, c, :]) if c < NC - 1 else link(
                        ve.bn_stats(small[0:NP, 6 * c:6 * c + 6], src[:, c, :]))
                for c in range(NC):
                    i_ = ve.bn_aggr(small[0:NP, 50 + 2 * c:52 + 2 * c], small[0:NP, 6 * c:6 * c + 6])
                link(i_)
                mv = small[0:NP, 50:60].rearrange("p (c t) -> p c t", t=2)
                ve.tensor_scalar(small[0:NP, 30:35], mv[:, :, 1], EPS, None, ALU.add).then_inc(ln_var, 1)
                ve.wait_ge(ln_sd, n + 1)
                link(ve.reciprocal(small[0:NP, 60:65], small[0:NP, 40:45]))
                for c in range(NC):
                    i_ = ve.tensor_scalar(dst[:, c, :], src[:, c, :], mv[:, c, 0:1], small[0:NP, 60 + c:61 + c],
                                          ALU.subtract, ALU.mult)
                    if gamma is None:
                        i_.then_inc(ln_out, 1)
                    else:
                        link(i_)
                        link(ve.tensor_tensor(dst[:, c, :], dst[:, c, :], row(gamma), ALU.mult))
                        ve.tensor_tensor(dst[:, c, :], dst[:, c, :], row(beta), ALU.add).then_inc(ln_out, 1)

            ve.wait_ge(ld_edges, 48)
            link(ve.tensor_copy(srcf, srci))
            link(ve.tensor_copy(dstf, dsti))
            for c in range(NC):
                link(ve.tensor_scalar(dstr[:, c, :], dstf, float(-NP * c), None, ALU.add))
            link(ve.tensor_scalar(ind, dstr, 0.0, None, ALU.is_ge))
            ve.scalar_tensor_tensor(ind2, dstr, float(NP), ind, ALU.is_lt, ALU.mult).then_inc(chunk_ind, 1)
            link(ve.tensor_copy(wbf, wgt))
            link(ve.tensor_copy(wpart[:, 0], wbf))
            link(ve.tensor_tensor(wrest[:, 0], wgt, wpart[:, 0], ALU.subtract))
            link(ve.tensor_copy(wbf, wrest[:, 0]))
            link(ve.tensor_copy(wpart[:, 1], wbf))
            link(ve.tensor_tensor(wpart[:, 2], wrest[:, 0], wpart[:, 1], ALU.subtract))
            ve.wait_ge(ld_x, 16)
            layer_norm(0, xres, N1)
            ve.wait_ge(range_full, 2)
            ve.wait_ge(consts, 11)
            flat = g_cnt.rearrange("p c g -> p (c g)")
            for h in range(2):
                link(ve.tensor_reduce(flat[:, 200 * h:200 * h + 200],
                                      bank(h, 1, 400).rearrange("p (g t) -> p g t", t=2), AX, ALU.add))
            link(ve.tensor_scalar(g_cnt, g_cnt, 0.5, None, ALU.is_gt))
            for c in range(NC):
                ve.tensor_tensor(g_a[:, c, :], g_cnt[:, c, :], iota_g[:, 0, :], ALU.mult)
                link(ve.tensor_tensor(g_b[:, c, :], g_cnt[:, c, :], iota_g[:, 1, :], ALU.mult))
            ve.tensor_reduce(g_hi, g_a, AX, ALU.max)
            link(ve.tensor_reduce(g_lo, g_b, AX, ALU.max))
            link(ve.tensor_scalar(g_n, g_lo, -1.0, float(EG), ALU.mult, ALU.add))
            link(ve.tensor_scalar(g_lo, g_n, float(EG - 1), None, ALU.min))
            link(ve.tensor_tensor(g_n, g_hi, g_lo, ALU.subtract))
            link(ve.tensor_scalar(g_hi, g_n, 1.0, None, ALU.max))
            link(ve.tensor_copy(bounds[:, 0, 0:NC], g_lo))
            ve.tensor_copy(bounds[:, 1, 0:NC], g_hi).then_inc(range_ready, 1)
            ve.wait_ge(range_ready, 1)
            for c in range(NC):
                first = ve.value_load(bounds[0:1, 0, c:c + 1], min_val=0, max_val=EG - 1)
                k = ve.value_load(bounds[0:1, 1, c:c + 1], min_val=1, max_val=EG)
                with ve.Fori(0, k) as j:
                    g = nc.s_assert_within(first + j, 0, EG - 1,
                                           skip_runtime_bounds_check_because="a chunk's groups end below EG")
                    for s in range(2):
                        ve.wait_ge(hot_free[c], j * 2 + s + 1)
                        e = bass.ds(g * 2 + s, 1)
                        for v in range(3):
                            ve.tensor_scalar(one_dst[:, s, v, 0:NP], iota_dst[:, 0:NP], dstr[:, c, e],
                                             wpart[:, v, e], ALU.is_equal, ALU.mult)
                        ve.tensor_scalar(one_dst[:, s, 3, 0:NP], iota_dst[:, 0:NP], dstr[:, c, e], None, ALU.is_equal)
                        ve.tensor_scalar(one_src[:, s, 0:N], iota_src[:, 0:N], srcf[:, e], None,
                                         ALU.is_equal).then_inc(hot_ready[c], 1)
            for s in range(NC):
                full(ve, "WT", 2 * s + 1)
                ve.tensor_copy(WT[:, s, 4 * NP:N], bank(unit_bank("WT", 2 * s + 1), NP, NP)).then_inc(freed_v, 1)
            for c in range(NC):
                full(ve, "agg", c)
                i_ = ve.scalar_tensor_tensor(xres[:, c, :], bank(unit_bank("agg", c), NP, D), 0.0, xres[:, c, :],
                                             ALU.max, ALU.add)
                i_.then_inc(freed_v, 1)
            ve.wait_ge(ld_const, 16 * 6)
            for n in range(8):
                m, h = divmod(n, 2)
                o, w = HALF[h]
                full(ve, "mq", n)
                b = unit_bank("mq", n)
                ve.tensor_scalar(fm[:, 0, 0:w], bank(b, P, w), col("mix_bq", m), 0.0, ALU.add, ALU.min).then_inc(fm_min, 1)
                link(ve.tensor_scalar(fm[:, 2, 0:w], bank(b, P, w), col("mix_bq", m), 1.0, ALU.add, ALU.add))
                ve.wait_ge(fm_exp, n + 1)
                i_ = ve.tensor_tensor(T2[:, m, o:o + w], fm[:, 2, 0:w], fm[:, 1, 0:w], ALU.max)
                i_.then_inc(freed_v, 1)
                ve.wait_ge(freed_v, freed_count("v", FIRST["mq"] + n))
            for c in range(NC):
                full(ve, "mk", c)
                link(ve.tensor_tensor(fm[0:NP, 2, :], bank(unit_bank("mk", c), NP, D), row("mix_bk"), ALU.add))
                ve.tensor_scalar(fm[0:NP, 0, :], fm[0:NP, 2, :], 0.0, None, ALU.min).then_inc(fm_min, 1)
                ve.wait_ge(fm_exp, 8 + c + 1)
                ve.scalar_tensor_tensor(N1[:, c, :], fm[0:NP, 2, :], 1.0, fm[0:NP, 1, :], ALU.add,
                                        ALU.max).then_inc(freed_v, 1)
                ve.wait_ge(freed_v, freed_count("v", FIRST["mk"] + c))
            for c in range(NC):
                full(ve, "mv", c)
                ve.tensor_tensor(N3[:, c, :], bank(unit_bank("mv", c), NP, D), row("mix_bv"), ALU.add).then_inc(freed_v, 1)

            def diagonal_blocks(stage, hd, turn):
                ve.wait_ge(bd_zero, turn)
                for m in range(KC):
                    full(ve, stage, m)
                    b = unit_bank(stage, m)
                    for h in range(P // hd):
                        r = slice(h * hd, (h + 1) * hd)
                        ve.tensor_copy(bd[r, m, r], psum[r, 512 * b + h * hd:512 * b + (h + 1) * hd])
                        i_ = ve.tensor_copy(bd[r, m, P + h:P + h + 1], psum[r, 512 * b + P:512 * b + P + 1])
                    i_.then_inc(freed_v, 1)

            def divided(stage, hd, dst, eps=None):
                nh = P // hd
                for c in range(NC):
                    for h in range(2):
                        full(ve, stage, 2 * c + h)
                        v = bank(unit_bank(stage, 2 * c + h), NP, 2 * (P + nh)).rearrange("p (m w) -> p m w", m=2)
                        z = mz[:, :, 0:nh]
                        if eps is None:
                            link(ve.reciprocal(z, v[:, :, P:P + nh]))
                        else:
                            link(ve.tensor_scalar(z, v[:, :, P:P + nh], eps, None, ALU.add))
                            link(ve.reciprocal(z, z))
                        for m in range(2):
                            o = (2 * h + m) * P
                            i_ = ve.tensor_tensor(
                                dst[:, c, o:o + P].rearrange("p (h d) -> p h d", d=hd),
                                v[:, m, 0:P].rearrange("p (h d) -> p h d", d=hd),
                                z[:, m, :].unsqueeze(2).to_broadcast([NP, nh, hd]), ALU.mult)
                            if m == 0:
                                link(i_)
                        i_.then_inc(freed_v, 1)
                        ve.wait_ge(freed_v, freed_count("v", FIRST[stage] + 2 * c + h))

            def add_rows(stage, base, dst, bias):
                for c in range(NC):
                    full(ve, stage, c)
                    link(ve.tensor_tensor(dst[:, c, :], bank(unit_bank(stage, c), NP, D), base[:, c, :], ALU.add))
                    ve.tensor_tensor(dst[:, c, :], dst[:, c, :], row(bias), ALU.add).then_inc(freed_v, 1)
                ve.wait_ge(freed_v, freed_count("v", FIRST[stage] + NC - 1))

            diagonal_blocks("mkv", 64, 1)
            divided("mo", 64, N2)
            add_rows("mp", xres, xres, "mix_bp")
            layer_norm(1, xres, N1)
            nmax = lambda u: small[0:NP, 100 + u:101 + u]
            total = lambda u: small[0:NP, 120 + u:121 + u]
            inv = lambda u: small[0:NP, 140 + u:141 + u]

            def attention(a, bv, dst):
                s = A[a]
                for first in ("pTv", "ctx"):
                    ve.nop().then_inc(s[first], 1)
                K = 20 if a == 0 else 30
                with ve.Fori(0, PAIRS) as i:
                    n = [0]

                    def lk(ins_):
                        n[0] += 1
                        ins_.then_inc(s["chain"], 1)
                        ve.wait_ge(s["chain"], i * K + n[0])

                    ve.wait_ge(s["proj"], i * 3 + 4)
                    for c, w in ((0, 4), (4, 1)):
                        src_ = bank(c // 4, NP, P * w).rearrange("p (c d) -> p c d", d=P)
                        if bv:
                            b_ = rows[:, ROWS[bv], bass.ds(i * P, P)].unsqueeze(1).to_broadcast([NP, w, P])
                            i_ = ve.tensor_tensor(vv[:, c:c + w, :], src_, b_, ALU.add)
                        else:
                            i_ = ve.tensor_copy(vv[:, c:c + w, :], src_)
                    i_.then_inc(s["v"], 1)
                    for t in range(13):
                        if t < 10:
                            hh, c = divmod(t, NC)
                            ve.wait_ge(s["score"], i * 10 + t + 1)
                            sc = psum[0:NP, 1024 * (t % 2):1024 * (t % 2) + N]
                            if a:
                                if t >= 2:
                                    ve.wait_ge(s["exp"], i * 10 + t - 1)
                                ve.memset(small[0:1, 90:91], 0.0)
                                lk(ve.tensor_tensor_reduce(Sp[:, t % 2, :], sc, maskb[:, c, :], 1.0, -3.0e38, ALU.add,
                                                           ALU.max, small[0:NP, 80 + t:81 + t]))
                            else:
                                lk(ve.tensor_reduce(small[0:NP, 80 + t:81 + t], sc, AX, ALU.max))
                            ve.tensor_scalar(nmax(t), small[0:NP, 80 + t:81 + t], -ASCALE, None,
                                             ALU.mult).then_inc(s["max"], 1)
                        if 1 <= t < 11:
                            u = t - 1
                            c = u % NC
                            ve.wait_ge(s["exp"], i * 10 + u + 1)
                            if a:
                                ve.tensor_tensor_reduce(Pr[:, u % 2, :], Pr[:, u % 2, :], cnt_adj[:, c, :], 1.0, 0.0,
                                                        ALU.mult, ALU.add, total(u)).then_inc(s["prob"], 1)
                                ve.wait_ge(s["prob"], i * 10 + u + 1)
                                lk(ve.tensor_scalar(total(u), total(u), 1e-16, None, ALU.add))
                            lk(ve.reciprocal(inv(u), total(u)))
                        if 2 <= t < 12:
                            u = t - 2
                            ve.wait_ge(s["pT"], i * 11 + u + 2)
                            if u >= 2:
                                ve.wait_ge(s["av"], i * 10 + u)
                            else:
                                ve.wait_ge(s["av"], i * 10 + 1)
                            ve.tensor_copy(PTs[:, u % 2, 4 * NP:N], bank(5, NP, NP)).then_inc(s["pTv"], 1)
                        if t >= 3:
                            u = t - 3
                            hh, c = divmod(u, NC)
                            ve.wait_ge(s["av"], i * 10 + u + 2)
                            ve.tensor_scalar(actx[:, c, hh * HD:(hh + 1) * HD], bank(6 + u % 2, NP, HD), inv(u),
                                             None, ALU.mult).then_inc(s["ctx"], 1)
                    ve.wait_ge(s["pT"], i * 11 + 12)
                    ve.tensor_copy(dst[:, bass.ds(i, 1), 4 * NP:N], bank(5, P, NP).unsqueeze(1)).then_inc(s["pTv"], 1)
                    assert n[0] == K

            attention(0, "ffn_bv", T2)
            add_rows("ao", N1, N2, "ffn_bo")
            layer_norm(2, N2, N3, "ln1_g", "ln1_b")

            lg = small[0:NP, 160:200].rearrange("p (c e) -> p c e", e=EX)
            ex = small[0:NP, 240:280].rearrange("p (c e) -> p c e", e=EX)
            one = small[0:NP, 200:240].rearrange("p (c e) -> p c e", e=EX)
            tmp = small[0:NP, 280:320].rearrange("p (c e) -> p c e", e=EX)
            mx = small[0:NP, 320:325]
            sm = small[0:NP, 325:330]
            gw = small[0:NP, 330:335]
            v5 = small[0:NP, 335:340]
            bc = lambda x: x.unsqueeze(2).to_broadcast([NP, NC, EX])

            def exp_gates(stage, n, bias):
                full(ve, stage, 0)
                v = bank(unit_bank(stage, 0), NP, NC * EX).rearrange("p (c e) -> p c e", e=EX)
                if bias:
                    i_ = ve.tensor_tensor(lg, v, gate_b[:].unsqueeze(1).to_broadcast([NP, NC, EX]), ALU.add)
                else:
                    i_ = ve.tensor_copy(lg, v)
                i_.then_inc(freed_v, 1)
                ve.wait_ge(freed_v, freed_count("v", FIRST[stage]))
                link(ve.tensor_reduce(mx, lg, AX, ALU.max))
                ve.tensor_tensor(lg, lg, bc(mx), ALU.subtract).then_inc(gl_in, 1)
                ve.wait_ge(gl_out, n)
                link(ve.tensor_reduce(sm, ex, AX, ALU.add))

            exp_gates("gate0", 1, True)
            link(ve.reciprocal(gw, sm))
            e8 = small[0:NP, 340:348]
            for e in range(EX):
                i_ = ve.memset(e8[:, e:e + 1], float(EX - e))
            link(i_)
            link(ve.tensor_reduce(v5, ex, AX, ALU.max))
            link(ve.tensor_tensor(tmp, ex, bc(v5), ALU.is_equal))
            link(ve.tensor_tensor(tmp, tmp, e8.unsqueeze(1).to_broadcast([NP, NC, EX]), ALU.mult))
            link(ve.tensor_reduce(v5, tmp, AX, ALU.max))
            ve.tensor_tensor(one, e8.unsqueeze(1).to_broadcast([NP, NC, EX]), bc(v5), ALU.is_equal).then_inc(gates_ready, 1)
            full(ve, "rank", 0)
            b = unit_bank("rank", 0)
            nt = small[0:NP, 350:358]
            ft = small[0:NP, 360:368]
            cnt_e = small[0:NP, 370:378]
            big = small[0:NP, 378:386]
            link(ve.tensor_copy(cnt_e, bank(b, NP, EX, EX * NC)))
            link(ve.memset(nt, 1.0))
            for k in range(1, KT):
                link(ve.tensor_scalar(big, cnt_e, k * TT + 0.5, None, ALU.is_gt))
                link(ve.tensor_tensor(nt, nt, big, ALU.add))
            link(ve.memset(ft[:, 0:1], 0.0))
            for e in range(1, EX):
                link(ve.tensor_tensor(ft[:, e:e + 1], ft[:, e - 1:e], nt[:, e - 1:e], ALU.add))
            link(ve.tensor_scalar(big, ft, float(TT), None, ALU.mult))
            ve.tensor_tensor(tmp, bank(b, NP, NC * EX).rearrange("p (c e) -> p c e", e=EX),
                             big.unsqueeze(1).to_broadcast([NP, NC, EX]), ALU.add).then_inc(freed_v, 1)
            ve.wait_ge(freed_v, freed_count("v", FIRST["rank"]))
            link(ve.tensor_tensor(tmp, tmp, one, ALU.mult))
            link(ve.tensor_reduce(v5, tmp, AX, ALU.add))
            link(ve.tensor_copy(idx[:], v5))
            link(ve.tensor_tensor(big[:, 0:1], ft[:, EX - 1:EX], nt[:, EX - 1:EX], ALU.add))
            link(ve.tensor_copy(tiles[:, 2, 0:1], big[0:1, 0:1]))
            link(ve.tensor_copy(tiles[:, 0, :], nt[0:1, :]))
            ve.tensor_copy(tiles[:, 1, :], ft[0:1, :]).then_inc(slots_ready, 1)
            ve.wait_ge(slots_ready, 1)
            ve.nop().then_inc(M["yv"], 1)
            with ve.Fori(0, EX // 2) as i:
                for par in range(2):
                    k = ve.value_load(tiles[0:1, 0, bass.ds(i * 2 + par, 1)], min_val=1, max_val=KT)
                    b0 = ve.value_load(tiles[0:1, 1, bass.ds(i * 2 + par, 1)], min_val=0, max_val=MAXT - 1)
                    with ve.Fori(0, k) as j:
                        g = b0 + j
                        for b in range(2):
                            ve.wait_ge(M["h"], g * 2 + b + 1)
                            ve.tensor_copy(hs[:, b * D:(b + 1) * D], bank(b, P, D)).then_inc(M["hs"], 1)
                        ve.wait_ge(M["y"], g + 2)
                        ve.wait_ge(M["st"], g * 32 + 16)
                        ve.wait_ge(M[f"second{par}"], i * 48 + 48)
                        ve.tensor_tensor(ys, bank(4, P, D // 2), eb2[par], ALU.add).then_inc(M["yv"], 1)
            ve.wait_ge(gathered, 16 * NC)
            for c in range(NC):
                i_ = ve.scalar_tensor_tensor(xres[:, c, :], yg[:, c, :], gw[:, c:c + 1], xres[:, c, :], ALU.mult, ALU.add)
            link(i_)
            layer_norm(3, xres, N2)
            ve.tensor_scalar(maskb, cnt_adj[:], 0.5, NEG, ALU.is_lt, ALU.mult).then_inc(mask_ready, 1)
            ve.wait_ge(mask_ready, 1)

            def batch_norm(n, g, beta):
                for m in range(KC):
                    for h, (o, w) in enumerate(HALF):
                        i_ = ve.bn_stats(small[:, 400 + 12 * m + 6 * h:406 + 12 * m + 6 * h], T2[:, m, o:o + w])
                link(i_)
                for m in range(KC):
                    i_ = ve.bn_aggr(small[:, 460 + 2 * m:462 + 2 * m], small[:, 400 + 12 * m:412 + 12 * m])
                link(i_)
                mv = small[:, 460:468].rearrange("p (m t) -> p m t", t=2)
                ve.tensor_scalar(small[:, 30:34], mv[:, :, 1], EPS, None, ALU.add).then_inc(bn_var, 1)
                ve.wait_ge(bn_sd, n + 1)
                link(ve.reciprocal(small[:, 470:474], small[:, 40:44]))
                link(ve.tensor_tensor(small[:, 474:478], small[:, 470:474], cols[:, COLS[g][0]:COLS[g][0] + 4], ALU.mult))
                link(ve.tensor_tensor(small[:, 478:482], small[:, 474:478], mv[:, :, 0], ALU.mult))
                link(ve.tensor_tensor(small[:, 482:486], cols[:, COLS[beta][0]:COLS[beta][0] + 4], small[:, 478:482],
                                      ALU.subtract))
                for m in range(KC):
                    i_ = ve.tensor_scalar(T2[:, m, :], T2[:, m, :], small[:, 474 + m:475 + m], small[:, 482 + m:483 + m],
                                          ALU.mult, ALU.add)
                    i_.then_inc(bn_out, 1)
                ve.wait_ge(bn_out, 4 * (n + 1))

            def add_cols(stage, base, bias):
                for n in range(8):
                    m, h = divmod(n, 2)
                    o, w = HALF[h]
                    full(ve, stage, n)
                    ve.scalar_tensor_tensor(T2[:, m, o:o + w], bank(unit_bank(stage, n), P, w), col(bias, m),
                                            base[:, m, o:o + w], ALU.add, ALU.add).then_inc(freed_v, 1)
                ve.wait_ge(freed_v, freed_count("v", FIRST[stage] + 7))

            for l in range(2):
                attention(1 + l, None, T3)
                add_cols(f"wo{l}", T1 if l == 0 else T2, f"bo{l}")
                batch_norm(2 * l, f"g1{l}", f"beta1{l}")
                add_cols(f"ffb{l}", T2, f"b2{l}")
                batch_norm(2 * l + 1, f"g2{l}", f"beta2{l}")
            stage_out(ve, "gN")
            layer_norm(4, N2, N2, "ln_g", "ln_b")
            ve.wait_ge(ln_out, 5 * NC)
            for c in range(NC):
                i_ = ve.tensor_tensor(xres[:, c, :], xres[:, c, :], N2[:, c, :], ALU.add)
            link(i_)
            diagonal_blocks("nkv", 32, 2)
            divided("no", 32, N2, 1e-15)
            add_rows("np", xres, xres, "proj_b")
            layer_norm(5, xres, N1)
            exp_gates("gate1", 2, False)
            for c in range(NC):
                i_ = ve.max(small[0:NP, 500 + 8 * c:508 + 8 * c], ex[:, c, :])
            link(i_)
            top = small[0:NP, 500:540].rearrange("p (c e) -> p c e", e=EX)
            pr = small[0:NP, 540:550].rearrange("p (c e) -> p c e", e=2)
            link(ve.reciprocal(gw, sm))
            link(ve.tensor_tensor(pr, top[:, :, 0:2], gw.unsqueeze(2).to_broadcast([NP, NC, 2]), ALU.mult))
            link(ve.tensor_reduce(mx, pr, AX, ALU.add))
            link(ve.reciprocal(sm, mx))
            link(ve.tensor_tensor(pr, pr, sm.unsqueeze(2).to_broadcast([NP, NC, 2]), ALU.mult))
            for w in range(2):
                ve.tensor_copy(pbl[:, w, :, :], pr[:, :, w].unsqueeze(2).to_broadcast([NP, NC, P])).then_inc(pb_l, 1)
            stage_out(ve, "pb")
            for n in range(16):
                f, h = divmod(n, 2)
                o, w = HALF[h]
                full(ve, "h1", n)
                b = unit_bank("h1", n)
                for q in range(2):
                    ve.tensor_tensor(hb[:, q, 0:w], bank(b, P, w), PB[:, q, o:o + w], ALU.mult).then_inc(h_in, 1)
                ve.wait_ge(h_g, 2 * n + 2)
                ve.tensor_tensor(h1T[:, f, o:o + w], hb[:, 2, 0:w], hb[:, 3, 0:w], ALU.add).then_inc(freed_v, 1)
                ve.wait_ge(freed_v, freed_count("v", FIRST["h1"] + n))
            for c in range(NC):
                full(ve, "o1", c)
                ve.tensor_tensor(xres[:, c, :], bank(unit_bank("o1", c), NP, D), xres[:, c, :], ALU.add).then_inc(x_done, 1)


def kernel(**inputs):
    import numpy as np
    import concourse.bacc as bacc
    from concourse.bass_utils import run_bass_kernel_spmd

    a = {k: np.asarray(v) for k, v in inputs.items()}

    def as_rows(x):
        return x.reshape(NC, NP, D).transpose(1, 0, 2)

    def edges(x):
        return x.reshape(ET, NP).T

    def weight(w):
        return w.reshape(w.shape[0] // P, P, w.shape[1]).transpose(1, 0, 2)

    def pair_weights(q, k, v):
        w = np.stack([q, k, v]).reshape(3, KC, P, PAIRS, P)
        return w.transpose(3, 2, 0, 1, 4)

    vectors = {"mix_bq": a["L0_mix_bq"], "ffn_bq": a["L0_ffn_bq"], "ffn_bk": a["L0_ffn_bk"],
               "moe_b1": a["L0_ffn_b1"], "l1_b1": a["L1_ffn_b1"]}
    for l in range(2):
        for v in ("bq", "bo", "b1", "b2", "g1", "beta1", "g2", "beta2"):
            vectors[f"{v}{l}"] = a[f"L1_gnn_{v}"][l]
    qkv = a["L1_mix_qkv_weight"]
    arrays = {
        "src": edges(a["src"]), "dst": edges(a["dst"]), "edge_w": edges(a["edge_weight"]), "x": as_rows(a["x"]),
        "cols": np.concatenate([vectors[n].reshape(w, P) for n, (_, w) in COLS.items()]).T,
        "rows": np.stack([a[n] for n in (
            "L0_mix_bk", "L0_mix_bv", "L0_mix_bp", "L0_ffn_bv", "L0_ffn_bo", "L0_ffn_ln1_g", "L0_ffn_ln1_b",
            "L1_gnn_ln_g", "L1_gnn_ln_b", "L1_mix_proj_bias")]),
        "gate_b": a["L0_ffn_gate_b"], "moe_b2": a["L0_ffn_b2"], "l1_b2": a["L1_ffn_b2"],
        "gateW": weight(a["L0_ffn_gate_W"]), "gateW1": weight(a["L1_ffn_Wg"]),
        "gnnW": weight(a["L0_gnn_weight"]), "mixWq": weight(a["L0_mix_Wq"]), "mixWk": weight(a["L0_mix_Wk"]),
        "mixWv": weight(a["L0_mix_Wv"]), "mixWp": weight(a["L0_mix_Wp"]), "ffnWo": weight(a["L0_ffn_Wo"]),
        "att0": pair_weights(a["L0_ffn_Wq"], a["L0_ffn_Wk"], a["L0_ffn_Wv"]),
        "moeW1": a["L0_ffn_W1"].reshape(EX, KC, P, FF).transpose(0, 2, 1, 3),
        "moeW2": a["L0_ffn_W2"].reshape(EX, FC, P, D).transpose(0, 2, 1, 3),
        "m1q": weight(qkv[0:D].T), "m1k": weight(qkv[D:2 * D].T), "m1v": weight(qkv[2 * D:].T),
        "m1p": weight(a["L1_mix_proj_weight"].T),
        "l1W1": weight(a["L1_ffn_W1"].transpose(1, 0, 2).reshape(D, EX * F1)),
        "l1W2": a["L1_ffn_W2"].transpose(1, 0, 2),
    }
    for l in range(2):
        arrays[f"att{l + 1}"] = pair_weights(*(a[f"L1_gnn_{w}"][l].T for w in ("Wq", "Wk", "Wv")))
        arrays[f"gnnWo{l}"] = weight(a["L1_gnn_Wo"][l].T)
        arrays[f"ffW1_{l}"] = weight(a["L1_gnn_W1"][l].T)
        arrays[f"ffW2_{l}"] = a["L1_gnn_W2"][l].T
    arrays = {f"in_{k}": np.ascontiguousarray(v) for k, v in arrays.items()}

    nc = bacc.Bacc("TRN2", target_bir_lowering=False, num_devices=1)
    ins = {k[3:]: nc.dram_tensor(k, v.shape, mybir.dt.from_np(v.dtype), kind="ExternalInput").ap()
           for k, v in arrays.items()}
    out = nc.dram_tensor("out_rows", [NP, NC, D], F32, kind="ExternalOutput").ap()
    build(nc, ins, out)
    r = run_bass_kernel_spmd(nc, [arrays], core_ids=[0])
    return r.results[0]["out_rows"].transpose(1, 0, 2).reshape(N, D)
```

```python
from contextlib import ExitStack

import concourse.bass as bass
from concourse import mybir

F32 = mybir.dt.float32
BF16 = mybir.dt.bfloat16
FP16 = mybir.dt.float16
I32 = mybir.dt.int32
U32 = mybir.dt.uint32
ALU = mybir.AluOpType
ACT = mybir.ActivationFunctionType
AX = mybir.AxisListType.X

N = 625
D = 512
P = 128
KC = D // P
NC = 5
NP = N // NC
EDGES = 20000
ET = EDGES // NP
EG = ET // 2
EX = 8
FF = 2048
FC = FF // P
TT = 64
MAXT = (N + EX * (TT - 1)) // TT
KT = -(-N // TT)
F1 = 128
HD = 64
PAIRS = D // (2 * HD)
ASCALE = HD ** -0.5
HALF = [(0, 313), (313, 312)]
WIDE = [(0, 512), (512, 113)]
NO_EDGE = 1.0e30
EPS = 1e-5

COLS = {}
_n = 0
for _name, _w in [("mix_bq", 4), ("ffn_bq", 4), ("ffn_bk", 4)] + [
        (f"{v}{l}", w) for l in range(2) for v, w in
        [("bq", 4), ("bo", 4), ("b1", 1), ("b2", 4), ("g1", 4), ("beta1", 4), ("g2", 4), ("beta2", 4)]] + [
        ("moe_b1", EX * FC), ("l1_b1", EX)]:
    COLS[_name] = (_n, _w)
    _n += _w
NCOL = _n
ROWS = {n: i for i, n in enumerate(
    ["mix_bk", "mix_bv", "mix_bp", "ffn_bv", "ffn_bo", "ln1_g", "ln1_b", "ln_g", "ln_b", "proj_b"])}
RING = [("gnnW", "hp"), ("mixWq", "mq"), ("mixWk", "mk"), ("mixWv", "mv"), ("mixWp", "mp"), ("ffnWo", "ao"),
        ("gnnWo0", "wo0"), ("gnnWo1", "wo1"), ("m1q", "nq"), ("m1k", "nk"), ("m1v", "nv"), ("m1p", "np")]

STAGES = [
    ("xnT0", 5, "a"), ("hp", 5, "a"), ("WT", 10, "av"), ("agg", 5, "v"),
    ("mq", 8, "v"), ("mk", 5, "v"), ("mv", 5, "v"), ("mkv", 4, "v"), ("mo", 10, "v"), ("moT", 5, "a"),
    ("mp", 5, "v"), ("yT", 5, "a"), ("ao", 5, "v"), ("tT", 5, "a"), ("gate0", 1, "v"), ("rank", 1, "v"),
    ("xnT1", 5, "a"),
    ("wo0", 8, "v"), ("ffa0", 2, "a"), ("ffb0", 8, "v"),
    ("wo1", 8, "v"), ("ffa1", 2, "a"), ("ffb1", 8, "v"), ("gN", 5, "a"),
    ("nq", 8, "a"), ("nk", 5, "a"), ("nv", 5, "a"), ("nkv", 4, "v"), ("no", 10, "v"), ("noT", 5, "a"),
    ("np", 5, "v"), ("zT", 5, "a"), ("gate1", 1, "v"), ("pb", 4, "a"), ("h1", 16, "v"), ("o1", 5, "v"),
]
UNIT = []
FIRST = {}
COUNT = {s: k for s, k, _ in STAGES}
for _s, _k, _e in STAGES:
    FIRST[_s] = len(UNIT)
    UNIT += [_e[i % len(_e)] for i in range(_k)]


def freed_count(engine, unit):
    return sum(e == engine for e in UNIT[:unit + 1])


def build(nc, ins, out):
    ctx = ExitStack()
    with ctx:
        def sem(name):
            return ctx.enter_context(nc.semaphore(name))

        def sb(name, shape, dt=F32):
            return ctx.enter_context(nc.sbuf_tensor(name, shape, dt))

        xres = sb("xres", [NP, NC, D])
        cnt_adj = sb("cnt_adj", [NP, NC, N])
        ident = sb("ident", [P, P])
        cols = sb("cols", [P, NCOL])
        rows = sb("rows", [NP, len(ROWS), D])
        gate_b = sb("gate_b", [NP, EX])
        onesf = sb("onesf", [P, P])
        upper = sb("upper", [NP, NP])
        twos = sb("twos", [EX, NP])
        b2rows = sb("b2rows", [EX, D])
        gateW = sb("gateW", [P, KC, EX])
        gateW1 = sb("gateW1", [P, KC, EX])
        ffW1 = sb("ffW1", [P, KC, F1])
        ffW2 = sb("ffW2", [P, D])
        small = sb("small", [P, 640])
        idx = sb("idx", [NP, NC], U32)
        bounds = sb("bounds", [1, 2, EX], I32)
        tiles = sb("tiles", [1, 3, EX], I32)
        AR = 8192 + 30901
        arena = sb("arena", [P, AR])

        def at(off, p, *dims):
            n = 1
            for d in dims:
                n *= d
            v = arena[0:p, off:off + n]
            if len(dims) == 2:
                return v.rearrange("p (a b) -> p a b", b=dims[1])
            if len(dims) == 3:
                return v.rearrange("p (a b c) -> p a b c", b=dims[1], c=dims[2])
            return v

        o_ring = 8192
        o_T = o_ring + 2 * KC * D
        o_N = o_T + 3 * KC * N
        o_A = o_N + 3 * NC * D
        o_M = o_A + 8500
        ring = [at(o_ring + i * KC * D, P, KC, D) for i in range(2)]
        T1, T2, T3 = [at(o_T + i * KC * N, P, KC, N) for i in range(3)]
        N1, N2, N3 = [at(o_N + i * NC * D, NP, NC, D) for i in range(3)]
        maskb = at(o_M, NP, NC, N)
        assert o_M + NC * N <= AR
        Wrows = maskb
        WT = at(o_T + KC * N, NP, NC, N)
        oa = [o_A]

        def take(p, *dims, dt=F32):
            n = 1
            for d in dims:
                n *= d
            w = n if dt in (F32, I32) else (n + 1) // 2
            v = arena[0:p, oa[0]:oa[0] + w]
            oa[0] += w
            assert oa[0] <= o_M
            if dt != F32:
                v = v.bitcast(dt)[:, 0:n]
            if len(dims) == 2:
                return v.rearrange("p (a b) -> p a b", b=dims[1])
            if len(dims) == 3:
                return v.rearrange("p (a b c) -> p a b c", b=dims[1], c=dims[2])
            return v

        srci, dsti = take(NP, ET, dt=I32), take(NP, ET, dt=I32)
        wgt = take(NP, ET)
        srcf, dstf, dstr = take(NP, ET), take(NP, ET), take(NP, NC, ET)
        wpart, wrest = take(NP, 3, ET), take(NP, 2, ET)
        wbf = take(NP, ET, dt=BF16)
        ind, ind2 = take(NP, NC, ET), take(NP, NC, ET)
        iota_src, iota_dst = take(NP, N + 1, dt=FP16), take(NP, NP + 1, dt=BF16)
        one_dst, one_src = take(NP, 2, 4, P, dt=BF16), take(NP, 2, N + 1, dt=BF16)
        zero_bf = take(NP, P, dt=BF16)
        zero_rows_sb = take(TT, D)
        iota_g = at(o_A + 6500, 1, 2, EG)
        g_cnt, g_a, g_b = [at(o_A + 6700 + 400 * i, 1, NC, EG) for i in range(3)]
        g_lo, g_hi, g_n = [at(o_A + 7900 + 8 * i, 1, NC) for i in range(3)]
        assert oa[0] <= o_A + 6500
        oa[0] = o_A
        aw = take(P, 3, KC, P)
        qt, kt = take(P, N), take(P, N)
        vv = take(NP, NC, P)
        Pr = take(NP, 2, N)
        diag = take(NP, 2, NP)
        PT = take(NP, 2 * NC, 2 * NP)
        oa[0] = o_A
        fm = take(P, 4, D)
        bd = take(P, KC, 132)
        mz = take(NP, 2, 8)
        hid = at(o_A, P, N)
        EW1 = [at(0, P, KC, FF), at(o_ring + 8192, P, KC, FF)]
        EW2 = [at(o_ring, P, FC, D), at(o_ring + 16384, P, FC, D)]
        o_E = o_ring + 3 * 8192
        xs = at(o_E, TT, D)
        xsT = at(o_E + 1024, P, KC, TT)
        hT = at(o_E + 1280, P, FC, TT)
        hs = at(o_E + 2304, P, FF // 2)
        ys = at(o_E + 3328, P, D // 2)
        eb2 = [at(o_E + 3584 + i * D // 2, P, D // 2) for i in range(2)]
        assert o_E + 3584 + D <= AR
        yg = at(o_N, NP, NC, D)
        l1W1 = at(0, P, KC, EX * F1)
        l1W2 = at(4096, P, EX, D)
        oa[0] = o_A
        pbl = take(NP, 2, NC, P)
        PB = take(P, 2, N)
        hb = take(P, 4, 320)
        h1T = at(o_T + KC * N, P, EX, N)

        psum = ctx.enter_context(nc.psum_tensor("psum", [P, 8 * 512], F32))

        def bank(b, p, w, off=0):
            return psum[0:p, 512 * b + off:512 * b + off + w]

        xs_dram = nc.dram_tensor("token_rows", [(MAXT + 2) * TT, D], F32, kind="Internal").ap()
        ys_dram = nc.dram_tensor("expert_rows", [MAXT * TT, D], F32, kind="Internal").ap()

        unit_full, freed_a, freed_v = sem("unit_full"), sem("freed_a"), sem("freed_v")
        ld_edges, ld_x, ld_const = sem("ld_edges"), sem("ld_x"), sem("ld_const")
        ld_ring = [sem(f"ld_ring{i}") for i in range(2)]
        ld_ff = sem("ld_ff")
        consts = sem("consts")
        dve, actc = sem("dve"), sem("actc")
        ln_var, ln_sd, ln_out = sem("ln_var"), sem("ln_sd"), sem("ln_out")
        bn_var, bn_sd, bn_out = sem("bn_var"), sem("bn_sd"), sem("bn_out")
        range_full, range_ready, chunk_ind = sem("range_full"), sem("range_ready"), sem("chunk_ind")
        hot_ready = [sem(f"hot_ready{c}") for c in range(NC)]
        hot_free = [sem(f"hot_free{c}") for c in range(NC)]
        adj_full, adj_out = sem("adj_full"), sem("adj_out")
        fm_min, fm_exp = sem("fm_min"), sem("fm_exp")
        bd_zero = sem("bd_zero")
        mask_ready, nbq_ready = sem("mask_ready"), sem("nbq_ready")
        A = []
        for a in range(3):
            A.append({n: sem(f"att{a}_{n}") for n in (
                "wqk", "wv", "q", "k", "v", "qc", "kc", "vc", "score", "max", "exp", "sum", "prob", "pT", "pTc",
                "av", "ctx")})
        gates_ready, slots_ready, scattered, gathered, zero_rows = (
            sem("gates_ready"), sem("slots_ready"), sem("scattered"), sem("gathered"), sem("zero_rows"))
        M = {n: sem(f"moe_{n}") for n in (
            "first0", "first1", "second0", "second1", "xs", "xsT", "xsTa", "h", "hs", "hT", "ha", "y", "yv",
            "st", "done")}
        p_top, pb_l = sem("p_top"), sem("pb_l")
        gl_in, gl_out = sem("gl_in"), sem("gl_out")
        h_in, h_g = sem("h_in"), sem("h_g")
        l1w, b2w = sem("l1w"), sem("b2w")
        x_done, stored = sem("x_done"), sem("stored")

        def full(eng, stage, i):
            eng.wait_ge(unit_full, FIRST[stage] + i % COUNT[stage] + 1)

        def stage_out(eng, stage, upto=None):
            last = FIRST[stage] + (COUNT[stage] if upto is None else upto) - 1
            for e, s in (("a", freed_a), ("v", freed_v)):
                if e in UNIT[FIRST[stage]:last + 1]:
                    eng.wait_ge(s, freed_count(e, last))

        def unit_bank(stage, i):
            return (FIRST[stage] + i) % 8

        def out_sem(stage, i):
            return freed_a if UNIT[FIRST[stage] + i] == "a" else freed_v

        nbq = small[:, 600:600 + 3 * KC]
        block = ctx.enter_context(nc.Block())
        col = lambda name, i=0: cols[:, COLS[name][0] + i:COLS[name][0] + i + 1]
        row = lambda name: rows[:, ROWS[name], :]

        @block.sync
        def _(sp):
            sp.dma_start(srci, ins["src"]).then_inc(ld_edges, 16)
            sp.dma_start(dsti, ins["dst"]).then_inc(ld_edges, 16)
            sp.dma_start(wgt, ins["edge_w"]).then_inc(ld_edges, 16)
            sp.dma_start(xres[:], ins["x"]).then_inc(ld_x, 16)
            sp.dma_start(ring[0], ins["gnnW"]).then_inc(ld_ring[0], 16)
            sp.dma_start(ring[1], ins["mixWq"]).then_inc(ld_ring[1], 16)
            sp.dma_start(cols[:], ins["cols"]).then_inc(ld_const, 16)
            sp.dma_start(rows[:], ins["rows"].partition_broadcast(NP)).then_inc(ld_const, 16)
            sp.dma_start(gate_b[:], ins["gate_b"].partition_broadcast(NP)).then_inc(ld_const, 16)
            sp.dma_start(b2rows[:], ins["l1_b2"]).then_inc(ld_const, 16)
            sp.dma_start(gateW[:], ins["gateW"]).then_inc(ld_const, 16)
            sp.dma_start(gateW1[:], ins["gateW1"]).then_inc(ld_const, 16)
            sp.dma_start(EW1[0], ins["moeW1"][0]).then_inc(M["first0"], 16)

            def ring_load(n):
                full(sp, RING[n - 2][1], -1)
                sp.dma_start(ring[n % 2], ins[RING[n][0]]).then_inc(ld_ring[n % 2], 16)

            def attention_loads(a, name):
                s = A[a]

                def load(i):
                    sp.dma_start(aw[:, 0:2], ins[name][i][:, 0:2]).then_inc(s["wqk"], 16)
                    sp.dma_start(aw[:, 2:3], ins[name][i][:, 2:3]).then_inc(s["wv"], 16)

                load(0)
                with sp.Fori(0, PAIRS - 1) as i:
                    sp.wait_ge(s["k"], i + 1)
                    sp.wait_ge(s["v"], i + 1)
                    load(i + 1)

            for n in range(2, 6):
                ring_load(n)
            stage_out(sp, "yT")
            sp.wait_ge(zero_rows, 16 * (2 * MAXT + 1))
            sp.wait_ge(M["st"], 16)
            attention_loads(0, "att0")

            def first_weights(buf, expert):
                sp.dma_start(EW1[buf], ins["moeW1"][expert]).then_inc(M[f"first{buf}"], 16)

            def second_weights(buf, expert):
                sp.dma_start(EW2[buf], ins["moeW2"][expert]).then_inc(M[f"second{buf}"], 16)
                for q in range(2):
                    sp.dma_start(eb2[buf][q * TT:(q + 1) * TT, :],
                                 ins["moe_b2"][expert, q * (D // 2):(q + 1) * (D // 2)].partition_broadcast(TT)
                                 ).then_inc(M[f"second{buf}"], 16)

            full(sp, "ao", -1)
            second_weights(0, 0)
            full(sp, "gate0", -1)
            first_weights(1, 1)
            sp.wait_ge(scattered, 16 * NC)
            second_weights(1, 1)
            with sp.Fori(0, EX // 2 - 1) as i:
                for buf in range(2):
                    end = sp.value_load(tiles[0:1, 1, bass.ds(i * 2 + (buf + 1), 1)], min_val=1, max_val=MAXT)
                    sp.wait_ge(M["h"], end * 2)
                    first_weights(buf, i * 2 + (buf + 2))
                    sp.wait_ge(M["yv"], end + 1)
                    second_weights(buf, i * 2 + (buf + 2))
            end = sp.value_load(tiles[0:1, 2, 0:1], min_val=EX, max_val=MAXT)
            sp.wait_ge(M["yv"], end + 1)
            sp.dma_start(l1W1, ins["l1W1"]).then_inc(l1w, 16)
            sp.dma_start(l1W2, ins["l1W2"]).then_inc(l1w, 16)
            sp.wait_ge(M["done"], 1)
            for n in range(6, 8):
                ring_load(n)
            for l in range(2):
                if l:
                    full(sp, f"ffb{l - 1}", -1)
                sp.dma_start(ffW1[:], ins[f"ffW1_{l}"]).then_inc(ld_ff, 16)
                sp.dma_start(ffW2[:], ins[f"ffW2_{l}"]).then_inc(ld_ff, 16)
                if l:
                    stage_out(sp, f"ffa{l - 1}")
                    stage_out(sp, f"ffb{l - 1}")
                attention_loads(1 + l, f"att{1 + l}")
            for n in range(8, 12):
                ring_load(n)
            sp.wait_ge(x_done, NC)
            sp.dma_start(out, xres[:]).then_inc(stored, 16)
            sp.wait_ge(stored, 16)

        @block.gpsimd
        def _(pool):
            pool.iota(iota_src[:, 0:N], [[1, N]], base=0, channel_multiplier=0,
                      allow_small_or_imprecise_dtypes=True).then_inc(consts, 1)
            pool.iota(iota_dst[:, 0:NP], [[1, NP]], base=0, channel_multiplier=0,
                      allow_small_or_imprecise_dtypes=True).then_inc(consts, 1)
            pool.iota(iota_g[:, 0, :], [[1, EG]], base=1, channel_multiplier=0,
                      allow_small_or_imprecise_dtypes=True).then_inc(consts, 1)
            pool.iota(iota_g[:, 1, :], [[-1, EG]], base=EG, channel_multiplier=0,
                      allow_small_or_imprecise_dtypes=True).then_inc(consts, 1)
            pool.memset(onesf[:], 1.0).then_inc(consts, 1)
            pool.memset(zero_bf, 0.0).then_inc(consts, 1)
            pool.memset(twos[:], 2.0).then_inc(consts, 1)
            pool.memset(ident[:], 0.0).then_inc(consts, 1)
            pool.memset(zero_rows_sb, 0.0).then_inc(consts, 1)
            pool.wait_ge(consts, 9)
            pool.affine_select(out=ident[:], in_=ident[:], compare_op=ALU.not_equal, fill=1.0, base=0,
                               pattern=[[-1, P]], channel_multiplier=1).then_inc(consts, 1)
            pool.affine_select(out=upper[:], in_=onesf[0:NP, 0:NP], compare_op=ALU.is_gt, fill=0.0, base=0,
                               pattern=[[1, NP]], channel_multiplier=-1).then_inc(consts, 1)
            for t in range(MAXT + 2):
                pool.dma_start(xs_dram[t * TT:(t + 1) * TT, :], zero_rows_sb).then_inc(
                    zero_rows if t <= MAXT else M["st"], 16)
                if t < MAXT:
                    pool.dma_start(ys_dram[t * TT:(t + 1) * TT, :], zero_rows_sb).then_inc(zero_rows, 16)
            pool.wait_ge(adj_out, 4 * NC)
            pool.memset(bd[:, :, :], 0.0).then_inc(bd_zero, 1)
            pool.wait_ge(zero_rows, 16 * (2 * MAXT + 1))
            pool.wait_ge(M["st"], 16)
            pool.wait_ge(slots_ready, 1)
            for c in range(NC):
                pool.indirect_dma_start(
                    out=xs_dram, out_offset=bass.IndirectOffsetOnAxis(ap=idx[:, c:c + 1], axis=0),
                    in_=N3[:, c, :], in_offset=None).then_inc(scattered, 16)
            pool.wait_ge(scattered, 16 * NC)
            pool.dma_start(xs, xs_dram[0:TT, :]).then_inc(M["xs"], 16)
            pool.wait_ge(M["xsT"], 1)
            pool.dma_start(xs, xs_dram[TT:2 * TT, :]).then_inc(M["xs"], 16)
            total_tiles = pool.value_load(tiles[0:1, 2, 0:1], min_val=EX, max_val=MAXT)
            with pool.Fori(0, total_tiles) as g:
                pool.wait_ge(M["xsT"], g + 2)
                pool.dma_start(xs, xs_dram[bass.ds((g + 2) * TT, TT), :]).then_inc(M["xs"], 16)
                pool.wait_ge(M["yv"], g + 2)
                for q in range(2):
                    pool.dma_start(ys_dram[bass.ds(g * TT, TT), q * (D // 2):(q + 1) * (D // 2)],
                                   ys[q * TT:(q + 1) * TT, :]).then_inc(M["st"], 16)
            pool.wait_ge(M["st"], total_tiles * 32 + 16)
            pool.wait_ge(M["xs"], total_tiles * 16 + 32)
            pool.nop().then_inc(M["done"], 1)
            for c in range(NC):
                pool.indirect_dma_start(
                    out=yg[:, c, :], out_offset=None, in_=ys_dram,
                    in_offset=bass.IndirectOffsetOnAxis(ap=idx[:, c:c + 1], axis=0)).then_inc(gathered, 16)
            stage_out(pool, "ffb1")
            pool.memset(bd[:, :, :], 0.0).then_inc(bd_zero, 1)

        @block.tensor
        def _(pe):
            def take_bank(stage, i):
                n = FIRST[stage] + i
                if n >= 8:
                    e = UNIT[n - 8]
                    pe.wait_ge(freed_a if e == "a" else freed_v, freed_count(e, n - 8))
                return n % 8

            def rows_to_cols(stage, src, ready):
                for c in range(NC):
                    ready(c)
                    b = take_bank(stage, c)
                    for k in range(KC):
                        mm = pe.transpose(bank(b, P, NP, NP * k), src[:, c, k * P:(k + 1) * P], ident[0:NP, 0:NP])
                    mm.then_inc(unit_full, 1)

            def ring_ready(n):
                pe.wait_ge(ld_ring[n % 2], 16 * (n // 2 + 1))

            def product_rows(stage, srcT, n):
                ring_ready(n)
                for c in range(NC):
                    b = take_bank(stage, c)
                    for k in range(KC):
                        mm = pe.matmul(bank(b, NP, D), srcT[:, k, c * NP:(c + 1) * NP], ring[n % 2][:, k, :],
                                       start=(k == 0), stop=(k == KC - 1))
                    mm.then_inc(unit_full, 1)

            def product_cols(stage, srcT, n):
                ring_ready(n)
                for m in range(KC):
                    for h, (o, w) in enumerate(HALF):
                        b = take_bank(stage, 2 * m + h)
                        for k in range(KC):
                            mm = pe.matmul(bank(b, P, w), ring[n % 2][:, k, m * P:(m + 1) * P],
                                           srcT[:, k, o:o + w], start=(k == 0), stop=(k == KC - 1))
                        mm.then_inc(unit_full, 1)

            pe.wait_ge(consts, 11)
            rows_to_cols("xnT0", N1, lambda c: pe.wait_ge(ln_out, c + 1))
            stage_out(pe, "xnT0")
            product_rows("hp", T1, 0)

            pe.wait_ge(chunk_ind, 1)
            stage_out(pe, "hp")
            for h in range(2):
                pe.matmul(bank(h, 1, 400), onesf[0:NP, 0:1],
                          ind2.rearrange("p c t -> p (c t)")[:, 400 * h:400 * h + 400],
                          start=True, stop=True).then_inc(range_full, 1)
            pe.wait_ge(range_ready, 1)
            for c in range(NC):
                k = pe.value_load(bounds[0:1, 1, c:c + 1], min_val=1, max_val=EG)
                b0 = 4 * (c % 2)
                if c >= 2:
                    pe.wait_ge(adj_out, 4 * (c - 1))
                for q in range(4):
                    w = WIDE[q % 2][1]
                    mm = pe.matmul(bank(b0 + q, NP, w), zero_bf[:, 0:NP], iota_src[:, 0:w],
                                   start=True, stop=False, skip_group_check=True)
                    if q >= 2:
                        mm.then_inc(hot_free[c], 1)
                with pe.Fori(0, k) as j:
                    for s in range(2):
                        pe.wait_ge(hot_ready[c], j * 2 + s + 1)
                        for v in range(4):
                            for h, (o, w) in enumerate(WIDE):
                                mm = pe.matmul(bank(b0 + (2 if v == 3 else 0) + h, NP, w), one_dst[:, s, v, 0:NP],
                                               one_src[:, s, o:o + w], start=False, stop=False,
                                               skip_group_check=True)
                        mm.then_inc(hot_free[c], 1)
                for q in range(4):
                    w = WIDE[q % 2][1]
                    mm = pe.matmul(bank(b0 + q, NP, w), zero_bf[:, 0:NP], iota_src[:, 0:w],
                                   start=False, stop=True, skip_group_check=True)
                mm.then_inc(adj_full, 1)
            pe.wait_ge(adj_out, 4 * NC)
            for s in range(NC):
                for h in range(2):
                    b = take_bank("WT", 2 * s + h)
                    for c in (range(4) if h == 0 else [4]):
                        mm = pe.transpose(bank(b, NP, NP, NP * (c % 4)), Wrows[:, c, s * NP:(s + 1) * NP],
                                          ident[0:NP, 0:NP])
                    mm.then_inc(unit_full, 1)
            stage_out(pe, "WT")
            for c in range(NC):
                b = take_bank("agg", c)
                for s in range(NC):
                    mm = pe.matmul(bank(b, NP, D), WT[:, s, c * NP:(c + 1) * NP], N2[:, s, :],
                                   start=(s == 0), stop=(s == NC - 1))
                mm.then_inc(unit_full, 1)

            product_cols("mq", T1, 1)
            product_rows("mk", T1, 2)
            product_rows("mv", T1, 3)

            def key_values(stage, kr, vr):
                for m in range(KC):
                    b = take_bank(stage, m)
                    for c in range(NC):
                        pe.matmul(bank(b, P, P), kr[:, c, m * P:(m + 1) * P], vr[:, c, m * P:(m + 1) * P],
                                  start=(c == 0), stop=(c == NC - 1))
                    for c in range(NC):
                        mm = pe.matmul(bank(b, P, 1, P), kr[:, c, m * P:(m + 1) * P], onesf[0:NP, 0:1],
                                       start=(c == 0), stop=(c == NC - 1))
                    mm.then_inc(unit_full, 1)

            def query_products(stage, qT, w):
                for c in range(NC):
                    for h in range(2):
                        b = take_bank(stage, 2 * c + h)
                        for m in (2 * h, 2 * h + 1):
                            mm = pe.matmul(bank(b, NP, w, w * (m % 2)), qT[:, m, c * NP:(c + 1) * NP],
                                           bd[:, m, 0:w], start=True, stop=True)
                        mm.then_inc(unit_full, 1)

            stage_out(pe, "mk")
            stage_out(pe, "mv")
            key_values("mkv", N1, N3)
            stage_out(pe, "mq")
            stage_out(pe, "mkv")
            query_products("mo", T2, 130)
            rows_to_cols("moT", N2, lambda c: stage_out(pe, "mo", 2 * c + 2))
            stage_out(pe, "moT")
            product_rows("mp", T3, 4)
            rows_to_cols("yT", N1, lambda c: pe.wait_ge(ln_out, NC + c + 1))
            stage_out(pe, "yT")

            def attention(a, srcT):
                s = A[a]
                pe.nop().then_inc(s["ctx"], 1)

                def projection(w, i):
                    for h, (o, n) in enumerate(WIDE):
                        for k in range(KC):
                            mm = pe.matmul(bank(2 * w + h, P, n), aw[:, w, k, :], srcT[:, k, o:o + n],
                                           start=(k == 0), stop=(k == KC - 1))
                    mm.then_inc(s["qk"[w]], 1)

                def scores(i, t):
                    c, hh = divmod(t, 2)
                    if t < 2:
                        pe.wait_ge(s["qc"], i + 1)
                        pe.wait_ge(s["kc"], i + 1)
                    else:
                        pe.wait_ge(s["exp"], i * 10 + t - 1)
                    for h, (o, n) in enumerate(WIDE):
                        mm = pe.matmul(bank(2 * (t % 2) + h, NP, n), qt[hh * HD:(hh + 1) * HD, c * NP:(c + 1) * NP],
                                       kt[hh * HD:(hh + 1) * HD, o:o + n], start=True, stop=True)
                    mm.then_inc(s["score"], 1)

                def values(i):
                    pe.wait_ge(s["wv"], i * 16 + 16)
                    for c in range(NC):
                        for k in range(KC):
                            mm = pe.matmul(bank(4, NP, P, P * c), srcT[:, k, c * NP:(c + 1) * NP], aw[:, 2, k, :],
                                           start=(k == 0), stop=(k == KC - 1))
                    mm.then_inc(s["v"], 1)

                def turned(i, t):
                    c, hh = divmod(t, 2)
                    pe.wait_ge(s["prob"], i * 10 + t + 1)
                    if t == 0:
                        pe.wait_ge(s["vc"], i + 1)
                    for j in range(NC):
                        b, o = (4 + hh, NP * j) if j < 4 else (6, NP * hh)
                        mm = pe.matmul(bank(b, NP, NP, o), Pr[:, t % 2, j * NP:(j + 1) * NP], diag[:, t % 2, :],
                                       start=True, stop=True)
                    mm.then_inc(s["pT"], 1)

                def context(i, c):
                    pe.wait_ge(s["pTc"], i * 15 + 3 * c + 3)
                    pe.wait_ge(s["ctx"], i * 5 + c + 1)
                    for j in range(NC):
                        for hh in range(2):
                            mm = pe.matmul(psum[hh * HD:(hh + 1) * HD, 7 * 512:7 * 512 + NP],
                                           vv[:, j, hh * HD:(hh + 1) * HD],
                                           PT[:, c % 2 * NC + j, hh * NP:(hh + 1) * NP],
                                           start=(j == 0), stop=(j == NC - 1))
                    mm.then_inc(s["av"], 1)

                def pair(i, last):
                    for t in range(10):
                        scores(i, t)
                        if t == 1:
                            values(i)
                        if t >= 4 and t % 2 == 0:
                            context(i, t // 2 - 2)
                        if t >= 2:
                            turned(i, t - 2)
                    if not last:
                        pe.wait_ge(s["wqk"], i * 16 + 32)
                        pe.wait_ge(s["exp"], i * 10 + 9)
                        projection(0, i + 1)
                    context(i, 3)
                    turned(i, 8)
                    turned(i, 9)
                    if not last:
                        pe.wait_ge(s["exp"], i * 10 + 10)
                        projection(1, i + 1)
                    context(i, 4)

                pe.wait_ge(s["wqk"], 16)
                projection(0, 0)
                projection(1, 0)
                with pe.Fori(0, PAIRS - 1) as i:
                    pair(i, False)
                pair(PAIRS - 1, True)
                pe.wait_ge(s["ctx"], 5 * PAIRS + 1)

            attention(0, T1)
            product_rows("ao", T2, 5)
            rows_to_cols("tT", N3, lambda c: pe.wait_ge(ln_out, 2 * NC + c + 1))
            stage_out(pe, "tT")

            def gates(stage, srcT, W):
                b = take_bank(stage, 0)
                for c in range(NC):
                    for k in range(KC):
                        mm = pe.matmul(bank(b, NP, EX, EX * c), srcT[:, k, c * NP:(c + 1) * NP], W[:, k, :],
                                       start=(k == 0), stop=(k == KC - 1))
                mm.then_inc(unit_full, 1)

            pe.wait_ge(ld_const, 16 * 6)
            gates("gate0", T3, gateW)
            pe.wait_ge(gates_ready, 1)
            b = take_bank("rank", 0)
            onehot = small[0:NP, 200:240].rearrange("p (c e) -> p c e", e=EX)
            for c in range(NC + 1):
                for s in range(min(c + 1, NC)):
                    mm = pe.matmul(bank(b, NP, EX, EX * c), upper[:] if s == c else onesf[0:NP, 0:NP],
                                   onehot[:, s, :], start=(s == 0), stop=(s == min(c, NC - 1)))
            mm.then_inc(unit_full, 1)

            pe.wait_ge(slots_ready, 1)
            pe.nop().then_inc(M["y"], 1)

            def tile_columns(n):
                pe.wait_ge(M["xs"], n * 16 + 16)
                pe.matmul(bank(5, P, TT), xs[:, 0:P], ident[0:TT, 0:TT], start=True, stop=True)
                for k4 in range(1, KC):
                    mm = pe.transpose(bank(5, P, TT, TT * k4), xs[:, k4 * P:(k4 + 1) * P], ident[0:TT, 0:TT])
                mm.then_inc(M["xsT"], 1)

            tile_columns(0)
            with pe.Fori(0, EX // 2) as i:
                for par in range(2):
                    k = pe.value_load(tiles[0:1, 0, bass.ds(i * 2 + par, 1)], min_val=1, max_val=KT)
                    b0 = pe.value_load(tiles[0:1, 1, bass.ds(i * 2 + par, 1)], min_val=0, max_val=MAXT - 1)
                    with pe.Fori(0, k) as j:
                        g = b0 + j
                        pe.wait_ge(M[f"first{par}"], i * 16 + 16)
                        pe.wait_ge(M["xsTa"], g + 1)
                        for b in range(2):
                            for k4 in range(KC):
                                for q in range(2):
                                    o = q * (FF // 2) + b * D
                                    mm = pe.matmul(psum[q * TT:(q + 1) * TT, 512 * b:512 * b + D], xsT[:, k4, :],
                                                   EW1[par][:, k4, o:o + D], start=(k4 == 0), stop=(k4 == KC - 1))
                            mm.then_inc(M["h"], 1)
                        for b in range(2):
                            pe.wait_ge(M["hs"], g * 2 + b + 1)
                            for j4 in range(4):
                                mm = pe.transpose(bank(2 + b, P, P, P * j4), hs[:, b * D + j4 * P:b * D + (j4 + 1) * P],
                                                  ident[:, :])
                            mm.then_inc(M["hT"], 1)
                            if b == 0:
                                tile_columns(g + 1)
                        pe.wait_ge(M[f"second{par}"], i * 48 + 48)
                        pe.wait_ge(M["yv"], g + 1)
                        for n in range(FC):
                            b, j4, q_ = n // 8, n // 2 % 4, n % 2
                            f = q_ * (FC // 2) + b * 4 + j4
                            if q_ == 0:
                                pe.wait_ge(M["ha"], g * 8 + n // 2 + 1)
                            for q in range(2):
                                mm = pe.matmul(psum[q * TT:(q + 1) * TT, 4 * 512:4 * 512 + D // 2], hT[:, f, :],
                                               EW2[par][:, f, q * (D // 2):(q + 1) * (D // 2)],
                                               start=(n == 0), stop=(n == FC - 1))
                        mm.then_inc(M["y"], 1)

            rows_to_cols("xnT1", N2, lambda c: pe.wait_ge(ln_out, 3 * NC + c + 1))
            stage_out(pe, "xnT1")
            for l in range(2):
                attention(1 + l, T1 if l == 0 else T2)
                product_cols(f"wo{l}", T3, 6 + l)
                pe.wait_ge(bn_out, 8 * l + 4)
                pe.wait_ge(ld_ff, 32 * (l + 1))
                for h, (o, w) in enumerate(HALF):
                    b = take_bank(f"ffa{l}", h)
                    for k in range(KC):
                        mm = pe.matmul(bank(b, P, w), ffW1[:, k, :], T2[:, k, o:o + w], start=(k == 0), stop=(k == KC - 1))
                    mm.then_inc(unit_full, 1)
                stage_out(pe, f"ffa{l}")
                for m in range(KC):
                    for h, (o, w) in enumerate(HALF):
                        b = take_bank(f"ffb{l}", 2 * m + h)
                        mm = pe.matmul(bank(b, P, w), ffW2[:, m * P:(m + 1) * P], hid[:, o:o + w], start=True, stop=True)
                        mm.then_inc(unit_full, 1)
                pe.wait_ge(bn_out, 8 * l + 8)
            for c in range(NC):
                b = take_bank("gN", c)
                for k in range(KC):
                    mm = pe.transpose(bank(b, NP, P, P * k), T2[:, k, c * NP:(c + 1) * NP], ident[:, :])
                mm.then_inc(unit_full, 1)

            product_cols("nq", T1, 8)
            product_rows("nk", T1, 9)
            product_rows("nv", T1, 10)
            stage_out(pe, "nk")
            stage_out(pe, "nv")
            key_values("nkv", N1, N3)
            stage_out(pe, "nq")
            stage_out(pe, "nkv")
            query_products("no", T3, 132)
            rows_to_cols("noT", N2, lambda c: stage_out(pe, "no", 2 * c + 2))
            stage_out(pe, "noT")
            product_rows("np", T2, 11)

            rows_to_cols("zT", N1, lambda c: pe.wait_ge(ln_out, 5 * NC + c + 1))
            stage_out(pe, "zT")
            gates("gate1", T1, gateW1)
            pe.wait_ge(pb_l, 2)
            for w in range(2):
                for h in range(2):
                    b = take_bank("pb", 2 * w + h)
                    for c in (range(4) if h == 0 else [4]):
                        mm = pe.matmul(bank(b, P, NP, NP * (c % 4)), pbl[:, w, c, :], ident[0:NP, 0:NP],
                                       start=True, stop=True)
                    mm.then_inc(unit_full, 1)
            pe.wait_ge(l1w, 32)
            for f in range(EX):
                for h, (o, w) in enumerate(HALF):
                    b = take_bank("h1", 2 * f + h)
                    for k in range(KC):
                        mm = pe.matmul(bank(b, P, w), l1W1[:, k, f * P:(f + 1) * P], T1[:, k, o:o + w],
                                       start=(k == 0), stop=(k == KC - 1))
                    mm.then_inc(unit_full, 1)
            stage_out(pe, "h1")
            for c in range(NC):
                b = take_bank("o1", c)
                for f in range(EX):
                    pe.matmul(bank(b, NP, D), h1T[:, f, c * NP:(c + 1) * NP], l1W2[:, f, :], start=(f == 0), stop=False)
                pe.matmul(bank(b, NP, D), twos[:], b2rows[:], start=False, stop=True).then_inc(unit_full, 1)

        @block.scalar
        def _(act):
            def chunk_view(b):
                return bank(b, P, KC * NP).rearrange("p (k n) -> p k n", k=KC)

            def cols_out(stage, dst):
                for c in range(NC):
                    full(act, stage, c)
                    act.activation(dst[:, :, c * NP:(c + 1) * NP], chunk_view(unit_bank(stage, c)),
                                   ACT.Copy).then_inc(freed_a, 1)

            def rows_out(stage, dst, func=ACT.Copy):
                for c in range(NC):
                    full(act, stage, c)
                    act.activation(dst[:, c, :], bank(unit_bank(stage, c), NP, D), func).then_inc(freed_a, 1)

            def deviation(n):
                act.wait_ge(ln_var, n + 1)
                act.activation(small[0:NP, 40:45], small[0:NP, 30:35], ACT.Sqrt).then_inc(ln_sd, 1)

            deviation(0)
            cols_out("xnT0", T1)
            rows_out("hp", N2)
            for c in range(NC):
                act.wait_ge(adj_full, c + 1)
                b0 = 4 * (c % 2)
                for q in range(4):
                    o, w = WIDE[q % 2]
                    dst = (Wrows if q < 2 else cnt_adj)[:, c, o:o + w]
                    act.activation(dst, bank(b0 + q, NP, w), ACT.Copy).then_inc(adj_out, 1)
            for s in range(NC):
                full(act, "WT", 2 * s)
                act.activation(WT[:, s, 0:4 * NP], bank(unit_bank("WT", 2 * s), NP, 4 * NP), ACT.Copy).then_inc(freed_a, 1)
            for n in range(8 + NC):
                act.wait_ge(fm_min, n + 1)
                p, w = (P, HALF[n % 2][1]) if n < 8 else (NP, D)
                act.activation(fm[0:p, 1, 0:w], fm[0:p, 0, 0:w], ACT.Exp).then_inc(fm_exp, 1)
            cols_out("moT", T3)
            deviation(1)
            cols_out("yT", T1)

            def attention(a, bk, dst):
                s = A[a]

                def queries(i):
                    act.wait_ge(s["q"], i + 1)
                    act.activation(qt, psum[:, 0:N], ACT.Identity, bias=nbq[:, bass.ds(i + a * KC, 1)],
                                   scale=-ASCALE).then_inc(s["qc"], 1)

                def keys(i):
                    act.wait_ge(s["k"], i + 1)
                    if bk:
                        act.activation(kt, psum[:, 1024:1024 + N], ACT.Identity,
                                       bias=cols[:, bass.ds(i + COLS[bk][0], 1)]).then_inc(s["kc"], 1)
                    else:
                        act.activation(kt, psum[:, 1024:1024 + N], ACT.Copy).then_inc(s["kc"], 1)

                def exponentials(i, t):
                    act.wait_ge(s["max"], i * 10 + t + 1)
                    if t >= 2:
                        act.wait_ge(s["pT"], i * 10 + t - 1)
                    sc = psum[0:NP, 1024 * (t % 2):1024 * (t % 2) + N]
                    nmax = small[0:NP, 80 + t:81 + t]
                    act.activation(Pr[:, t % 2, :], sc, ACT.Exp, bias=nmax, scale=-1.0,
                                   accum_out=None if a else small[0:NP, 120 + t:121 + t]).then_inc(s["exp"], 1)

                def turned_out(i, t):
                    c, hh = divmod(t, 2)
                    act.wait_ge(s["pT"], i * 10 + t + 1)
                    act.activation(PT[:, c % 2 * NC:c % 2 * NC + 4, hh * NP:(hh + 1) * NP],
                                   bank(4 + hh, NP, 4 * NP).rearrange("p (j n) -> p j n", j=4),
                                   ACT.Copy).then_inc(s["pTc"], 1)
                    if hh:
                        act.activation(PT[:, c % 2 * NC + 4, :], bank(6, NP, 2 * NP), ACT.Copy).then_inc(s["pTc"], 1)

                def context_out(i, c):
                    act.wait_ge(s["av"], i * 5 + c + 1)
                    act.activation(dst[:, bass.ds(i, 1), c * NP:(c + 1) * NP], bank(7, P, NP).unsqueeze(1),
                                   ACT.Copy).then_inc(s["ctx"], 1)

                def pair(i, last):
                    for t in range(10):
                        exponentials(i, t)
                        if t >= 4 and t % 2 == 0:
                            context_out(i, t // 2 - 2)
                        if t >= 2:
                            turned_out(i, t - 2)
                    if not last:
                        queries(i + 1)
                    context_out(i, 3)
                    turned_out(i, 8)
                    turned_out(i, 9)
                    if not last:
                        keys(i + 1)
                    context_out(i, 4)

                queries(0)
                keys(0)
                with act.Fori(0, PAIRS - 1) as i:
                    pair(i, False)
                pair(PAIRS - 1, True)

            act.wait_ge(ld_const, 16 * 6)
            act.wait_ge(nbq_ready, 3)
            attention(0, "ffn_bk", T2)
            deviation(2)
            cols_out("tT", T3)
            act.wait_ge(gl_in, 1)
            act.activation(small[0:NP, 240:280], small[0:NP, 160:200], ACT.Exp).then_inc(gl_out, 1)
            act.wait_ge(slots_ready, 1)

            def tile_columns(n):
                act.wait_ge(M["xsT"], n + 1)
                act.activation(xsT.rearrange("p a b -> p (a b)"), bank(5, P, KC * TT), ACT.Copy).then_inc(M["xsTa"], 1)

            tile_columns(0)
            with act.Fori(0, EX) as e:
                k = act.value_load(tiles[0:1, 0, bass.ds(e, 1)], min_val=1, max_val=KT)
                b0 = act.value_load(tiles[0:1, 1, bass.ds(e, 1)], min_val=0, max_val=MAXT - 1)
                with act.Fori(0, k) as j:
                    g = b0 + j
                    act.wait_ge(M["y"], g + 1)
                    for b in range(2):
                        act.wait_ge(M["hT"], g * 2 + b + 1)
                        for j4 in range(4):
                            for q in range(2):
                                f = q * (FC // 2) + b * 4 + j4
                                done = act.activation(hT[:, f, :], bank(2 + b, P, TT, P * j4 + TT * q),
                                                      ACT.Gelu_apprx_tanh,
                                                      bias=cols[:, bass.ds(e * FC + (COLS["moe_b1"][0] + f), 1)])
                            done.then_inc(M["ha"], 1)
                    tile_columns(g + 1)
            deviation(3)
            cols_out("xnT1", T1)

            def batch_deviation(n):
                act.wait_ge(bn_var, n + 1)
                act.activation(small[:, 40:44], small[:, 30:34], ACT.Sqrt).then_inc(bn_sd, 1)

            for l in range(2):
                attention(1 + l, None, T3)
                batch_deviation(2 * l)
                for h, (o, w) in enumerate(HALF):
                    full(act, f"ffa{l}", h)
                    act.activation(hid[:, o:o + w], bank(unit_bank(f"ffa{l}", h), P, w), ACT.Relu,
                                   bias=col(f"b1{l}")).then_inc(freed_a, 1)
                batch_deviation(2 * l + 1)
            rows_out("gN", N2)
            deviation(4)
            for m in range(KC):
                for h, (o, w) in enumerate(HALF):
                    full(act, "nq", 2 * m + h)
                    act.activation(T3[:, m, o:o + w], bank(unit_bank("nq", 2 * m + h), P, w), ACT.Relu).then_inc(freed_a, 1)
            rows_out("nk", N1, ACT.Relu)
            rows_out("nv", N3)
            cols_out("noT", T2)
            deviation(5)
            cols_out("zT", T1)
            act.wait_ge(gl_in, 2)
            act.activation(small[0:NP, 240:280], small[0:NP, 160:200], ACT.Exp).then_inc(gl_out, 1)
            for w in range(2):
                for h, (o, n) in enumerate([(0, 4 * NP), (4 * NP, NP)]):
                    full(act, "pb", 2 * w + h)
                    act.activation(PB[:, w, o:o + n], bank(unit_bank("pb", 2 * w + h), P, n), ACT.Copy).then_inc(freed_a, 1)
            for n in range(16):
                f, h = divmod(n, 2)
                w = HALF[h][1]
                for q in range(2):
                    act.wait_ge(h_in, 2 * n + q + 1)
                    act.activation(hb[:, 2 + q, 0:w], hb[:, q, 0:w], ACT.Gelu, bias=col("l1_b1", f)).then_inc(h_g, 1)

        @block.vector
        def _(ve):
            done = [0]

            def link(ins_):
                done[0] += 1
                ins_.then_inc(dve, 1)
                ve.wait_ge(dve, done[0])

            def layer_norm(n, src, dst, gamma=None, beta=None):
                for c in range(NC):
                    ve.bn_stats(small[0:NP, 6 * c:6 * c + 6], src[:, c, :]) if c < NC - 1 else link(
                        ve.bn_stats(small[0:NP, 6 * c:6 * c + 6], src[:, c, :]))
                for c in range(NC):
                    i_ = ve.bn_aggr(small[0:NP, 50 + 2 * c:52 + 2 * c], small[0:NP, 6 * c:6 * c + 6])
                link(i_)
                mv = small[0:NP, 50:60].rearrange("p (c t) -> p c t", t=2)
                ve.tensor_scalar(small[0:NP, 30:35], mv[:, :, 1], EPS, None, ALU.add).then_inc(ln_var, 1)
                ve.wait_ge(ln_sd, n + 1)
                link(ve.reciprocal(small[0:NP, 60:65], small[0:NP, 40:45]))
                for c in range(NC):
                    i_ = ve.tensor_scalar(dst[:, c, :], src[:, c, :], mv[:, c, 0:1], small[0:NP, 60 + c:61 + c],
                                          ALU.subtract, ALU.mult)
                    if gamma is None:
                        i_.then_inc(ln_out, 1)
                    else:
                        link(i_)
                        link(ve.tensor_tensor(dst[:, c, :], dst[:, c, :], row(gamma), ALU.mult))
                        ve.tensor_tensor(dst[:, c, :], dst[:, c, :], row(beta), ALU.add).then_inc(ln_out, 1)

            ve.wait_ge(ld_edges, 48)
            link(ve.tensor_copy(srcf, srci))
            link(ve.tensor_copy(dstf, dsti))
            for c in range(NC):
                link(ve.tensor_scalar(dstr[:, c, :], dstf, float(-NP * c), None, ALU.add))
            link(ve.tensor_scalar(ind, dstr, 0.0, None, ALU.is_ge))
            ve.scalar_tensor_tensor(ind2, dstr, float(NP), ind, ALU.is_lt, ALU.mult).then_inc(chunk_ind, 1)
            link(ve.tensor_copy(wbf, wgt))
            link(ve.tensor_copy(wpart[:, 0], wbf))
            link(ve.tensor_tensor(wrest[:, 0], wgt, wpart[:, 0], ALU.subtract))
            link(ve.tensor_copy(wbf, wrest[:, 0]))
            link(ve.tensor_copy(wpart[:, 1], wbf))
            link(ve.tensor_tensor(wpart[:, 2], wrest[:, 0], wpart[:, 1], ALU.subtract))
            ve.wait_ge(ld_x, 16)
            layer_norm(0, xres, N1)
            ve.wait_ge(range_full, 2)
            ve.wait_ge(consts, 11)
            flat = g_cnt.rearrange("p c g -> p (c g)")
            for h in range(2):
                link(ve.tensor_reduce(flat[:, 200 * h:200 * h + 200],
                                      bank(h, 1, 400).rearrange("p (g t) -> p g t", t=2), AX, ALU.add))
            link(ve.tensor_scalar(g_cnt, g_cnt, 0.5, None, ALU.is_gt))
            for c in range(NC):
                ve.tensor_tensor(g_a[:, c, :], g_cnt[:, c, :], iota_g[:, 0, :], ALU.mult)
                link(ve.tensor_tensor(g_b[:, c, :], g_cnt[:, c, :], iota_g[:, 1, :], ALU.mult))
            ve.tensor_reduce(g_hi, g_a, AX, ALU.max)
            link(ve.tensor_reduce(g_lo, g_b, AX, ALU.max))
            link(ve.tensor_scalar(g_n, g_lo, -1.0, float(EG), ALU.mult, ALU.add))
            link(ve.tensor_scalar(g_lo, g_n, float(EG - 1), None, ALU.min))
            link(ve.tensor_tensor(g_n, g_hi, g_lo, ALU.subtract))
            link(ve.tensor_scalar(g_hi, g_n, 1.0, None, ALU.max))
            link(ve.tensor_copy(bounds[:, 0, 0:NC], g_lo))
            ve.tensor_copy(bounds[:, 1, 0:NC], g_hi).then_inc(range_ready, 1)
            ve.wait_ge(range_ready, 1)
            for c in range(NC):
                first = ve.value_load(bounds[0:1, 0, c:c + 1], min_val=0, max_val=EG - 1)
                k = ve.value_load(bounds[0:1, 1, c:c + 1], min_val=1, max_val=EG)
                with ve.Fori(0, k) as j:
                    g = nc.s_assert_within(first + j, 0, EG - 1,
                                           skip_runtime_bounds_check_because="a chunk's groups end below EG")
                    for s in range(2):
                        ve.wait_ge(hot_free[c], j * 2 + s + 1)
                        e = bass.ds(g * 2 + s, 1)
                        for v in range(3):
                            ve.tensor_scalar(one_dst[:, s, v, 0:NP], iota_dst[:, 0:NP], dstr[:, c, e],
                                             wpart[:, v, e], ALU.is_equal, ALU.mult)
                        ve.tensor_scalar(one_dst[:, s, 3, 0:NP], iota_dst[:, 0:NP], dstr[:, c, e], None, ALU.is_equal)
                        ve.tensor_scalar(one_src[:, s, 0:N], iota_src[:, 0:N], srcf[:, e], None,
                                         ALU.is_equal).then_inc(hot_ready[c], 1)
            for s in range(NC):
                full(ve, "WT", 2 * s + 1)
                ve.tensor_copy(WT[:, s, 4 * NP:N], bank(unit_bank("WT", 2 * s + 1), NP, NP)).then_inc(freed_v, 1)
            for c in range(NC):
                full(ve, "agg", c)
                i_ = ve.scalar_tensor_tensor(xres[:, c, :], bank(unit_bank("agg", c), NP, D), 0.0, xres[:, c, :],
                                             ALU.max, ALU.add)
                i_.then_inc(freed_v, 1)
            ve.wait_ge(ld_const, 16 * 6)
            for n in range(8):
                m, h = divmod(n, 2)
                o, w = HALF[h]
                full(ve, "mq", n)
                b = unit_bank("mq", n)
                ve.tensor_scalar(fm[:, 0, 0:w], bank(b, P, w), col("mix_bq", m), 0.0, ALU.add, ALU.min).then_inc(fm_min, 1)
                link(ve.tensor_scalar(fm[:, 2, 0:w], bank(b, P, w), col("mix_bq", m), 1.0, ALU.add, ALU.add))
                ve.wait_ge(fm_exp, n + 1)
                i_ = ve.tensor_tensor(T2[:, m, o:o + w], fm[:, 2, 0:w], fm[:, 1, 0:w], ALU.max)
                i_.then_inc(freed_v, 1)
                ve.wait_ge(freed_v, freed_count("v", FIRST["mq"] + n))
            for c in range(NC):
                full(ve, "mk", c)
                link(ve.tensor_tensor(fm[0:NP, 2, :], bank(unit_bank("mk", c), NP, D), row("mix_bk"), ALU.add))
                ve.tensor_scalar(fm[0:NP, 0, :], fm[0:NP, 2, :], 0.0, None, ALU.min).then_inc(fm_min, 1)
                ve.wait_ge(fm_exp, 8 + c + 1)
                ve.scalar_tensor_tensor(N1[:, c, :], fm[0:NP, 2, :], 1.0, fm[0:NP, 1, :], ALU.add,
                                        ALU.max).then_inc(freed_v, 1)
                ve.wait_ge(freed_v, freed_count("v", FIRST["mk"] + c))
            for c in range(NC):
                full(ve, "mv", c)
                ve.tensor_tensor(N3[:, c, :], bank(unit_bank("mv", c), NP, D), row("mix_bv"), ALU.add).then_inc(freed_v, 1)

            def diagonal_blocks(stage, hd, turn):
                ve.wait_ge(bd_zero, turn)
                for m in range(KC):
                    full(ve, stage, m)
                    b = unit_bank(stage, m)
                    for h in range(P // hd):
                        r = slice(h * hd, (h + 1) * hd)
                        ve.tensor_copy(bd[r, m, r], psum[r, 512 * b + h * hd:512 * b + (h + 1) * hd])
                        i_ = ve.tensor_copy(bd[r, m, P + h:P + h + 1], psum[r, 512 * b + P:512 * b + P + 1])
                    i_.then_inc(freed_v, 1)

            def divided(stage, hd, dst, eps=None):
                nh = P // hd
                for c in range(NC):
                    for h in range(2):
                        full(ve, stage, 2 * c + h)
                        v = bank(unit_bank(stage, 2 * c + h), NP, 2 * (P + nh)).rearrange("p (m w) -> p m w", m=2)
                        z = mz[:, :, 0:nh]
                        if eps is None:
                            link(ve.reciprocal(z, v[:, :, P:P + nh]))
                        else:
                            link(ve.tensor_scalar(z, v[:, :, P:P + nh], eps, None, ALU.add))
                            link(ve.reciprocal(z, z))
                        for m in range(2):
                            o = (2 * h + m) * P
                            i_ = ve.tensor_tensor(
                                dst[:, c, o:o + P].rearrange("p (h d) -> p h d", d=hd),
                                v[:, m, 0:P].rearrange("p (h d) -> p h d", d=hd),
                                z[:, m, :].unsqueeze(2).to_broadcast([NP, nh, hd]), ALU.mult)
                            if m == 0:
                                link(i_)
                        i_.then_inc(freed_v, 1)
                        ve.wait_ge(freed_v, freed_count("v", FIRST[stage] + 2 * c + h))

            def add_rows(stage, base, dst, bias):
                for c in range(NC):
                    full(ve, stage, c)
                    link(ve.tensor_tensor(dst[:, c, :], bank(unit_bank(stage, c), NP, D), base[:, c, :], ALU.add))
                    ve.tensor_tensor(dst[:, c, :], dst[:, c, :], row(bias), ALU.add).then_inc(freed_v, 1)
                ve.wait_ge(freed_v, freed_count("v", FIRST[stage] + NC - 1))

            diagonal_blocks("mkv", 64, 1)
            divided("mo", 64, N2)
            add_rows("mp", xres, xres, "mix_bp")
            layer_norm(1, xres, N1)
            for a, name in enumerate(["ffn_bq", "bq0", "bq1"]):
                ve.tensor_scalar(nbq[:, a * KC:(a + 1) * KC], cols[:, COLS[name][0]:COLS[name][0] + KC], -ASCALE,
                                 None, ALU.mult).then_inc(nbq_ready, 1)

            def attention(a, bv):
                s = A[a]

                def values(i):
                    ve.wait_ge(s["v"], i + 1)
                    for c, w in ((0, 4), (4, 1)):
                        src_ = bank(4 + c // 4, NP, P * w).rearrange("p (c d) -> p c d", d=P)
                        if bv:
                            b_ = rows[:, ROWS[bv], bass.ds(i * P, P)].unsqueeze(1).to_broadcast([NP, w, P])
                            i_ = ve.tensor_tensor(vv[:, c:c + w, :], src_, b_, ALU.add)
                        else:
                            i_ = ve.tensor_copy(vv[:, c:c + w, :], src_)
                    i_.then_inc(s["vc"], 1)

                def largest(i, t):
                    ve.wait_ge(s["score"], i * 10 + t + 1)
                    sc = psum[0:NP, 1024 * (t % 2):1024 * (t % 2) + N]
                    if a:
                        ve.memset(small[0:1, 90 + t:91 + t], 0.0)
                        ve.tensor_tensor_reduce(sc, sc, maskb[:, t // 2, :], 1.0, 3.0e38, ALU.add, ALU.min,
                                                small[0:NP, 80 + t:81 + t]).then_inc(s["max"], 1)
                    else:
                        ve.tensor_reduce(small[0:NP, 80 + t:81 + t], sc, AX, ALU.min).then_inc(s["max"], 1)

                def sums(i, t):
                    total = small[0:NP, 120 + t:121 + t]
                    inv = small[0:NP, 140 + t:141 + t]
                    n = 2 if a else 1
                    ve.wait_ge(s["exp"], i * 10 + t + 1)
                    if a:
                        ve.tensor_tensor_reduce(Pr[:, t % 2, :], Pr[:, t % 2, :], cnt_adj[:, t // 2, :], 1.0, 1e-16,
                                                ALU.mult, ALU.add, total).then_inc(s["sum"], 1)
                        ve.wait_ge(s["sum"], i * 20 + 2 * t + 1)
                    ve.reciprocal(inv, total).then_inc(s["sum"], 1)
                    ve.wait_ge(s["sum"], i * (10 * n) + n * (t + 1))
                    if t >= 2:
                        ve.wait_ge(s["pT"], i * 10 + t - 1)
                    ve.tensor_scalar(diag[:, t % 2, :], ident[0:NP, 0:NP], inv, None,
                                     ALU.mult).then_inc(s["prob"], 1)

                with ve.Fori(0, PAIRS) as i:
                    for t in range(11):
                        if t < 10:
                            largest(i, t)
                        if t >= 1:
                            sums(i, t - 1)
                        if t == 1:
                            values(i)

            attention(0, "ffn_bv")
            add_rows("ao", N1, N2, "ffn_bo")
            layer_norm(2, N2, N3, "ln1_g", "ln1_b")

            lg = small[0:NP, 160:200].rearrange("p (c e) -> p c e", e=EX)
            ex = small[0:NP, 240:280].rearrange("p (c e) -> p c e", e=EX)
            one = small[0:NP, 200:240].rearrange("p (c e) -> p c e", e=EX)
            tmp = small[0:NP, 280:320].rearrange("p (c e) -> p c e", e=EX)
            mx = small[0:NP, 320:325]
            sm = small[0:NP, 325:330]
            gw = small[0:NP, 330:335]
            v5 = small[0:NP, 335:340]
            bc = lambda x: x.unsqueeze(2).to_broadcast([NP, NC, EX])

            def exp_gates(stage, n, bias):
                full(ve, stage, 0)
                v = bank(unit_bank(stage, 0), NP, NC * EX).rearrange("p (c e) -> p c e", e=EX)
                if bias:
                    i_ = ve.tensor_tensor(lg, v, gate_b[:].unsqueeze(1).to_broadcast([NP, NC, EX]), ALU.add)
                else:
                    i_ = ve.tensor_copy(lg, v)
                i_.then_inc(freed_v, 1)
                ve.wait_ge(freed_v, freed_count("v", FIRST[stage]))
                link(ve.tensor_reduce(mx, lg, AX, ALU.max))
                ve.tensor_tensor(lg, lg, bc(mx), ALU.subtract).then_inc(gl_in, 1)
                ve.wait_ge(gl_out, n)
                link(ve.tensor_reduce(sm, ex, AX, ALU.add))

            exp_gates("gate0", 1, True)
            link(ve.reciprocal(gw, sm))
            e8 = small[0:NP, 340:348]
            for e in range(EX):
                i_ = ve.memset(e8[:, e:e + 1], float(EX - e))
            link(i_)
            link(ve.tensor_reduce(v5, ex, AX, ALU.max))
            link(ve.tensor_tensor(tmp, ex, bc(v5), ALU.is_equal))
            link(ve.tensor_tensor(tmp, tmp, e8.unsqueeze(1).to_broadcast([NP, NC, EX]), ALU.mult))
            link(ve.tensor_reduce(v5, tmp, AX, ALU.max))
            ve.tensor_tensor(one, e8.unsqueeze(1).to_broadcast([NP, NC, EX]), bc(v5), ALU.is_equal).then_inc(gates_ready, 1)
            full(ve, "rank", 0)
            b = unit_bank("rank", 0)
            nt = small[0:NP, 350:358]
            ft = small[0:NP, 360:368]
            cnt_e = small[0:NP, 370:378]
            big = small[0:NP, 378:386]
            link(ve.tensor_copy(cnt_e, bank(b, NP, EX, EX * NC)))
            link(ve.memset(nt, 1.0))
            for k in range(1, KT):
                link(ve.tensor_scalar(big, cnt_e, k * TT + 0.5, None, ALU.is_gt))
                link(ve.tensor_tensor(nt, nt, big, ALU.add))
            link(ve.memset(ft[:, 0:1], 0.0))
            for e in range(1, EX):
                link(ve.tensor_tensor(ft[:, e:e + 1], ft[:, e - 1:e], nt[:, e - 1:e], ALU.add))
            link(ve.tensor_scalar(big, ft, float(TT), None, ALU.mult))
            ve.tensor_tensor(tmp, bank(b, NP, NC * EX).rearrange("p (c e) -> p c e", e=EX),
                             big.unsqueeze(1).to_broadcast([NP, NC, EX]), ALU.add).then_inc(freed_v, 1)
            ve.wait_ge(freed_v, freed_count("v", FIRST["rank"]))
            link(ve.tensor_tensor(tmp, tmp, one, ALU.mult))
            link(ve.tensor_reduce(v5, tmp, AX, ALU.add))
            link(ve.tensor_copy(idx[:], v5))
            link(ve.tensor_tensor(big[:, 0:1], ft[:, EX - 1:EX], nt[:, EX - 1:EX], ALU.add))
            link(ve.tensor_copy(tiles[:, 2, 0:1], big[0:1, 0:1]))
            link(ve.tensor_copy(tiles[:, 0, :], nt[0:1, :]))
            ve.tensor_copy(tiles[:, 1, :], ft[0:1, :]).then_inc(slots_ready, 1)
            ve.wait_ge(slots_ready, 1)
            ve.nop().then_inc(M["yv"], 1)
            with ve.Fori(0, EX // 2) as i:
                for par in range(2):
                    k = ve.value_load(tiles[0:1, 0, bass.ds(i * 2 + par, 1)], min_val=1, max_val=KT)
                    b0 = ve.value_load(tiles[0:1, 1, bass.ds(i * 2 + par, 1)], min_val=0, max_val=MAXT - 1)
                    with ve.Fori(0, k) as j:
                        g = b0 + j
                        for b in range(2):
                            ve.wait_ge(M["h"], g * 2 + b + 1)
                            ve.tensor_copy(hs[:, b * D:(b + 1) * D], bank(b, P, D)).then_inc(M["hs"], 1)
                        ve.wait_ge(M["y"], g + 2)
                        ve.wait_ge(M["st"], g * 32 + 16)
                        ve.wait_ge(M[f"second{par}"], i * 48 + 48)
                        ve.tensor_tensor(ys, bank(4, P, D // 2), eb2[par], ALU.add).then_inc(M["yv"], 1)
            ve.wait_ge(gathered, 16 * NC)
            for c in range(NC):
                i_ = ve.scalar_tensor_tensor(xres[:, c, :], yg[:, c, :], gw[:, c:c + 1], xres[:, c, :], ALU.mult, ALU.add)
            link(i_)
            layer_norm(3, xres, N2)
            ve.tensor_scalar(maskb, cnt_adj[:], 0.5, NO_EDGE, ALU.is_lt, ALU.mult).then_inc(mask_ready, 1)
            ve.wait_ge(mask_ready, 1)

            def batch_norm(n, g, beta):
                for m in range(KC):
                    for h, (o, w) in enumerate(HALF):
                        i_ = ve.bn_stats(small[:, 400 + 12 * m + 6 * h:406 + 12 * m + 6 * h], T2[:, m, o:o + w])
                link(i_)
                for m in range(KC):
                    i_ = ve.bn_aggr(small[:, 460 + 2 * m:462 + 2 * m], small[:, 400 + 12 * m:412 + 12 * m])
                link(i_)
                mv = small[:, 460:468].rearrange("p (m t) -> p m t", t=2)
                ve.tensor_scalar(small[:, 30:34], mv[:, :, 1], EPS, None, ALU.add).then_inc(bn_var, 1)
                ve.wait_ge(bn_sd, n + 1)
                link(ve.reciprocal(small[:, 470:474], small[:, 40:44]))
                link(ve.tensor_tensor(small[:, 474:478], small[:, 470:474], cols[:, COLS[g][0]:COLS[g][0] + 4], ALU.mult))
                link(ve.tensor_tensor(small[:, 478:482], small[:, 474:478], mv[:, :, 0], ALU.mult))
                link(ve.tensor_tensor(small[:, 482:486], cols[:, COLS[beta][0]:COLS[beta][0] + 4], small[:, 478:482],
                                      ALU.subtract))
                for m in range(KC):
                    i_ = ve.tensor_scalar(T2[:, m, :], T2[:, m, :], small[:, 474 + m:475 + m], small[:, 482 + m:483 + m],
                                          ALU.mult, ALU.add)
                    i_.then_inc(bn_out, 1)
                ve.wait_ge(bn_out, 4 * (n + 1))

            def add_cols(stage, base, bias):
                for n in range(8):
                    m, h = divmod(n, 2)
                    o, w = HALF[h]
                    full(ve, stage, n)
                    ve.scalar_tensor_tensor(T2[:, m, o:o + w], bank(unit_bank(stage, n), P, w), col(bias, m),
                                            base[:, m, o:o + w], ALU.add, ALU.add).then_inc(freed_v, 1)
                ve.wait_ge(freed_v, freed_count("v", FIRST[stage] + 7))

            for l in range(2):
                attention(1 + l, None)
                add_cols(f"wo{l}", T1 if l == 0 else T2, f"bo{l}")
                batch_norm(2 * l, f"g1{l}", f"beta1{l}")
                add_cols(f"ffb{l}", T2, f"b2{l}")
                batch_norm(2 * l + 1, f"g2{l}", f"beta2{l}")
            stage_out(ve, "gN")
            layer_norm(4, N2, N2, "ln_g", "ln_b")
            ve.wait_ge(ln_out, 5 * NC)
            for c in range(NC):
                i_ = ve.tensor_tensor(xres[:, c, :], xres[:, c, :], N2[:, c, :], ALU.add)
            link(i_)
            diagonal_blocks("nkv", 32, 2)
            divided("no", 32, N2, 1e-15)
            add_rows("np", xres, xres, "proj_b")
            layer_norm(5, xres, N1)
            exp_gates("gate1", 2, False)
            for c in range(NC):
                i_ = ve.max(small[0:NP, 500 + 8 * c:508 + 8 * c], ex[:, c, :])
            link(i_)
            top = small[0:NP, 500:540].rearrange("p (c e) -> p c e", e=EX)
            pr = small[0:NP, 540:550].rearrange("p (c e) -> p c e", e=2)
            link(ve.reciprocal(gw, sm))
            link(ve.tensor_tensor(pr, top[:, :, 0:2], gw.unsqueeze(2).to_broadcast([NP, NC, 2]), ALU.mult))
            link(ve.tensor_reduce(mx, pr, AX, ALU.add))
            link(ve.reciprocal(sm, mx))
            link(ve.tensor_tensor(pr, pr, sm.unsqueeze(2).to_broadcast([NP, NC, 2]), ALU.mult))
            for w in range(2):
                ve.tensor_copy(pbl[:, w, :, :], pr[:, :, w].unsqueeze(2).to_broadcast([NP, NC, P])).then_inc(pb_l, 1)
            stage_out(ve, "pb")
            for n in range(16):
                f, h = divmod(n, 2)
                o, w = HALF[h]
                full(ve, "h1", n)
                b = unit_bank("h1", n)
                for q in range(2):
                    ve.tensor_tensor(hb[:, q, 0:w], bank(b, P, w), PB[:, q, o:o + w], ALU.mult).then_inc(h_in, 1)
                ve.wait_ge(h_g, 2 * n + 2)
                ve.tensor_tensor(h1T[:, f, o:o + w], hb[:, 2, 0:w], hb[:, 3, 0:w], ALU.add).then_inc(freed_v, 1)
                ve.wait_ge(freed_v, freed_count("v", FIRST["h1"] + n))
            for c in range(NC):
                full(ve, "o1", c)
                ve.tensor_tensor(xres[:, c, :], bank(unit_bank("o1", c), NP, D), xres[:, c, :], ALU.add).then_inc(x_done, 1)


def kernel(**inputs):
    import numpy as np
    import concourse.bacc as bacc
    from concourse.bass_utils import run_bass_kernel_spmd

    a = {k: np.asarray(v) for k, v in inputs.items()}

    def as_rows(x):
        return x.reshape(NC, NP, D).transpose(1, 0, 2)

    def edges(x):
        return x.reshape(ET, NP).T

    def weight(w):
        return w.reshape(w.shape[0] // P, P, w.shape[1]).transpose(1, 0, 2)

    def pair_weights(q, k, v):
        w = np.stack([q, k, v]).reshape(3, KC, P, PAIRS, P)
        return w.transpose(3, 2, 0, 1, 4)

    vectors = {"mix_bq": a["L0_mix_bq"], "ffn_bq": a["L0_ffn_bq"], "ffn_bk": a["L0_ffn_bk"],
               "moe_b1": a["L0_ffn_b1"], "l1_b1": a["L1_ffn_b1"]}
    for l in range(2):
        for v in ("bq", "bo", "b1", "b2", "g1", "beta1", "g2", "beta2"):
            vectors[f"{v}{l}"] = a[f"L1_gnn_{v}"][l]
    qkv = a["L1_mix_qkv_weight"]
    arrays = {
        "src": edges(a["src"]), "dst": edges(a["dst"]), "edge_w": edges(a["edge_weight"]), "x": as_rows(a["x"]),
        "cols": np.concatenate([vectors[n].reshape(w, P) for n, (_, w) in COLS.items()]).T,
        "rows": np.stack([a[n] for n in (
            "L0_mix_bk", "L0_mix_bv", "L0_mix_bp", "L0_ffn_bv", "L0_ffn_bo", "L0_ffn_ln1_g", "L0_ffn_ln1_b",
            "L1_gnn_ln_g", "L1_gnn_ln_b", "L1_mix_proj_bias")]),
        "gate_b": a["L0_ffn_gate_b"], "moe_b2": a["L0_ffn_b2"], "l1_b2": a["L1_ffn_b2"],
        "gateW": weight(a["L0_ffn_gate_W"]), "gateW1": weight(a["L1_ffn_Wg"]),
        "gnnW": weight(a["L0_gnn_weight"]), "mixWq": weight(a["L0_mix_Wq"]), "mixWk": weight(a["L0_mix_Wk"]),
        "mixWv": weight(a["L0_mix_Wv"]), "mixWp": weight(a["L0_mix_Wp"]), "ffnWo": weight(a["L0_ffn_Wo"]),
        "att0": pair_weights(a["L0_ffn_Wq"], a["L0_ffn_Wk"], a["L0_ffn_Wv"]),
        "moeW1": a["L0_ffn_W1"].reshape(EX, KC, P, FF).transpose(0, 2, 1, 3),
        "moeW2": a["L0_ffn_W2"].reshape(EX, FC, P, D).transpose(0, 2, 1, 3),
        "m1q": weight(qkv[0:D].T), "m1k": weight(qkv[D:2 * D].T), "m1v": weight(qkv[2 * D:].T),
        "m1p": weight(a["L1_mix_proj_weight"].T),
        "l1W1": weight(a["L1_ffn_W1"].transpose(1, 0, 2).reshape(D, EX * F1)),
        "l1W2": a["L1_ffn_W2"].transpose(1, 0, 2),
    }
    for l in range(2):
        arrays[f"att{l + 1}"] = pair_weights(*(a[f"L1_gnn_{w}"][l].T for w in ("Wq", "Wk", "Wv")))
        arrays[f"gnnWo{l}"] = weight(a["L1_gnn_Wo"][l].T)
        arrays[f"ffW1_{l}"] = weight(a["L1_gnn_W1"][l].T)
        arrays[f"ffW2_{l}"] = a["L1_gnn_W2"][l].T
    arrays = {f"in_{k}": np.ascontiguousarray(v) for k, v in arrays.items()}

    nc = bacc.Bacc("TRN2", target_bir_lowering=False, num_devices=1)
    ins = {k[3:]: nc.dram_tensor(k, v.shape, mybir.dt.from_np(v.dtype), kind="ExternalInput").ap()
           for k, v in arrays.items()}
    out = nc.dram_tensor("out_rows", [NP, NC, D], F32, kind="ExternalOutput").ap()
    build(nc, ins, out)
    r = run_bass_kernel_spmd(nc, [arrays], core_ids=[0])
    return r.results[0]["out_rows"].transpose(1, 0, 2).reshape(N, D)
```

```python
from contextlib import ExitStack

import concourse.bass as bass
from concourse import mybir

F32 = mybir.dt.float32
BF16 = mybir.dt.bfloat16
FP16 = mybir.dt.float16
I32 = mybir.dt.int32
U32 = mybir.dt.uint32
F32R = mybir.dt.float32r
ALU = mybir.AluOpType
ACT = mybir.ActivationFunctionType
AX = mybir.AxisListType.X

N = 625
D = 512
P = 128
KC = D // P
NC = 5
NP = N // NC
EDGES = 20000
ET = EDGES // NP
GT = 4
EG = ET // GT
EX = 8
FF = 2048
FC = FF // P
TT = 64
MAXT = (N + EX * (TT - 1)) // TT
KT = -(-N // TT)
F1 = 128
HD = 64
PAIRS = D // (2 * HD)
ASCALE = HD ** -0.5
HALF = [(0, 312), (312, 313)]
EVEN = [(0, 312), (312, 314)]
WIDE = [(0, 512), (512, 113)]
WMIN = 64
NO_EDGE = 1.0e30
EPS = 1e-5

COLS = {}
_n = 0
for _name, _w in [("mix_bq", 4), ("ln1_g", 4), ("ln1_b", 4), ("ffn_bq", 4), ("ffn_bk", 4)] + [
        (f"{v}{l}", w) for l in range(2) for v, w in
        [("bq", 4), ("bo", 4), ("b1", 1), ("b2", 4), ("g1", 4), ("beta1", 4), ("g2", 4), ("beta2", 4)]] + [
        ("moe_b1", EX * FC), ("l1_b1", EX)]:
    COLS[_name] = (_n, _w)
    _n += _w
NCOL = _n
ROWS = {n: i for i, n in enumerate(
    ["mix_bk", "mix_bv", "mix_bp", "ffn_bv", "ffn_bo", "ln1_g", "ln1_b", "ln_g", "ln_b", "proj_b"])}
RING = [("gnnW", "hp"), ("mixWq", "mq"), ("mixWk", "mk"), ("mixWv", "mv"), ("mixWp", "mp"), ("ffnWo", "ao"),
        ("gnnWo0", "wo0"), ("m1k", "nk"), ("m1q", "nq"), ("gnnWo1", "wo1"), ("m1v", "nv"), ("m1p", "np")]

STAGES = [
    ("xnT0", 5, "a"), ("hp", 5, "a"), ("WT", 10, "av"), ("agg", 5, "v"),
    ("mq", 8, "v"), ("mk", 5, "v"), ("mv", 5, "v"), ("mkv", 4, "v"), ("mo", 10, "v"), ("moT", 5, "a"),
    ("mp", 5, "v"), ("yT", 5, "a"), ("ao", 5, "v"), ("tT", 5, "a"), ("gate0", 1, "v"), ("rank", 1, "v"),
    ("xnT1", 5, "a"),
    ("wo0", 8, "v"), ("nk", 5, "a"), ("ffa0", 2, "a"), ("ffb0", 8, "v"), ("nq", 8, "a"),
    ("wo1", 8, "v"), ("nv", 5, "a"), ("ffa1", 2, "a"), ("ffb1", 8, "v"), ("nkv", 4, "v"), ("gN", 5, "a"),
    ("no", 10, "v"), ("noT", 5, "a"),
    ("np", 5, "v"), ("zT", 5, "a"), ("gate1", 1, "v"), ("h1a", 4, "v"), ("pb", 4, "a"), ("h1b", 12, "v"),
    ("o1", 5, "v"),
]
UNIT = []
FIRST = {}
COUNT = {s: k for s, k, _ in STAGES}
for _s, _k, _e in STAGES:
    FIRST[_s] = len(UNIT)
    UNIT += [_e[i % len(_e)] for i in range(_k)]


def freed_count(engine, unit):
    return sum(e == engine for e in UNIT[:unit + 1])


def build(nc, ins, out):
    ctx = ExitStack()
    with ctx:
        def sem(name):
            return ctx.enter_context(nc.semaphore(name))

        def sb(name, shape, dt=F32):
            return ctx.enter_context(nc.sbuf_tensor(name, shape, dt))

        xres = sb("xres", [NP, NC, D])
        cnt_adj = sb("cnt_adj", [NP, NC, N])
        ident = sb("ident", [P, P])
        cols = sb("cols", [P, NCOL])
        rows = sb("rows", [NP, len(ROWS), D])
        gate_b = sb("gate_b", [NP, EX])
        onesf = sb("onesf", [P, P])
        upper = sb("upper", [NP, NP])
        twos = sb("twos", [EX, NP])
        b2rows = sb("b2rows", [EX, D])
        gateW = sb("gateW", [P, KC * EX + WMIN])
        gateW1 = sb("gateW1", [P, KC * EX + WMIN])
        ffW1 = sb("ffW1", [P, KC, F1])
        ffW2 = sb("ffW2", [P, D])
        small = sb("small", [P, 688])
        idx = sb("idx", [NP, NC], U32)
        bounds = sb("bounds", [1, 2, EX], I32)
        tiles = sb("tiles", [1, 3, EX], I32)
        AR = 8192 + 30901
        with nc.sbuf_tensor("one_dst", [NP, GT, 3, P], F32R) as one_dst_r, \
                nc.sbuf_tensor("one_src", [NP, GT, N + 1], F32R) as one_src_r:
            pass
        arena = sb("arena", [P, AR])

        def at(off, p, *dims):
            n = 1
            for d in dims:
                n *= d
            v = arena[0:p, off:off + n]
            if len(dims) == 2:
                return v.rearrange("p (a b) -> p a b", b=dims[1])
            if len(dims) == 3:
                return v.rearrange("p (a b c) -> p a b c", b=dims[1], c=dims[2])
            return v

        o_ring = 8192
        o_T = o_ring + 2 * KC * D
        o_N = o_T + 3 * KC * N
        o_A = o_N + 3 * NC * D
        o_M = o_A + 8500
        ring = [at(o_ring + i * KC * D, P, KC, D) for i in range(2)]
        T1, T2, T3 = [at(o_T + i * KC * N, P, KC, N) for i in range(3)]
        N1, N2, N3 = [at(o_N + i * NC * D, NP, NC, D) for i in range(3)]
        maskb = at(o_M, NP, NC, N)
        assert o_M + NC * N <= AR
        Wrows = maskb
        WT = at(o_T + KC * N, NP, NC, N)
        oa = [o_A]

        def take(p, *dims, dt=F32):
            n = 1
            for d in dims:
                n *= d
            w = n if dt in (F32, I32) else (n + 1) // 2
            v = arena[0:p, oa[0]:oa[0] + w]
            oa[0] += w
            assert oa[0] <= o_M
            if dt != F32:
                v = v.bitcast(dt)[:, 0:n]
            if len(dims) == 2:
                return v.rearrange("p (a b) -> p a b", b=dims[1])
            if len(dims) == 3:
                return v.rearrange("p (a b c) -> p a b c", b=dims[1], c=dims[2])
            return v

        srci, dsti = take(NP, ET, dt=I32), take(NP, ET, dt=I32)
        wgt = take(NP, ET)
        srcf, dstf, dstr = take(NP, ET), take(NP, ET), take(NP, NC, ET)
        wpart = take(NP, 2, ET)
        ind, ind2 = take(NP, NC, ET), take(NP, NC, ET)
        iota_src, iota_dst = take(NP, N + 1, dt=FP16), take(NP, NP + 1, dt=BF16)
        zero_bf = take(NP, P, dt=BF16)
        zero_rows_sb = take(TT, D)
        iota_g = take(1, 2, EG)
        g_cnt, g_a, g_b = [take(1, NC, EG) for i in range(3)]
        g_lo, g_hi, g_n = [take(1, NC) for i in range(3)]
        oa[0] = o_A
        aw = take(P, 3, KC, P)
        qt, kt = take(P, N), take(P, N)
        vv = take(NP, NC, P)
        Pr = take(NP, 2, N)
        diag = take(NP, 4, NP)
        inv_rows = take(P, NP)
        PT = take(NP, 2 * NC, 2 * NP)
        oa[0] = o_A
        fm = take(P, 4, D)
        bd = take(P, KC, 132)
        mz = take(NP, 2, 8)
        Q2 = at(o_N + NC * D, P, KC, N)
        N4 = at(o_M, NP, NC, D)
        hid = at(o_A, P, N)
        GN = at(o_A + 3000, NP, NC, D)
        EW1 = [at(0, P, KC, FF), at(o_ring + 8192, P, KC, FF)]
        EW2 = [at(o_ring, P, FC, D), at(o_ring + 16384, P, FC, D)]
        o_E = o_ring + 3 * 8192
        xs = at(o_E, TT, D)
        xsT = at(o_E + 1024, P, KC, TT)
        hT = at(o_E + 1280, P, FC, TT)
        hs = at(o_E + 2304, P, FF // 2)
        ys = at(o_E + 3328, P, D // 2)
        eb2 = [at(o_E + 3584 + i * D // 2, P, D // 2) for i in range(2)]
        assert o_E + 3584 + D <= AR
        yg = at(o_N, NP, NC, D)
        l1W1 = at(0, P, KC, EX * F1)
        l1W2 = at(4096, P, EX, D)
        oa[0] = o_A
        pbl = take(NP, 2, NC, P)
        PB = take(P, 2, N)
        hb = take(P, 4, 320)
        h1T = at(o_T + KC * N, P, EX, N)

        psum = ctx.enter_context(nc.psum_tensor("psum", [P, 8 * 512], F32))

        def bank(b, p, w, off=0):
            return psum[0:p, 512 * b + off:512 * b + off + w]

        xs_dram = nc.dram_tensor("token_rows", [(MAXT + 2) * TT, D], F32, kind="Internal").ap()
        ys_dram = nc.dram_tensor("expert_rows", [MAXT * TT, D], F32, kind="Internal").ap()

        unit_full, freed_a, freed_v = sem("unit_full"), sem("freed_a"), sem("freed_v")
        ld_edges, ld_x, ld_const = sem("ld_edges"), sem("ld_x"), sem("ld_const")
        ld_ring = [sem(f"ld_ring{i}") for i in range(2)]
        ld_ff = sem("ld_ff")
        consts = sem("consts")
        dve, actc = sem("dve"), sem("actc")
        ln_var, ln_sd, ln_out = sem("ln_var"), sem("ln_sd"), sem("ln_out")
        bn_var, bn_sd, bn_out = sem("bn_var"), sem("bn_sd"), sem("bn_out")
        range_full, range_ready, chunk_ind = sem("range_full"), sem("range_ready"), sem("chunk_ind")
        hot_ready = [sem(f"hot_ready{c}") for c in range(NC)]
        hot_free = [sem(f"hot_free{c}") for c in range(NC)]
        hot_plain = [sem(f"hot_plain{c}") for c in range(NC)]
        hot_scaled = [sem(f"hot_scaled{c}") for c in range(NC)]
        adj_full, adj_out = sem("adj_full"), sem("adj_out")
        fm_min, fm_exp = sem("fm_min"), sem("fm_exp")
        bd_zero = sem("bd_zero")
        token_rows, x_biased = sem("token_rows"), sem("x_biased")
        mask_ready, nbq_ready = sem("mask_ready"), sem("nbq_ready")
        A = []
        for a in range(3):
            A.append({n: sem(f"att{a}_{n}") for n in (
                "wqk", "wv", "q", "k", "v", "qc", "kc", "vc", "score", "max", "exp", "sum", "prob", "pT", "pTc",
                "bc", "bcc", "av", "ctx")})
        gates_ready, slots_ready, scattered, zero_rows = (
            sem("gates_ready"), sem("slots_ready"), sem("scattered"), sem("zero_rows"))
        gathered = [sem(f"gathered{c}") for c in range(NC)]
        M = {n: sem(f"moe_{n}") for n in (
            "first0", "first1", "second0", "second1", "xs", "xsT", "xsTv", "h", "hs", "hT", "ha", "y", "yv",
            "st", "done")}
        p_top, pb_l = sem("p_top"), sem("pb_l")
        gl_in, gl_out = sem("gl_in"), sem("gl_out")
        h_in, h_g = sem("h_in"), sem("h_g")
        l1w, b2w = sem("l1w"), sem("b2w")
        x_done, stored = sem("x_done"), sem("stored")

        def full(eng, stage, i):
            eng.wait_ge(unit_full, FIRST[stage] + i % COUNT[stage] + 1)

        def stage_out(eng, stage, upto=None):
            last = FIRST[stage] + (COUNT[stage] if upto is None else upto) - 1
            for e, s in (("a", freed_a), ("v", freed_v)):
                if e in UNIT[FIRST[stage]:last + 1]:
                    eng.wait_ge(s, freed_count(e, last))

        def unit_bank(stage, i):
            return (FIRST[stage] + i) % 8

        def out_sem(stage, i):
            return freed_a if UNIT[FIRST[stage] + i] == "a" else freed_v

        nbq = small[:, 600:600 + 3 * KC]
        block = ctx.enter_context(nc.Block())
        col = lambda name, i=0: cols[:, COLS[name][0] + i:COLS[name][0] + i + 1]
        row = lambda name: rows[:, ROWS[name], :]

        @block.sync
        def _(sp):
            sp.dma_start(srci, ins["src"]).then_inc(ld_edges, 16)
            sp.dma_start(dsti, ins["dst"]).then_inc(ld_edges, 16)
            sp.dma_start(wgt, ins["edge_w"]).then_inc(ld_edges, 16)
            sp.dma_start(xres[:], ins["x"]).then_inc(ld_x, 16)
            sp.dma_start(ring[0], ins["gnnW"]).then_inc(ld_ring[0], 16)
            sp.dma_start(ring[1], ins["mixWq"]).then_inc(ld_ring[1], 16)
            sp.dma_start(cols[:], ins["cols"]).then_inc(ld_const, 16)
            sp.dma_start(rows[:], ins["rows"].partition_broadcast(NP)).then_inc(ld_const, 16)
            sp.dma_start(gate_b[:], ins["gate_b"].partition_broadcast(NP)).then_inc(ld_const, 16)
            sp.dma_start(b2rows[:], ins["l1_b2"]).then_inc(ld_const, 16)
            sp.dma_start(gateW[:, 0:KC * EX], ins["gateW"]).then_inc(ld_const, 16)
            sp.dma_start(gateW1[:, 0:KC * EX], ins["gateW1"]).then_inc(ld_const, 16)
            def ring_load(n):
                full(sp, RING[n - 2][1], -1)
                sp.dma_start(ring[n % 2], ins[RING[n][0]]).then_inc(ld_ring[n % 2], 16)

            def attention_loads(a, name, between=lambda: None):
                s = A[a]

                def load(i):
                    sp.dma_start(aw[:, 0:2], ins[name][i][:, 0:2]).then_inc(s["wqk"], 16)
                    sp.dma_start(aw[:, 2:3], ins[name][i][:, 2:3]).then_inc(s["wv"], 16)

                load(0)
                between()
                with sp.Fori(0, PAIRS - 1) as i:
                    sp.wait_ge(s["k"], i + 1)
                    sp.wait_ge(s["v"], i + 1)
                    load(i + 1)

            sp.wait_ge(adj_full, NC)
            sp.dma_start(EW1[0], ins["moeW1"][0]).then_inc(M["first0"], 16)
            for n in range(2, 6):
                ring_load(n)
            stage_out(sp, "yT")
            sp.wait_ge(zero_rows, 16 * (2 * MAXT + 1))
            sp.wait_ge(M["st"], 16)
            attention_loads(0, "att0")

            def first_weights(buf, expert):
                sp.dma_start(EW1[buf], ins["moeW1"][expert]).then_inc(M[f"first{buf}"], 16)

            def second_weights(buf, expert):
                sp.dma_start(EW2[buf], ins["moeW2"][expert]).then_inc(M[f"second{buf}"], 16)
                for q in range(2):
                    sp.dma_start(eb2[buf][q * TT:(q + 1) * TT, :],
                                 ins["moe_b2"][expert, q * (D // 2):(q + 1) * (D // 2)].partition_broadcast(TT)
                                 ).then_inc(M[f"second{buf}"], 16)

            full(sp, "ao", -1)
            second_weights(0, 0)
            full(sp, "gate0", -1)
            first_weights(1, 1)
            sp.wait_ge(scattered, 16 * NC)
            sp.wait_ge(M["xs"], 16)
            second_weights(1, 1)
            with sp.Fori(0, EX // 2 - 1) as i:
                for buf in range(2):
                    end = sp.value_load(tiles[0:1, 1, bass.ds(i * 2 + (buf + 1), 1)], min_val=1, max_val=MAXT)
                    sp.wait_ge(M["h"], end * 2)
                    first_weights(buf, i * 2 + (buf + 2))
                    sp.wait_ge(M["yv"], end + 1)
                    second_weights(buf, i * 2 + (buf + 2))
            for c in range(NC):
                sp.wait_ge(gathered[c], 16)

            def ff_loads(l):
                sp.dma_start(ffW1[:], ins[f"ffW1_{l}"]).then_inc(ld_ff, 16)
                sp.dma_start(ffW2[:], ins[f"ffW2_{l}"]).then_inc(ld_ff, 16)

            def later_loads():
                for n in range(6, 8):
                    ring_load(n)
                ff_loads(0)
                sp.dma_start(l1W1, ins["l1W1"]).then_inc(l1w, 16)
                sp.dma_start(l1W2, ins["l1W2"]).then_inc(l1w, 16)

            attention_loads(1, "att1", later_loads)
            ring_load(8)
            ring_load(9)
            ring_load(10)
            full(sp, "ffb0", -1)
            ff_loads(1)
            stage_out(sp, "ffa0")
            stage_out(sp, "ffb0")
            attention_loads(2, "att2")
            for n in range(11, 12):
                ring_load(n)
            sp.wait_ge(x_done, NC)
            sp.dma_start(out, xres[:]).then_inc(stored, 16)
            sp.wait_ge(stored, 16)

        @block.gpsimd
        def _(pool):
            pool.iota(iota_src[:, :], [[1, N + 1]], base=0, channel_multiplier=0,
                      allow_small_or_imprecise_dtypes=True).then_inc(consts, 1)
            pool.iota(iota_dst[:, 0:NP], [[1, NP]], base=0, channel_multiplier=0,
                      allow_small_or_imprecise_dtypes=True).then_inc(consts, 1)
            pool.iota(iota_g[:, 0, :], [[1, EG]], base=1, channel_multiplier=0,
                      allow_small_or_imprecise_dtypes=True).then_inc(consts, 1)
            pool.iota(iota_g[:, 1, :], [[-1, EG]], base=EG, channel_multiplier=0,
                      allow_small_or_imprecise_dtypes=True).then_inc(consts, 1)
            pool.memset(onesf[:], 1.0).then_inc(consts, 1)
            pool.memset(zero_bf, 0.0).then_inc(consts, 1)
            pool.memset(twos[:], 2.0).then_inc(consts, 1)
            pool.memset(ident[:], 0.0).then_inc(consts, 1)
            pool.memset(zero_rows_sb, 0.0).then_inc(consts, 1)
            pool.memset(gateW[:, KC * EX:], 0.0).then_inc(consts, 1)
            pool.memset(gateW1[:, KC * EX:], 0.0).then_inc(consts, 1)
            pool.wait_ge(consts, 11)
            pool.affine_select(out=ident[:], in_=ident[:], compare_op=ALU.not_equal, fill=1.0, base=0,
                               pattern=[[-1, P]], channel_multiplier=1).then_inc(consts, 1)
            pool.affine_select(out=upper[:], in_=onesf[0:NP, 0:NP], compare_op=ALU.is_gt, fill=0.0, base=0,
                               pattern=[[1, NP]], channel_multiplier=-1).then_inc(consts, 1)
            for t in range(MAXT + 2):
                pool.dma_start(xs_dram[t * TT:(t + 1) * TT, :], zero_rows_sb).then_inc(
                    zero_rows if t <= MAXT else M["st"], 16)
                if t < MAXT:
                    pool.dma_start(ys_dram[t * TT:(t + 1) * TT, :], zero_rows_sb).then_inc(zero_rows, 16)
            pool.wait_ge(adj_out, 4 * NC)
            pool.memset(bd[:, :, :], 0.0).then_inc(bd_zero, 1)
            pool.wait_ge(ld_const, 16 * 6)
            for c in range(NC):
                full(pool, "tT", c)
                pool.tensor_tensor(N3[:, c, :], N3[:, c, :], row("ln1_g"), ALU.mult).then_inc(token_rows, 1)
            for c in range(NC):
                pool.wait_ge(token_rows, c + 1)
                pool.tensor_tensor(N3[:, c, :], N3[:, c, :], row("ln1_b"), ALU.add).then_inc(token_rows, 1)
            pool.wait_ge(token_rows, 2 * NC)
            pool.wait_ge(zero_rows, 16 * (2 * MAXT + 1))
            pool.wait_ge(M["st"], 16)
            pool.wait_ge(slots_ready, 1)
            for c in range(NC):
                pool.indirect_dma_start(
                    out=xs_dram, out_offset=bass.IndirectOffsetOnAxis(ap=idx[:, c:c + 1], axis=0),
                    in_=N3[:, c, :], in_offset=None).then_inc(scattered, 16)
            pool.wait_ge(scattered, 16 * NC)
            pool.dma_start(xs, xs_dram[0:TT, :]).then_inc(M["xs"], 16)
            pool.wait_ge(M["xsT"], 1)
            pool.dma_start(xs, xs_dram[TT:2 * TT, :]).then_inc(M["xs"], 16)
            total_tiles = pool.value_load(tiles[0:1, 2, 0:1], min_val=EX, max_val=MAXT)
            with pool.Fori(0, total_tiles) as g:
                pool.wait_ge(M["xsT"], g + 2)
                pool.dma_start(xs, xs_dram[bass.ds((g + 2) * TT, TT), :]).then_inc(M["xs"], 16)
                pool.wait_ge(M["yv"], g + 2)
                for q in range(2):
                    pool.dma_start(ys_dram[bass.ds(g * TT, TT), q * (D // 2):(q + 1) * (D // 2)],
                                   ys[q * TT:(q + 1) * TT, :]).then_inc(M["st"], 16)
            pool.wait_ge(M["st"], total_tiles * 32 + 16)
            pool.wait_ge(M["xs"], total_tiles * 16 + 32)
            pool.wait_ge(M["yv"], total_tiles + 1)
            pool.nop().then_inc(M["done"], 1)
            for c in range(NC):
                pool.indirect_dma_start(
                    out=yg[:, c, :], out_offset=None, in_=ys_dram,
                    in_offset=bass.IndirectOffsetOnAxis(ap=idx[:, c:c + 1], axis=0)).then_inc(gathered[c], 16)
            pool.wait_ge(ln_out, 4 * NC)
            for n, name in enumerate(["ln_b", "proj_b"]):
                for c in range(NC):
                    if n:
                        pool.wait_ge(x_biased, c + 1)
                    pool.tensor_tensor(xres[:, c, :], xres[:, c, :], row(name), ALU.add).then_inc(x_biased, 1)
            stage_out(pool, "ffb1")
            pool.memset(bd[:, :, :], 0.0).then_inc(bd_zero, 1)

        @block.tensor
        def _(pe):
            def take_bank(stage, i):
                n = FIRST[stage] + i
                if n >= 8:
                    e = UNIT[n - 8]
                    pe.wait_ge(freed_a if e == "a" else freed_v, freed_count(e, n - 8))
                return n % 8

            def rows_to_cols(stage, src, ready):
                for c in range(NC):
                    ready(c)
                    b = take_bank(stage, c)
                    for k in range(KC):
                        mm = pe.transpose(bank(b, P, NP, NP * k), src[:, c, k * P:(k + 1) * P], ident[0:NP, 0:NP])
                    mm.then_inc(unit_full, 1)

            def ring_ready(n):
                pe.wait_ge(ld_ring[n % 2], 16 * (n // 2 + 1))

            def product_rows(stage, srcT, n):
                ring_ready(n)
                for c in range(NC):
                    b = take_bank(stage, c)
                    for k in range(KC):
                        mm = pe.matmul(bank(b, NP, D), srcT[:, k, c * NP:(c + 1) * NP], ring[n % 2][:, k, :],
                                       start=(k == 0), stop=(k == KC - 1))
                    mm.then_inc(unit_full, 1)

            def product_cols(stage, srcT, n):
                ring_ready(n)
                for m in range(KC):
                    for h, (o, w) in enumerate(HALF):
                        b = take_bank(stage, 2 * m + h)
                        for k in range(KC):
                            mm = pe.matmul(bank(b, P, w), ring[n % 2][:, k, m * P:(m + 1) * P],
                                           srcT[:, k, o:o + w], start=(k == 0), stop=(k == KC - 1))
                        mm.then_inc(unit_full, 1)

            pe.wait_ge(consts, 13)
            pe.wait_ge(chunk_ind, 1)
            for h in range(2):
                pe.matmul(bank(h, 1, 400), onesf[0:NP, 0:1],
                          ind2.rearrange("p c t -> p (c t)")[:, 400 * h:400 * h + 400],
                          start=True, stop=True).then_inc(range_full, 1)
            pe.wait_ge(range_ready, 1)
            for c in range(NC):
                k = pe.value_load(bounds[0:1, 1, c:c + 1], min_val=1, max_val=EG)
                b0 = 4 * (c % 2)
                if c >= 2:
                    pe.wait_ge(adj_out, 4 * (c - 1))
                for q in range(4):
                    w = EVEN[q % 2][1]
                    mm = pe.matmul(bank(b0 + q, NP, w), zero_bf[:, 0:NP], iota_src[:, 0:w],
                                   start=True, stop=False, skip_group_check=True)
                    mm.then_inc(hot_free[c], 1)
                with pe.Fori(0, k) as j:
                    for s in range(GT):
                        pe.wait_ge(hot_ready[c], j * GT + s + 1)
                        pe.wait_ge(hot_scaled[c], j * GT + s + 1)
                        for v in range(3):
                            for h, (o, w) in enumerate(EVEN):
                                mm = pe.matmul(bank(b0 + (2 if v == 2 else 0) + h, NP, w), one_dst_r[:, s, v, 0:NP],
                                               one_src_r[:, s, o:o + w], start=False, stop=False,
                                               skip_group_check=True)
                        mm.then_inc(hot_free[c], 1)
                for q in range(4):
                    w = EVEN[q % 2][1]
                    mm = pe.matmul(bank(b0 + q, NP, w), zero_bf[:, 0:NP], iota_src[:, 0:w],
                                   start=False, stop=True, skip_group_check=True)
                mm.then_inc(adj_full, 1)
            pe.wait_ge(adj_out, 4 * NC)
            rows_to_cols("xnT0", N1, lambda c: pe.wait_ge(ln_out, c + 1))
            stage_out(pe, "xnT0")
            product_rows("hp", T1, 0)
            for s in range(NC):
                for h in range(2):
                    b = take_bank("WT", 2 * s + h)
                    for c in (range(4) if h == 0 else [4]):
                        mm = pe.transpose(bank(b, NP, NP, NP * (c % 4)), Wrows[:, c, s * NP:(s + 1) * NP],
                                          ident[0:NP, 0:NP])
                    mm.then_inc(unit_full, 1)
            stage_out(pe, "WT")
            for c in range(NC):
                b = take_bank("agg", c)
                for s in range(NC):
                    mm = pe.matmul(bank(b, NP, D), WT[:, s, c * NP:(c + 1) * NP], N2[:, s, :],
                                   start=(s == 0), stop=(s == NC - 1))
                mm.then_inc(unit_full, 1)

            product_cols("mq", T1, 1)
            product_rows("mk", T1, 2)
            product_rows("mv", T1, 3)

            def key_values(stage, kr, vr):
                for m in range(KC):
                    b = take_bank(stage, m)
                    for c in range(NC):
                        pe.matmul(bank(b, P, P), kr[:, c, m * P:(m + 1) * P], vr[:, c, m * P:(m + 1) * P],
                                  start=(c == 0), stop=(c == NC - 1))
                    for c in range(NC):
                        mm = pe.matmul(bank(b, P, WMIN, P), kr[:, c, m * P:(m + 1) * P], onesf[0:NP, 0:WMIN],
                                       start=(c == 0), stop=(c == NC - 1))
                    mm.then_inc(unit_full, 1)

            def query_products(stage, qT, w):
                for c in range(NC):
                    for h in range(2):
                        b = take_bank(stage, 2 * c + h)
                        for m in (2 * h, 2 * h + 1):
                            mm = pe.matmul(bank(b, NP, w, w * (m % 2)), qT[:, m, c * NP:(c + 1) * NP],
                                           bd[:, m, 0:w], start=True, stop=True)
                        mm.then_inc(unit_full, 1)

            stage_out(pe, "mk")
            stage_out(pe, "mv")
            key_values("mkv", N1, N3)
            stage_out(pe, "mq")
            stage_out(pe, "mkv")
            query_products("mo", T2, 130)
            rows_to_cols("moT", N2, lambda c: stage_out(pe, "mo", 2 * c + 2))
            stage_out(pe, "moT")
            product_rows("mp", T3, 4)
            rows_to_cols("yT", N1, lambda c: pe.wait_ge(ln_out, NC + c + 1))
            stage_out(pe, "yT")

            def attention(a, srcT):
                s = A[a]
                pe.nop().then_inc(s["ctx"], 1)

                def projection(w, i):
                    for h, (o, n) in enumerate(WIDE):
                        for k in range(KC):
                            mm = pe.matmul(bank(2 * w + h, P, n), aw[:, w, k, :], srcT[:, k, o:o + n],
                                           start=(k == 0), stop=(k == KC - 1))
                    mm.then_inc(s["qk"[w]], 1)

                def scores(i, t):
                    c, hh = divmod(t, 2)
                    if t < 2:
                        pe.wait_ge(s["qc"], i + 1)
                        pe.wait_ge(s["kc"], i + 1)
                    else:
                        pe.wait_ge(s["exp"], i * 10 + t - 1)
                    for h, (o, n) in enumerate(WIDE):
                        mm = pe.matmul(bank(2 * (t % 2) + h, NP, n), qt[hh * HD:(hh + 1) * HD, c * NP:(c + 1) * NP],
                                       kt[hh * HD:(hh + 1) * HD, o:o + n], start=True, stop=True)
                    mm.then_inc(s["score"], 1)

                def values(i):
                    pe.wait_ge(s["wv"], i * 16 + 16)
                    for c in range(NC):
                        for k in range(KC):
                            mm = pe.matmul(bank(4, NP, P, P * c), srcT[:, k, c * NP:(c + 1) * NP], aw[:, 2, k, :],
                                           start=(k == 0), stop=(k == KC - 1))
                    mm.then_inc(s["v"], 1)

                def turned(i, t):
                    c, hh = divmod(t, 2)
                    if a:
                        pe.wait_ge(s["sum"], i * 20 + 2 * t + 1)
                    else:
                        pe.wait_ge(s["exp"], i * 10 + t + 1)
                    if t == 0:
                        pe.wait_ge(s["vc"], i + 1)
                    elif hh == 0:
                        pe.wait_ge(s["pTc"], i * 15 + 3 * c)
                    if hh or t == 0:
                        pe.wait_ge(s["bcc"], i * 5 + c + 1)
                    for j in range(NC):
                        b, o = (4 + hh, NP * j) if j < 4 else (6, NP * hh)
                        mm = pe.transpose(bank(b, NP, NP, o), Pr[:, t % 2, j * NP:(j + 1) * NP], ident[0:NP, 0:NP])
                    mm.then_inc(s["pT"], 1)

                def context(i, c):
                    pe.wait_ge(s["pTc"], i * 15 + 3 * c + 3)
                    pe.wait_ge(s["prob"], i * 10 + 2 * c + 2)
                    for hh in range(2):
                        mm = pe.matmul(psum[hh * HD:(hh + 1) * HD, 6 * 512 + 256:6 * 512 + 256 + NP],
                                       onesf[0:NP, 0:HD], diag[:, (2 * c + hh) % 4, :], start=True, stop=True)
                    mm.then_inc(s["bc"], 1)
                    pe.wait_ge(s["ctx"], i * 5 + c + 1)
                    for j in range(NC):
                        for hh in range(2):
                            mm = pe.matmul(psum[hh * HD:(hh + 1) * HD, 7 * 512:7 * 512 + NP],
                                           vv[:, j, hh * HD:(hh + 1) * HD],
                                           PT[:, c % 2 * NC + j, hh * NP:(hh + 1) * NP],
                                           start=(j == 0), stop=(j == NC - 1))
                    mm.then_inc(s["av"], 1)

                def pair(i, last):
                    for t in range(10):
                        scores(i, t)
                        if t == 1:
                            values(i)
                        if t >= 2:
                            turned(i, t - 2)
                        if t >= 4 and t % 2 == 0:
                            context(i, t // 2 - 2)
                    if not last:
                        pe.wait_ge(s["wqk"], i * 16 + 32)
                        pe.wait_ge(s["exp"], i * 10 + 9)
                        projection(0, i + 1)
                    turned(i, 8)
                    context(i, 3)
                    turned(i, 9)
                    if not last:
                        pe.wait_ge(s["exp"], i * 10 + 10)
                        projection(1, i + 1)
                    context(i, 4)

                pe.wait_ge(s["wqk"], 16)
                projection(0, 0)
                projection(1, 0)
                with pe.Fori(0, PAIRS - 1) as i:
                    pair(i, False)
                pair(PAIRS - 1, True)
                pe.wait_ge(s["ctx"], 5 * PAIRS + 1)

            attention(0, T1)
            product_rows("ao", T2, 5)
            rows_to_cols("tT", N3, lambda c: pe.wait_ge(ln_out, 2 * NC + c + 1))
            stage_out(pe, "tT")

            def gates(stage, srcT, W):
                b = take_bank(stage, 0)
                for c in range(NC):
                    for k in range(KC):
                        mm = pe.matmul(bank(b, NP, WMIN, WMIN * c), srcT[:, k, c * NP:(c + 1) * NP],
                                       W[:, k * EX:k * EX + WMIN], start=(k == 0), stop=(k == KC - 1))
                mm.then_inc(unit_full, 1)

            pe.wait_ge(ld_const, 16 * 6)
            gates("gate0", T3, gateW)
            pe.wait_ge(gates_ready, 1)
            b = take_bank("rank", 0)
            onehot = small[0:NP, 640:688]
            pe.matmul(bank(b, NP, EX * (NC + 1)), upper[:], onehot, start=True, stop=False, skip_group_check=True)
            for d in range(1, NC + 1):
                mm = pe.matmul(bank(b, NP, EX * (NC + 1 - d), EX * d), onesf[0:NP, 0:NP],
                               onehot[:, 0:EX * (NC + 1 - d)], start=False, stop=(d == NC), skip_group_check=True)
            mm.then_inc(unit_full, 1)

            pe.wait_ge(slots_ready, 1)
            pe.nop().then_inc(M["y"], 1)

            def tile_columns(n):
                pe.wait_ge(M["xs"], n * 16 + 16)
                pe.matmul(bank(5, P, TT), xs[:, 0:P], ident[0:TT, 0:TT], start=True, stop=True)
                for k4 in range(1, KC):
                    mm = pe.transpose(bank(5, P, TT, TT * k4), xs[:, k4 * P:(k4 + 1) * P], ident[0:TT, 0:TT])
                mm.then_inc(M["xsT"], 1)

            tile_columns(0)
            with pe.Fori(0, EX // 2) as i:
                for par in range(2):
                    k = pe.value_load(tiles[0:1, 0, bass.ds(i * 2 + par, 1)], min_val=1, max_val=KT)
                    b0 = pe.value_load(tiles[0:1, 1, bass.ds(i * 2 + par, 1)], min_val=0, max_val=MAXT - 1)
                    with pe.Fori(0, k) as j:
                        g = b0 + j
                        pe.wait_ge(M[f"first{par}"], i * 16 + 16)
                        pe.wait_ge(M["xsTv"], g + 1)
                        for b in range(2):
                            for k4 in range(KC):
                                for q in range(2):
                                    o = q * (FF // 2) + b * D
                                    mm = pe.matmul(psum[q * TT:(q + 1) * TT, 512 * b:512 * b + D], xsT[:, k4, :],
                                                   EW1[par][:, k4, o:o + D], start=(k4 == 0), stop=(k4 == KC - 1))
                            mm.then_inc(M["h"], 1)
                        for b in range(2):
                            pe.wait_ge(M["hs"], g * 2 + b + 1)
                            for j4 in range(4):
                                mm = pe.transpose(bank(2 + b, P, P, P * j4), hs[:, b * D + j4 * P:b * D + (j4 + 1) * P],
                                                  ident[:, :])
                            mm.then_inc(M["hT"], 1)
                            if b == 0:
                                tile_columns(g + 1)
                        pe.wait_ge(M[f"second{par}"], i * 48 + 48)
                        pe.wait_ge(M["yv"], g + 1)
                        for n in range(FC):
                            b, j4, q_ = n // 8, n // 2 % 4, n % 2
                            f = q_ * (FC // 2) + b * 4 + j4
                            if q_ == 0:
                                pe.wait_ge(M["ha"], g * 8 + n // 2 + 1)
                            for q in range(2):
                                mm = pe.matmul(psum[q * TT:(q + 1) * TT, 4 * 512:4 * 512 + D // 2], hT[:, f, :],
                                               EW2[par][:, f, q * (D // 2):(q + 1) * (D // 2)],
                                               start=(n == 0), stop=(n == FC - 1))
                        mm.then_inc(M["y"], 1)

            rows_to_cols("xnT1", N2, lambda c: pe.wait_ge(ln_out, 3 * NC + c + 1))
            stage_out(pe, "xnT1")
            for l in range(2):
                attention(1 + l, T1 if l == 0 else T2)
                product_cols(f"wo{l}", T3, 6 + 3 * l)
                product_rows("nk" if l == 0 else "nv", T1, 7 + 3 * l)
                pe.wait_ge(bn_out, 8 * l + 4)
                pe.wait_ge(ld_ff, 32 * (l + 1))
                for h, (o, w) in enumerate(HALF):
                    b = take_bank(f"ffa{l}", h)
                    for k in range(KC):
                        mm = pe.matmul(bank(b, P, w), ffW1[:, k, :], T2[:, k, o:o + w], start=(k == 0), stop=(k == KC - 1))
                    mm.then_inc(unit_full, 1)
                stage_out(pe, f"ffa{l}")
                for m in range(KC):
                    for h, (o, w) in enumerate(HALF):
                        b = take_bank(f"ffb{l}", 2 * m + h)
                        mm = pe.matmul(bank(b, P, w), ffW2[:, m * P:(m + 1) * P], hid[:, o:o + w], start=True, stop=True)
                        mm.then_inc(unit_full, 1)
                if l == 0:
                    product_cols("nq", T1, 8)
                    stage_out(pe, "nq")
                else:
                    stage_out(pe, "nk")
                    stage_out(pe, "nv")
                    key_values("nkv", N1, N3)
                pe.wait_ge(bn_out, 8 * l + 8)
            for c in range(NC):
                b = take_bank("gN", c)
                for k in range(KC):
                    mm = pe.transpose(bank(b, NP, P, P * k), T2[:, k, c * NP:(c + 1) * NP], ident[:, :])
                mm.then_inc(unit_full, 1)

            stage_out(pe, "nkv")
            query_products("no", Q2, 132)
            rows_to_cols("noT", N4, lambda c: stage_out(pe, "no", 2 * c + 2))
            stage_out(pe, "noT")
            product_rows("np", T2, 11)

            rows_to_cols("zT", N1, lambda c: pe.wait_ge(ln_out, 5 * NC + c + 1))
            stage_out(pe, "zT")
            gates("gate1", T1, gateW1)
            pe.wait_ge(l1w, 32)

            def hidden(stage, first):
                for n in range(COUNT[stage]):
                    f, h = divmod(first + n, 2)
                    o, w = HALF[h]
                    b = take_bank(stage, n)
                    for k in range(KC):
                        mm = pe.matmul(bank(b, P, w), l1W1[:, k, f * P:(f + 1) * P], T1[:, k, o:o + w],
                                       start=(k == 0), stop=(k == KC - 1))
                    mm.then_inc(unit_full, 1)

            hidden("h1a", 0)
            pe.wait_ge(pb_l, 2)
            for w in range(2):
                for h in range(2):
                    b = take_bank("pb", 2 * w + h)
                    for c in (range(4) if h == 0 else [4]):
                        mm = pe.matmul(bank(b, P, NP, NP * (c % 4)), pbl[:, w, c, :], ident[0:NP, 0:NP],
                                       start=True, stop=True)
                    mm.then_inc(unit_full, 1)
            hidden("h1b", COUNT["h1a"])
            for c in range(NC):
                b = take_bank("o1", c)
                for f in range(EX):
                    if c == 0:
                        n = 2 * f + 2
                        stage_out(pe, "h1a", min(n, COUNT["h1a"])) if n <= COUNT["h1a"] else stage_out(
                            pe, "h1b", n - COUNT["h1a"])
                    pe.matmul(bank(b, NP, D), h1T[:, f, c * NP:(c + 1) * NP], l1W2[:, f, :], start=(f == 0), stop=False)
                pe.matmul(bank(b, NP, D), twos[:], b2rows[:], start=False, stop=True).then_inc(unit_full, 1)

        @block.scalar
        def _(act):
            def chunk_view(b):
                return bank(b, P, KC * NP).rearrange("p (k n) -> p k n", k=KC)

            def cols_out(stage, dst):
                for c in range(NC):
                    full(act, stage, c)
                    act.activation(dst[:, :, c * NP:(c + 1) * NP], chunk_view(unit_bank(stage, c)),
                                   ACT.Copy).then_inc(freed_a, 1)

            def rows_out(stage, dst, func=ACT.Copy):
                for c in range(NC):
                    full(act, stage, c)
                    act.activation(dst[:, c, :], bank(unit_bank(stage, c), NP, D), func).then_inc(freed_a, 1)

            def deviation(n):
                act.wait_ge(ln_var, n + 1)
                act.activation(small[0:NP, 40:45], small[0:NP, 30:35], ACT.Sqrt).then_inc(ln_sd, 1)

            deviation(0)
            act.wait_ge(range_ready, 1)
            for c in range(NC):
                first = act.value_load(bounds[0:1, 0, c:c + 1], min_val=0, max_val=EG - 1)
                k = act.value_load(bounds[0:1, 1, c:c + 1], min_val=1, max_val=EG)
                with act.Fori(0, k) as j:
                    g = nc.s_assert_within(first + j, 0, EG - 1,
                                           skip_runtime_bounds_check_because="a chunk's groups end below EG")
                    for s in range(GT):
                        act.wait_ge(hot_plain[c], j * GT + s + 1)
                        e = bass.ds(g * GT + s, 1)
                        for v in range(2):
                            done = act.activation(one_dst_r[:, s, v, 0:NP], one_dst_r[:, s, 2, 0:NP], ACT.Copy,
                                                  scale=wpart[:, v, e])
                        done.then_inc(hot_scaled[c], 1)
                act.wait_ge(adj_full, c + 1)
                b0 = 4 * (c % 2)
                for q in range(4):
                    o, w = HALF[q % 2]
                    dst = (Wrows if q < 2 else cnt_adj)[:, c, o:o + w]
                    act.activation(dst, bank(b0 + q, NP, w), ACT.Copy).then_inc(adj_out, 1)
            cols_out("xnT0", T1)
            rows_out("hp", N2)
            for s in range(NC):
                full(act, "WT", 2 * s)
                act.activation(WT[:, s, 0:4 * NP], bank(unit_bank("WT", 2 * s), NP, 4 * NP), ACT.Copy).then_inc(freed_a, 1)
            for n in range(8 + NC):
                act.wait_ge(fm_min, n + 1)
                p, w = (P, HALF[n % 2][1]) if n < 8 else (NP, D)
                act.activation(fm[0:p, 1, 0:w], fm[0:p, 0, 0:w], ACT.Exp).then_inc(fm_exp, 1)
            cols_out("moT", T3)
            deviation(1)
            cols_out("yT", T1)

            def attention(a, bk):
                s = A[a]

                def queries(i):
                    act.wait_ge(s["q"], i + 1)
                    act.activation(qt, psum[:, 0:N], ACT.Identity, bias=nbq[:, bass.ds(i + a * KC, 1)],
                                   scale=-ASCALE).then_inc(s["qc"], 1)

                def keys(i):
                    act.wait_ge(s["k"], i + 1)
                    if bk:
                        act.activation(kt, psum[:, 1024:1024 + N], ACT.Identity,
                                       bias=cols[:, bass.ds(i + COLS[bk][0], 1)]).then_inc(s["kc"], 1)
                    else:
                        act.activation(kt, psum[:, 1024:1024 + N], ACT.Copy).then_inc(s["kc"], 1)

                def exponentials(i, t):
                    act.wait_ge(s["max"], i * 10 + t + 1)
                    if t >= 2:
                        act.wait_ge(s["pT"], i * 10 + t - 1)
                    sc = psum[0:NP, 1024 * (t % 2):1024 * (t % 2) + N]
                    nmax = small[0:NP, 80 + t:81 + t]
                    act.activation(Pr[:, t % 2, :], sc, ACT.Exp, bias=nmax, scale=-1.0,
                                   accum_out=None if a else small[0:NP, 120 + t:121 + t]).then_inc(s["exp"], 1)

                def turned_out(i, t):
                    c, hh = divmod(t, 2)
                    act.wait_ge(s["pT"], i * 10 + t + 1)
                    if hh == 0:
                        if c >= 2:
                            act.wait_ge(s["av"], i * 5 + c - 1)
                        else:
                            act.wait_ge(s["ctx"], i * 5 + 1)
                    act.activation(PT[:, c % 2 * NC:c % 2 * NC + 4, hh * NP:(hh + 1) * NP],
                                   bank(4 + hh, NP, 4 * NP).rearrange("p (j n) -> p j n", j=4),
                                   ACT.Copy).then_inc(s["pTc"], 1)
                    if hh:
                        act.activation(PT[:, c % 2 * NC + 4, :], bank(6, NP, 2 * NP), ACT.Copy).then_inc(s["pTc"], 1)

                def inverses_out(i, c):
                    act.wait_ge(s["bc"], i * 5 + c + 1)
                    act.wait_ge(s["ctx"], i * 5 + c + 1)
                    act.activation(inv_rows, bank(6, P, NP, 256), ACT.Copy).then_inc(s["bcc"], 1)

                def pair(i, last):
                    for t in range(10):
                        if t >= 2:
                            turned_out(i, t - 2)
                        exponentials(i, t)
                        if t >= 4 and t % 2 == 0:
                            inverses_out(i, t // 2 - 2)
                    if not last:
                        queries(i + 1)
                    turned_out(i, 8)
                    inverses_out(i, 3)
                    turned_out(i, 9)
                    if not last:
                        keys(i + 1)
                    inverses_out(i, 4)

                act.nop().then_inc(s["bcc"], 1)
                act.activation(small[0:1, 95 + a:96 + a], onesf[0:1, 0:1], ACT.Exp)
                queries(0)
                keys(0)
                with act.Fori(0, PAIRS - 1) as i:
                    pair(i, False)
                pair(PAIRS - 1, True)

            act.wait_ge(ld_const, 16 * 6)
            act.wait_ge(nbq_ready, 3)
            attention(0, "ffn_bk")
            deviation(2)
            for c in range(NC):
                full(act, "tT", c)
                for k in range(KC):
                    i_ = act.activation(T3[:, k, c * NP:(c + 1) * NP], bank(unit_bank("tT", c), P, NP, NP * k),
                                        ACT.Identity, bias=col("ln1_b", k), scale=col("ln1_g", k))
                i_.then_inc(freed_a, 1)
            act.wait_ge(gl_in, 1)
            act.activation(small[0:NP, 240:280], small[0:NP, 160:200], ACT.Exp).then_inc(gl_out, 1)
            act.wait_ge(slots_ready, 1)

            act.activation(small[0:1, 94:95], onesf[0:1, 0:1], ACT.Gelu_apprx_tanh)
            with act.Fori(0, EX) as e:
                k = act.value_load(tiles[0:1, 0, bass.ds(e, 1)], min_val=1, max_val=KT)
                b0 = act.value_load(tiles[0:1, 1, bass.ds(e, 1)], min_val=0, max_val=MAXT - 1)
                with act.Fori(0, k) as j:
                    g = b0 + j
                    act.wait_ge(M["y"], g + 1)
                    for b in range(2):
                        act.wait_ge(M["hT"], g * 2 + b + 1)
                        for j4 in range(4):
                            for q in range(2):
                                f = q * (FC // 2) + b * 4 + j4
                                done = act.activation(hT[:, f, :], bank(2 + b, P, TT, P * j4 + TT * q),
                                                      ACT.Gelu_apprx_tanh,
                                                      bias=cols[:, bass.ds(e * FC + (COLS["moe_b1"][0] + f), 1)])
                            done.then_inc(M["ha"], 1)
            deviation(3)
            cols_out("xnT1", T1)

            def batch_deviation(n):
                act.wait_ge(bn_var, n + 1)
                act.activation(small[:, 40:44], small[:, 30:34], ACT.Sqrt).then_inc(bn_sd, 1)

            for l in range(2):
                attention(1 + l, None)
                batch_deviation(2 * l)
                if l == 0:
                    rows_out("nk", N1, ACT.Relu)
                else:
                    rows_out("nv", N3)
                for h, (o, w) in enumerate(HALF):
                    full(act, f"ffa{l}", h)
                    act.activation(hid[:, o:o + w], bank(unit_bank(f"ffa{l}", h), P, w), ACT.Relu,
                                   bias=col(f"b1{l}")).then_inc(freed_a, 1)
                batch_deviation(2 * l + 1)
                if l == 0:
                    for m in range(KC):
                        for h, (o, w) in enumerate(HALF):
                            full(act, "nq", 2 * m + h)
                            act.activation(Q2[:, m, o:o + w], bank(unit_bank("nq", 2 * m + h), P, w),
                                           ACT.Relu).then_inc(freed_a, 1)
            rows_out("gN", GN)
            cols_out("noT", T2)
            deviation(4)
            deviation(5)
            cols_out("zT", T1)
            act.wait_ge(gl_in, 2)
            act.activation(small[0:NP, 240:280], small[0:NP, 160:200], ACT.Exp).then_inc(gl_out, 1)
            for w in range(2):
                for h, (o, n) in enumerate([(0, 4 * NP), (4 * NP, NP)]):
                    full(act, "pb", 2 * w + h)
                    act.activation(PB[:, w, o:o + n], bank(unit_bank("pb", 2 * w + h), P, n), ACT.Copy).then_inc(freed_a, 1)
            for n in range(16):
                f, h = divmod(n, 2)
                w = HALF[h][1]
                for q in range(2):
                    act.wait_ge(h_in, 2 * n + q + 1)
                    act.activation(hb[:, 2 + q, 0:w], hb[:, q, 0:w], ACT.Gelu, bias=col("l1_b1", f)).then_inc(h_g, 1)

        @block.vector
        def _(ve):
            done = [0]

            def link(ins_):
                done[0] += 1
                ins_.then_inc(dve, 1)
                ve.wait_ge(dve, done[0])

            def chunk_stats(src, c):
                return ve.bn_stats(small[0:NP, 6 * c:6 * c + 6], src[:, c, :])

            def layer_norm(n, src, dst, stats=True):
                if stats:
                    for c in range(NC):
                        i_ = chunk_stats(src, c)
                    link(i_)
                for c in range(NC):
                    i_ = ve.bn_aggr(small[0:NP, 50 + 2 * c:52 + 2 * c], small[0:NP, 6 * c:6 * c + 6])
                link(i_)
                mv = small[0:NP, 50:60].rearrange("p (c t) -> p c t", t=2)
                ve.tensor_scalar(small[0:NP, 30:35], mv[:, :, 1], EPS, None, ALU.add).then_inc(ln_var, 1)
                ve.wait_ge(ln_sd, n + 1)
                link(ve.reciprocal(small[0:NP, 60:65], small[0:NP, 40:45]))
                for c in range(NC):
                    i_ = ve.tensor_scalar(dst[:, c, :], src[:, c, :], mv[:, c, 0:1], small[0:NP, 60 + c:61 + c],
                                          ALU.subtract, ALU.mult)
                    i_.then_inc(ln_out, 1)

            ve.wait_ge(ld_edges, 48)
            link(ve.tensor_copy(srcf, srci))
            link(ve.tensor_copy(dstf, dsti))
            for c in range(NC):
                link(ve.tensor_scalar(dstr[:, c, :], dstf, float(-NP * c), None, ALU.add))
            link(ve.tensor_scalar(ind, dstr, 0.0, None, ALU.is_ge))
            ve.scalar_tensor_tensor(ind2, dstr, float(NP), ind, ALU.is_lt, ALU.mult).then_inc(chunk_ind, 1)
            link(ve.tensor_scalar(wpart[:, 0].bitcast(I32), wgt.bitcast(I32), -4096, None, ALU.bitwise_and))
            link(ve.tensor_tensor(wpart[:, 1], wgt, wpart[:, 0], ALU.subtract))
            ve.wait_ge(ld_x, 16)
            layer_norm(0, xres, N1)
            ve.wait_ge(range_full, 2)
            ve.wait_ge(consts, 13)
            flat = g_cnt.rearrange("p c g -> p (c g)")
            for h in range(2):
                w = NC * EG // 2
                link(ve.tensor_reduce(flat[:, w * h:w * h + w],
                                      bank(h, 1, 400).rearrange("p (g t) -> p g t", t=GT), AX, ALU.add))
            link(ve.tensor_scalar(g_cnt, g_cnt, 0.5, None, ALU.is_gt))
            ve.tensor_tensor(g_a, g_cnt, iota_g[:, 0, :].unsqueeze(1).to_broadcast([1, NC, EG]), ALU.mult)
            link(ve.tensor_tensor(g_b, g_cnt, iota_g[:, 1, :].unsqueeze(1).to_broadcast([1, NC, EG]), ALU.mult))
            ve.tensor_reduce(g_hi, g_a, AX, ALU.max)
            link(ve.tensor_reduce(g_lo, g_b, AX, ALU.max))
            link(ve.tensor_scalar(g_n, g_lo, -1.0, float(EG), ALU.mult, ALU.add))
            link(ve.tensor_scalar(g_lo, g_n, float(EG - 1), None, ALU.min))
            link(ve.tensor_tensor(g_n, g_hi, g_lo, ALU.subtract))
            link(ve.tensor_scalar(g_hi, g_n, 1.0, None, ALU.max))
            link(ve.tensor_copy(bounds[:, 0, 0:NC], g_lo))
            ve.tensor_copy(bounds[:, 1, 0:NC], g_hi).then_inc(range_ready, 1)
            ve.wait_ge(range_ready, 1)
            for c in range(NC):
                first = ve.value_load(bounds[0:1, 0, c:c + 1], min_val=0, max_val=EG - 1)
                k = ve.value_load(bounds[0:1, 1, c:c + 1], min_val=1, max_val=EG)
                with ve.Fori(0, k) as j:
                    g = nc.s_assert_within(first + j, 0, EG - 1,
                                           skip_runtime_bounds_check_because="a chunk's groups end below EG")
                    for s in range(GT):
                        ve.wait_ge(hot_free[c], j * GT + s + 1)
                        e = bass.ds(g * GT + s, 1)
                        ve.tensor_scalar(one_dst_r[:, s, 2, 0:NP], iota_dst[:, 0:NP], dstr[:, c, e], None,
                                         ALU.is_equal).then_inc(hot_plain[c], 1)
                        ve.tensor_scalar(one_src_r[:, s, :], iota_src[:, :], srcf[:, e], None,
                                         ALU.is_equal).then_inc(hot_ready[c], 1)
            for s in range(NC):
                full(ve, "WT", 2 * s + 1)
                ve.tensor_copy(WT[:, s, 4 * NP:N], bank(unit_bank("WT", 2 * s + 1), NP, NP)).then_inc(freed_v, 1)
            for c in range(NC):
                full(ve, "agg", c)
                i_ = ve.scalar_tensor_tensor(xres[:, c, :], bank(unit_bank("agg", c), NP, D), 0.0, xres[:, c, :],
                                             ALU.max, ALU.add)
                i_.then_inc(freed_v, 1)
            ve.wait_ge(ld_const, 16 * 6)
            for n in range(8):
                m, h = divmod(n, 2)
                o, w = HALF[h]
                full(ve, "mq", n)
                b = unit_bank("mq", n)
                ve.tensor_scalar(fm[:, 0, 0:w], bank(b, P, w), col("mix_bq", m), 0.0, ALU.add, ALU.min).then_inc(fm_min, 1)
                link(ve.tensor_scalar(fm[:, 2, 0:w], bank(b, P, w), col("mix_bq", m), 1.0, ALU.add, ALU.add))
                ve.wait_ge(fm_exp, n + 1)
                i_ = ve.tensor_tensor(T2[:, m, o:o + w], fm[:, 2, 0:w], fm[:, 1, 0:w], ALU.max)
                i_.then_inc(freed_v, 1)
                ve.wait_ge(freed_v, freed_count("v", FIRST["mq"] + n))
            for c in range(NC):
                full(ve, "mk", c)
                link(ve.tensor_tensor(fm[0:NP, 2, :], bank(unit_bank("mk", c), NP, D), row("mix_bk"), ALU.add))
                ve.tensor_scalar(fm[0:NP, 0, :], fm[0:NP, 2, :], 0.0, None, ALU.min).then_inc(fm_min, 1)
                ve.wait_ge(fm_exp, 8 + c + 1)
                ve.scalar_tensor_tensor(N1[:, c, :], fm[0:NP, 2, :], 1.0, fm[0:NP, 1, :], ALU.add,
                                        ALU.max).then_inc(freed_v, 1)
                ve.wait_ge(freed_v, freed_count("v", FIRST["mk"] + c))
            for c in range(NC):
                full(ve, "mv", c)
                ve.tensor_tensor(N3[:, c, :], bank(unit_bank("mv", c), NP, D), row("mix_bv"), ALU.add).then_inc(freed_v, 1)

            def diagonal_blocks(stage, hd, turn):
                ve.wait_ge(bd_zero, turn)
                for m in range(KC):
                    full(ve, stage, m)
                    b = unit_bank(stage, m)
                    for h in range(P // hd):
                        r = slice(h * hd, (h + 1) * hd)
                        ve.tensor_copy(bd[r, m, r], psum[r, 512 * b + h * hd:512 * b + (h + 1) * hd])
                        i_ = ve.tensor_copy(bd[r, m, P + h:P + h + 1], psum[r, 512 * b + P:512 * b + P + 1])
                    i_.then_inc(freed_v, 1)

            def divided(stage, hd, dst, eps=None):
                nh = P // hd
                for c in range(NC):
                    for h in range(2):
                        full(ve, stage, 2 * c + h)
                        v = bank(unit_bank(stage, 2 * c + h), NP, 2 * (P + nh)).rearrange("p (m w) -> p m w", m=2)
                        z = mz[:, :, 0:nh]
                        if eps is None:
                            link(ve.reciprocal(z, v[:, :, P:P + nh]))
                        else:
                            link(ve.tensor_scalar(z, v[:, :, P:P + nh], eps, None, ALU.add))
                            link(ve.reciprocal(z, z))
                        for m in range(2):
                            o = (2 * h + m) * P
                            i_ = ve.tensor_tensor(
                                dst[:, c, o:o + P].rearrange("p (h d) -> p h d", d=hd),
                                v[:, m, 0:P].rearrange("p (h d) -> p h d", d=hd),
                                z[:, m, :].unsqueeze(2).to_broadcast([NP, nh, hd]), ALU.mult)
                            if m == 0:
                                link(i_)
                        i_.then_inc(freed_v, 1)
                        ve.wait_ge(freed_v, freed_count("v", FIRST[stage] + 2 * c + h))

            def add_rows(stage, base, dst, bias):
                for c in range(NC):
                    full(ve, stage, c)
                    i_ = ve.tensor_tensor(dst[:, c, :], bank(unit_bank(stage, c), NP, D), base[:, c, :], ALU.add)
                    if bias:
                        link(i_)
                        i_ = ve.tensor_tensor(dst[:, c, :], dst[:, c, :], row(bias), ALU.add)
                    i_.then_inc(freed_v, 1)
                    ve.wait_ge(freed_v, freed_count("v", FIRST[stage] + c))
                    i_ = chunk_stats(dst, c)
                link(i_)

            diagonal_blocks("mkv", 64, 1)
            divided("mo", 64, N2)
            add_rows("mp", xres, xres, "mix_bp")
            layer_norm(1, xres, N1, stats=False)
            for a, name in enumerate(["ffn_bq", "bq0", "bq1"]):
                ve.tensor_scalar(nbq[:, a * KC:(a + 1) * KC], cols[:, COLS[name][0]:COLS[name][0] + KC], -ASCALE,
                                 None, ALU.mult).then_inc(nbq_ready, 1)

            def attention(a, bv, dst):
                s = A[a]

                def values(i):
                    ve.wait_ge(s["v"], i + 1)
                    for c, w in ((0, 4), (4, 1)):
                        src_ = bank(4 + c // 4, NP, P * w).rearrange("p (c d) -> p c d", d=P)
                        if bv:
                            b_ = rows[:, ROWS[bv], bass.ds(i * P, P)].unsqueeze(1).to_broadcast([NP, w, P])
                            i_ = ve.tensor_tensor(vv[:, c:c + w, :], src_, b_, ALU.add)
                        else:
                            i_ = ve.tensor_copy(vv[:, c:c + w, :], src_)
                    i_.then_inc(s["vc"], 1)

                def largest(i, t):
                    ve.wait_ge(s["score"], i * 10 + t + 1)
                    sc = psum[0:NP, 1024 * (t % 2):1024 * (t % 2) + N]
                    if a:
                        ve.memset(small[0:1, 90 + t:91 + t], 0.0)
                        ve.tensor_tensor_reduce(sc, sc, maskb[:, t // 2, :], 1.0, 3.0e38, ALU.add, ALU.min,
                                                small[0:NP, 80 + t:81 + t]).then_inc(s["max"], 1)
                    else:
                        ve.tensor_reduce(small[0:NP, 80 + t:81 + t], sc, AX, ALU.min).then_inc(s["max"], 1)

                def sums(i, t):
                    total = small[0:NP, 120 + t:121 + t]
                    inv = small[0:NP, 140 + t:141 + t]
                    n = 2 if a else 1
                    ve.wait_ge(s["exp"], i * 10 + t + 1)
                    if a:
                        ve.tensor_tensor_reduce(Pr[:, t % 2, :], Pr[:, t % 2, :], cnt_adj[:, t // 2, :], 1.0, 1e-16,
                                                ALU.mult, ALU.add, total).then_inc(s["sum"], 1)
                        ve.wait_ge(s["sum"], i * 20 + 2 * t + 1)
                    ve.reciprocal(inv, total).then_inc(s["sum"], 1)
                    ve.wait_ge(s["sum"], i * (10 * n) + n * (t + 1))
                    if t >= 4:
                        ve.wait_ge(s["av"], i * 5 + t // 2 - 1)
                    ve.tensor_scalar(diag[:, t % 4, :], ident[0:NP, 0:NP], inv, None,
                                     ALU.mult).then_inc(s["prob"], 1)

                def context_out(i, c):
                    ve.wait_ge(s["av"], i * 5 + c + 1)
                    ve.wait_ge(s["bcc"], i * 5 + c + 2)
                    ve.tensor_tensor(dst[:, bass.ds(i, 1), c * NP:(c + 1) * NP], bank(7, P, NP).unsqueeze(1),
                                     inv_rows.unsqueeze(1), ALU.mult).then_inc(s["ctx"], 1)

                with ve.Fori(0, PAIRS) as i:
                    for t in range(11):
                        if t < 10:
                            largest(i, t)
                        if t >= 1:
                            sums(i, t - 1)
                        if t == 1:
                            values(i)
                        if t >= 5 and t % 2:
                            context_out(i, t // 2 - 2)
                    context_out(i, 3)
                    context_out(i, 4)

            attention(0, "ffn_bv", T2)
            add_rows("ao", N1, N2, "ffn_bo")
            layer_norm(2, N2, N3, stats=False)

            lg = small[0:NP, 160:200].rearrange("p (c e) -> p c e", e=EX)
            ex = small[0:NP, 240:280].rearrange("p (c e) -> p c e", e=EX)
            one = small[0:NP, 640:680].rearrange("p (c e) -> p c e", e=EX)
            tmp = small[0:NP, 280:320].rearrange("p (c e) -> p c e", e=EX)
            mx = small[0:NP, 320:325]
            sm = small[0:NP, 325:330]
            gw = small[0:NP, 330:335]
            v5 = small[0:NP, 335:340]
            bc = lambda x: x.unsqueeze(2).to_broadcast([NP, NC, EX])

            def exp_gates(stage, n, bias):
                full(ve, stage, 0)
                v = bank(unit_bank(stage, 0), NP, NC * WMIN).rearrange("p (c e) -> p c e", e=WMIN)[:, :, 0:EX]
                if bias:
                    i_ = ve.tensor_tensor(lg, v, gate_b[:].unsqueeze(1).to_broadcast([NP, NC, EX]), ALU.add)
                else:
                    i_ = ve.tensor_copy(lg, v)
                i_.then_inc(freed_v, 1)
                ve.wait_ge(freed_v, freed_count("v", FIRST[stage]))
                link(ve.tensor_reduce(mx, lg, AX, ALU.max))
                ve.tensor_tensor(lg, lg, bc(mx), ALU.subtract).then_inc(gl_in, 1)
                ve.wait_ge(gl_out, n)
                link(ve.tensor_reduce(sm, ex, AX, ALU.add))

            exp_gates("gate0", 1, True)
            link(ve.reciprocal(gw, sm))
            e8 = small[0:NP, 340:348]
            for e in range(EX):
                i_ = ve.memset(e8[:, e:e + 1], float(EX - e))
            i_ = ve.memset(small[0:NP, 680:688], 0.0)
            link(i_)
            link(ve.tensor_reduce(v5, ex, AX, ALU.max))
            link(ve.tensor_tensor(tmp, ex, bc(v5), ALU.is_equal))
            link(ve.tensor_tensor(tmp, tmp, e8.unsqueeze(1).to_broadcast([NP, NC, EX]), ALU.mult))
            link(ve.tensor_reduce(v5, tmp, AX, ALU.max))
            ve.tensor_tensor(one, e8.unsqueeze(1).to_broadcast([NP, NC, EX]), bc(v5), ALU.is_equal).then_inc(gates_ready, 1)
            steps = small[0:NP, 500:500 + KT]
            over = small[0:NP, 512:512 + EX * KT].rearrange("p (e k) -> p e k", k=KT)
            for k in range(KT):
                i_ = ve.memset(steps[:, k:k + 1], k * TT + 0.5 if k else -1.0)
            link(i_)
            full(ve, "rank", 0)
            b = unit_bank("rank", 0)
            nt = small[0:NP, 350:358]
            ft = small[0:NP, 360:368]
            cnt_e = small[0:NP, 370:378]
            big = small[0:NP, 378:386]
            link(ve.tensor_copy(cnt_e, bank(b, NP, EX, EX * NC)))
            link(ve.tensor_tensor(over, cnt_e.unsqueeze(2).to_broadcast([NP, EX, KT]),
                                  steps.unsqueeze(1).to_broadcast([NP, EX, KT]), ALU.is_gt))
            link(ve.tensor_reduce(nt, over, AX, ALU.add))
            sums_ = [nt, small[0:NP, 388:396], small[0:NP, 396:404], small[0:NP, 404:412]]
            for p in range(3):
                w = 1 << p
                ve.tensor_copy(sums_[p + 1][:, 0:w], sums_[p][:, 0:w])
                link(ve.tensor_tensor(sums_[p + 1][:, w:EX], sums_[p][:, w:EX], sums_[p][:, 0:EX - w], ALU.add))
            link(ve.tensor_tensor(ft, sums_[3], nt, ALU.subtract))
            link(ve.tensor_scalar(big, ft, float(TT), None, ALU.mult))
            ve.tensor_tensor(tmp, bank(b, NP, NC * EX).rearrange("p (c e) -> p c e", e=EX),
                             big.unsqueeze(1).to_broadcast([NP, NC, EX]), ALU.add).then_inc(freed_v, 1)
            ve.wait_ge(freed_v, freed_count("v", FIRST["rank"]))
            link(ve.tensor_tensor(tmp, tmp, one, ALU.mult))
            link(ve.tensor_reduce(v5, tmp, AX, ALU.add))
            link(ve.tensor_copy(idx[:], v5))
            link(ve.tensor_tensor(big[:, 0:1], ft[:, EX - 1:EX], nt[:, EX - 1:EX], ALU.add))
            link(ve.tensor_copy(tiles[:, 2, 0:1], big[0:1, 0:1]))
            link(ve.tensor_copy(tiles[:, 0, :], nt[0:1, :]))
            ve.tensor_copy(tiles[:, 1, :], ft[0:1, :]).then_inc(slots_ready, 1)
            ve.wait_ge(slots_ready, 1)
            ve.nop().then_inc(M["yv"], 1)

            def tile_columns(n):
                ve.wait_ge(M["xsT"], n + 1)
                ve.tensor_copy(xsT.rearrange("p a b -> p (a b)"), bank(5, P, KC * TT)).then_inc(M["xsTv"], 1)

            tile_columns(0)
            with ve.Fori(0, EX // 2) as i:
                for par in range(2):
                    k = ve.value_load(tiles[0:1, 0, bass.ds(i * 2 + par, 1)], min_val=1, max_val=KT)
                    b0 = ve.value_load(tiles[0:1, 1, bass.ds(i * 2 + par, 1)], min_val=0, max_val=MAXT - 1)
                    with ve.Fori(0, k) as j:
                        g = b0 + j
                        for b in range(2):
                            ve.wait_ge(M["h"], g * 2 + b + 1)
                            ve.tensor_copy(hs[:, b * D:(b + 1) * D], bank(b, P, D)).then_inc(M["hs"], 1)
                        tile_columns(g + 1)
                        ve.wait_ge(M["y"], g + 2)
                        ve.wait_ge(M["st"], g * 32 + 16)
                        ve.wait_ge(M[f"second{par}"], i * 48 + 48)
                        ve.tensor_tensor(ys, bank(4, P, D // 2), eb2[par], ALU.add).then_inc(M["yv"], 1)
            for c in range(NC):
                ve.wait_ge(gathered[c], 16)
                link(ve.scalar_tensor_tensor(xres[:, c, :], yg[:, c, :], gw[:, c:c + 1], xres[:, c, :], ALU.mult, ALU.add))
                i_ = chunk_stats(xres, c)
            link(i_)
            layer_norm(3, xres, N2, stats=False)
            ve.tensor_scalar(maskb, cnt_adj[:], 0.5, NO_EDGE, ALU.is_lt, ALU.mult).then_inc(mask_ready, 1)
            ve.wait_ge(mask_ready, 1)

            def batch_norm(n, g, beta):
                for m in range(KC):
                    for h, (o, w) in enumerate(HALF):
                        i_ = ve.bn_stats(small[:, 400 + 12 * m + 6 * h:406 + 12 * m + 6 * h], T2[:, m, o:o + w])
                link(i_)
                for m in range(KC):
                    i_ = ve.bn_aggr(small[:, 460 + 2 * m:462 + 2 * m], small[:, 400 + 12 * m:412 + 12 * m])
                link(i_)
                mv = small[:, 460:468].rearrange("p (m t) -> p m t", t=2)
                ve.tensor_scalar(small[:, 30:34], mv[:, :, 1], EPS, None, ALU.add).then_inc(bn_var, 1)
                ve.wait_ge(bn_sd, n + 1)
                link(ve.reciprocal(small[:, 470:474], small[:, 40:44]))
                link(ve.tensor_tensor(small[:, 474:478], small[:, 470:474], cols[:, COLS[g][0]:COLS[g][0] + 4], ALU.mult))
                link(ve.tensor_tensor(small[:, 478:482], small[:, 474:478], mv[:, :, 0], ALU.mult))
                link(ve.tensor_tensor(small[:, 482:486], cols[:, COLS[beta][0]:COLS[beta][0] + 4], small[:, 478:482],
                                      ALU.subtract))
                for m in range(KC):
                    i_ = ve.tensor_scalar(T2[:, m, :], T2[:, m, :], small[:, 474 + m:475 + m], small[:, 482 + m:483 + m],
                                          ALU.mult, ALU.add)
                    i_.then_inc(bn_out, 1)
                ve.wait_ge(bn_out, 4 * (n + 1))

            def add_cols(stage, base, bias):
                for n in range(8):
                    m, h = divmod(n, 2)
                    o, w = HALF[h]
                    full(ve, stage, n)
                    ve.scalar_tensor_tensor(T2[:, m, o:o + w], bank(unit_bank(stage, n), P, w), col(bias, m),
                                            base[:, m, o:o + w], ALU.add, ALU.add).then_inc(freed_v, 1)
                ve.wait_ge(freed_v, freed_count("v", FIRST[stage] + 7))

            for l in range(2):
                attention(1 + l, None, T3)
                add_cols(f"wo{l}", T1 if l == 0 else T2, f"bo{l}")
                batch_norm(2 * l, f"g1{l}", f"beta1{l}")
                add_cols(f"ffb{l}", T2, f"b2{l}")
                batch_norm(2 * l + 1, f"g2{l}", f"beta2{l}")
            diagonal_blocks("nkv", 32, 2)
            divided("no", 32, N4, 1e-15)
            stage_out(ve, "gN")
            layer_norm(4, GN, GN)
            ve.wait_ge(ln_out, 5 * NC)
            ve.wait_ge(x_biased, 2 * NC)
            for c in range(NC):
                i_ = ve.tensor_tensor(GN[:, c, :], GN[:, c, :], row("ln_g"), ALU.mult)
            link(i_)
            for c in range(NC):
                i_ = ve.tensor_tensor(xres[:, c, :], xres[:, c, :], GN[:, c, :], ALU.add)
            link(i_)
            add_rows("np", xres, xres, None)
            layer_norm(5, xres, N1, stats=False)
            exp_gates("gate1", 2, False)
            for c in range(NC):
                i_ = ve.max(small[0:NP, 500 + 8 * c:508 + 8 * c], ex[:, c, :])
            link(i_)
            top = small[0:NP, 500:540].rearrange("p (c e) -> p c e", e=EX)
            pr = small[0:NP, 540:550].rearrange("p (c e) -> p c e", e=2)
            link(ve.reciprocal(gw, sm))
            link(ve.tensor_tensor(pr, top[:, :, 0:2], gw.unsqueeze(2).to_broadcast([NP, NC, 2]), ALU.mult))
            link(ve.tensor_reduce(mx, pr, AX, ALU.add))
            link(ve.reciprocal(sm, mx))
            link(ve.tensor_tensor(pr, pr, sm.unsqueeze(2).to_broadcast([NP, NC, 2]), ALU.mult))
            for w in range(2):
                ve.tensor_copy(pbl[:, w, :, :], pr[:, :, w].unsqueeze(2).to_broadcast([NP, NC, P])).then_inc(pb_l, 1)
            stage_out(ve, "pb")
            for n in range(16):
                f, h = divmod(n, 2)
                o, w = HALF[h]
                stage, u = ("h1a", n) if n < COUNT["h1a"] else ("h1b", n - COUNT["h1a"])
                full(ve, stage, u)
                b = unit_bank(stage, u)
                for q in range(2):
                    ve.tensor_tensor(hb[:, q, 0:w], bank(b, P, w), PB[:, q, o:o + w], ALU.mult).then_inc(h_in, 1)
                ve.wait_ge(h_g, 2 * n + 2)
                ve.tensor_tensor(h1T[:, f, o:o + w], hb[:, 2, 0:w], hb[:, 3, 0:w], ALU.add).then_inc(freed_v, 1)
                ve.wait_ge(freed_v, freed_count("v", FIRST[stage] + u))
            for c in range(NC):
                full(ve, "o1", c)
                ve.tensor_tensor(xres[:, c, :], bank(unit_bank("o1", c), NP, D), xres[:, c, :], ALU.add).then_inc(x_done, 1)


def kernel(**inputs):
    import numpy as np
    import concourse.bacc as bacc
    from concourse.bass_utils import run_bass_kernel_spmd

    a = {k: np.asarray(v) for k, v in inputs.items()}

    def as_rows(x):
        return x.reshape(NC, NP, D).transpose(1, 0, 2)

    def edges(x):
        return x.reshape(ET, NP).T

    def weight(w):
        return w.reshape(w.shape[0] // P, P, w.shape[1]).transpose(1, 0, 2)

    def pair_weights(q, k, v):
        w = np.stack([q, k, v]).reshape(3, KC, P, PAIRS, P)
        return w.transpose(3, 2, 0, 1, 4)

    vectors = {"mix_bq": a["L0_mix_bq"], "ln1_g": a["L0_ffn_ln1_g"], "ln1_b": a["L0_ffn_ln1_b"], "ffn_bq": a["L0_ffn_bq"], "ffn_bk": a["L0_ffn_bk"],
               "moe_b1": a["L0_ffn_b1"], "l1_b1": a["L1_ffn_b1"]}
    for l in range(2):
        for v in ("bq", "bo", "b1", "b2", "g1", "beta1", "g2", "beta2"):
            vectors[f"{v}{l}"] = a[f"L1_gnn_{v}"][l]
    qkv = a["L1_mix_qkv_weight"]
    arrays = {
        "src": edges(a["src"]), "dst": edges(a["dst"]), "edge_w": edges(a["edge_weight"]), "x": as_rows(a["x"]),
        "cols": np.concatenate([vectors[n].reshape(w, P) for n, (_, w) in COLS.items()]).T,
        "rows": np.stack([a[n] for n in (
            "L0_mix_bk", "L0_mix_bv", "L0_mix_bp", "L0_ffn_bv", "L0_ffn_bo", "L0_ffn_ln1_g", "L0_ffn_ln1_b",
            "L1_gnn_ln_g", "L1_gnn_ln_b", "L1_mix_proj_bias")]),
        "gate_b": a["L0_ffn_gate_b"], "moe_b2": a["L0_ffn_b2"], "l1_b2": a["L1_ffn_b2"],
        "gateW": weight(a["L0_ffn_gate_W"]).reshape(P, -1), "gateW1": weight(a["L1_ffn_Wg"]).reshape(P, -1),
        "gnnW": weight(a["L0_gnn_weight"]), "mixWq": weight(a["L0_mix_Wq"]), "mixWk": weight(a["L0_mix_Wk"]),
        "mixWv": weight(a["L0_mix_Wv"]), "mixWp": weight(a["L0_mix_Wp"]), "ffnWo": weight(a["L0_ffn_Wo"]),
        "att0": pair_weights(a["L0_ffn_Wq"], a["L0_ffn_Wk"], a["L0_ffn_Wv"]),
        "moeW1": a["L0_ffn_W1"].reshape(EX, KC, P, FF).transpose(0, 2, 1, 3),
        "moeW2": a["L0_ffn_W2"].reshape(EX, FC, P, D).transpose(0, 2, 1, 3),
        "m1q": weight(qkv[0:D].T), "m1k": weight(qkv[D:2 * D].T), "m1v": weight(qkv[2 * D:].T),
        "m1p": weight(a["L1_mix_proj_weight"].T),
        "l1W1": weight(a["L1_ffn_W1"].transpose(1, 0, 2).reshape(D, EX * F1)),
        "l1W2": a["L1_ffn_W2"].transpose(1, 0, 2),
    }
    for l in range(2):
        arrays[f"att{l + 1}"] = pair_weights(*(a[f"L1_gnn_{w}"][l].T for w in ("Wq", "Wk", "Wv")))
        arrays[f"gnnWo{l}"] = weight(a["L1_gnn_Wo"][l].T)
        arrays[f"ffW1_{l}"] = weight(a["L1_gnn_W1"][l].T)
        arrays[f"ffW2_{l}"] = a["L1_gnn_W2"][l].T
    arrays = {f"in_{k}": np.ascontiguousarray(v) for k, v in arrays.items()}

    nc = bacc.Bacc("TRN2", target_bir_lowering=False, num_devices=1)
    ins = {k[3:]: nc.dram_tensor(k, v.shape, mybir.dt.from_np(v.dtype), kind="ExternalInput").ap()
           for k, v in arrays.items()}
    out = nc.dram_tensor("out_rows", [NP, NC, D], F32, kind="ExternalOutput").ap()
    build(nc, ins, out)
    r = run_bass_kernel_spmd(nc, [arrays], core_ids=[0])
    return r.results[0]["out_rows"].transpose(1, 0, 2).reshape(N, D)
```
